# Optimizing a Trainium2 kernel written in Bass

```python
import numpy as np
import jax
import jax.numpy as jnp

def _softmax(x, axis=-1):
    return jax.nn.softmax(x, axis=axis)

def _gelu(x):
    return jax.nn.gelu(x, approximate=True)

def _silu(x):
    return jax.nn.silu(x)

def _sigmoid(x):
    return jax.nn.sigmoid(x)

def _layernorm(x, axis=-1, eps=1e-05):
    m = jnp.mean(x, axis=axis, keepdims=True)
    v = jnp.var(x, axis=axis, keepdims=True)
    return (x - m) / jnp.sqrt(v + eps)

def _scatter_add(tgt, idx, src, axis=0):
    return tgt.at[idx].add(src)

def _segment_sum(src, seg, n):
    return jax.ops.segment_sum(src, seg, n)
kernel_name = 'mk_gnn_ffn_d1_gnn_r16_f12fc8'

def setup_inputs(seed: int=0):
    np.random.seed(seed)
    _w = jnp.asarray

    def _rec_inputs():
        import jax
        import jax.numpy as jnp
        _gk = jax.random.key(seed)
        x = -0.0003713 + 1 * jax.random.normal(jax.random.fold_in(_gk, 1), (6250, 256), jnp.float32)
        _s = jax.random.randint(jax.random.fold_in(_gk, 2), (50000,), 0, 6250, jnp.int32)
        _d = jax.random.randint(jax.random.fold_in(_gk, 3), (50000,), 0, 6250, jnp.int32)
        _loop = jnp.arange(6250, dtype=jnp.int32)
        src = jnp.concatenate([_s, _d, _loop])
        dst = jnp.concatenate([_d, _s, _loop])
        _o = jnp.argsort(dst, stable=True)
        src = src[_o]
        dst = dst[_o]
        edge_attr_4 = jax.random.uniform(jax.random.fold_in(_gk, 11), (106250, 4), jnp.float32, 0.0, 0.999999)
        return (x, src, dst, edge_attr_4)
    x, src, dst, edge_attr_4 = _rec_inputs()

    def _L0_gnn_setup():
        import jax, jax.numpy as jnp
        import numpy as np
        N_NODES = 3125
        N_EDGES = 20000
        HIDDEN = 256
        N_LAYERS = 5
        BN_EPS = 1e-05

        def _mpnn(x, edge_index, edge_attr, mlp_w, mlp_b, ew1, ew2, bn_g, bn_b):
            n = x.shape[0]
            row, col = (edge_index[0], edge_index[1])
            deg = jax.ops.segment_sum(jnp.ones((edge_index.shape[1],), x.dtype), col, num_segments=n)
            dinv = jnp.where(deg > 0, deg ** (-0.5), 0.0)
            norm = dinv[row] * dinv[col]
            h = x
            for l in range(N_LAYERS):
                edge_fea = jnp.concatenate([edge_attr[:, 3:] @ ew1[l], edge_attr[:, 0:3] @ ew2[l]], axis=-1)
                msg = norm[:, None] * (h[row] + edge_fea)
                agg = jax.ops.segment_sum(msg, col, num_segments=n)
                h = jax.nn.relu(jnp.concatenate([h, agg], axis=1) @ mlp_w[l] + mlp_b[l])
                mu = h.mean(axis=0)
                var = h.var(axis=0)
                h = (h - mu) * jax.lax.rsqrt(var + BN_EPS) * bn_g[l] + bn_b[l]
                if l != N_LAYERS - 1:
                    h = jax.nn.relu(h)
            return h
        key = jax.random.key(seed)
        ks = jax.random.split(key, 8)
        x = jax.random.normal(ks[0], (N_NODES, HIDDEN), dtype=jnp.float32)
        edge_index = jax.random.randint(ks[1], (2, N_EDGES), 0, N_NODES, dtype=jnp.int64)
        edge_attr = jax.random.uniform(ks[2], (N_EDGES, 4), dtype=jnp.float32)
        mlp_w = jax.random.normal(ks[3], (N_LAYERS, 2 * HIDDEN, HIDDEN), dtype=jnp.float32) * (1.0 / np.sqrt(2 * HIDDEN))
        mlp_b = jnp.zeros((N_LAYERS, HIDDEN), dtype=jnp.float32)
        ew1 = jax.random.normal(ks[4], (N_LAYERS, 1, HIDDEN // 2), dtype=jnp.float32)
        ew2 = jax.random.normal(ks[5], (N_LAYERS, 3, HIDDEN // 2), dtype=jnp.float32) * (1.0 / np.sqrt(3.0))
        bn_g = jnp.ones((N_LAYERS, HIDDEN), dtype=jnp.float32)
        bn_b = jnp.zeros((N_LAYERS, HIDDEN), dtype=jnp.float32)
        return {'x': x, 'edge_index': edge_index, 'edge_attr': edge_attr, 'mlp_w': mlp_w, 'mlp_b': mlp_b, 'ew1': ew1, 'ew2': ew2, 'bn_g': bn_g, 'bn_b': bn_b}
    _L0_gnn_all = _L0_gnn_setup()
    _L0_gnn_in = {k: v for k, v in _L0_gnn_all.items() if k in ('mlp_w', 'mlp_b', 'ew1', 'ew2', 'bn_g', 'bn_b')}
    del _L0_gnn_all

    def _L0_ffn_setup():
        import jax, jax.numpy as jnp
        import numpy as np
        B, S, D, F, E, K = (8, 128, 256, 1024, 8, 2)
        key = jax.random.key(seed)
        ks = jax.random.split(key, 10)
        s = 0.02
        return {'x': jax.random.normal(ks[0], (B, S, D), dtype=jnp.float32), 'Wr': jax.random.normal(ks[1], (D, E), dtype=jnp.float32) * s, 'W1s': jax.random.normal(ks[2], (D, F), dtype=jnp.float32) * s, 'b1s': jnp.zeros((F,), dtype=jnp.float32), 'W2s': jax.random.normal(ks[3], (F, D), dtype=jnp.float32) * s, 'b2s': jnp.zeros((D,), dtype=jnp.float32), 'W1p': jax.random.normal(ks[4], (E, D, F), dtype=jnp.float32) * s, 'b1p': jnp.zeros((E, F), dtype=jnp.float32), 'W2p': jax.random.normal(ks[5], (E, F, D), dtype=jnp.float32) * s, 'b2p': jnp.zeros((E, D), dtype=jnp.float32)}
    _L0_ffn_all = _L0_ffn_setup()
    _L0_ffn_in = {k: v for k, v in _L0_ffn_all.items() if k in ('Wr', 'W1s', 'b1s', 'W2s', 'b2s', 'W1p', 'b1p', 'W2p', 'b2p')}
    del _L0_ffn_all
    return {'x': x, 'src': src, 'dst': dst, 'edge_attr_4': edge_attr_4, 'L0_gnn_mlp_w': _L0_gnn_in['mlp_w'], 'L0_gnn_mlp_b': _L0_gnn_in['mlp_b'], 'L0_gnn_ew1': _L0_gnn_in['ew1'], 'L0_gnn_ew2': _L0_gnn_in['ew2'], 'L0_gnn_bn_g': _L0_gnn_in['bn_g'], 'L0_gnn_bn_b': _L0_gnn_in['bn_b'], 'L0_ffn_Wr': _L0_ffn_in['Wr'], 'L0_ffn_W1s': _L0_ffn_in['W1s'], 'L0_ffn_b1s': _L0_ffn_in['b1s'], 'L0_ffn_W2s': _L0_ffn_in['W2s'], 'L0_ffn_b2s': _L0_ffn_in['b2s'], 'L0_ffn_W1p': _L0_ffn_in['W1p'], 'L0_ffn_b1p': _L0_ffn_in['b1p'], 'L0_ffn_W2p': _L0_ffn_in['W2p'], 'L0_ffn_b2p': _L0_ffn_in['b2p']}

def reference(x, src, dst, edge_attr_4, L0_gnn_mlp_w, L0_gnn_mlp_b, L0_gnn_ew1, L0_gnn_ew2, L0_gnn_bn_g, L0_gnn_bn_b, L0_ffn_Wr, L0_ffn_W1s, L0_ffn_b1s, L0_ffn_W2s, L0_ffn_b2s, L0_ffn_W1p, L0_ffn_b1p, L0_ffn_W2p, L0_ffn_b2p):
    import jax
    import jax.numpy as jnp

    def _L0_gnn_ref(x, edge_index, edge_attr, mlp_w, mlp_b, ew1, ew2, bn_g, bn_b):
        import jax, jax.numpy as jnp
        import numpy as np
        N_NODES = 3125
        N_EDGES = 20000
        HIDDEN = 256
        N_LAYERS = 5
        BN_EPS = 1e-05

        def _mpnn(x, edge_index, edge_attr, mlp_w, mlp_b, ew1, ew2, bn_g, bn_b):
            n = x.shape[0]
            row, col = (edge_index[0], edge_index[1])
            deg = jax.ops.segment_sum(jnp.ones((edge_index.shape[1],), x.dtype), col, num_segments=n)
            dinv = jnp.where(deg > 0, deg ** (-0.5), 0.0)
            norm = dinv[row] * dinv[col]
            h = x
            for l in range(N_LAYERS):
                edge_fea = jnp.concatenate([edge_attr[:, 3:] @ ew1[l], edge_attr[:, 0:3] @ ew2[l]], axis=-1)
                msg = norm[:, None] * (h[row] + edge_fea)
                agg = jax.ops.segment_sum(msg, col, num_segments=n)
                h = jax.nn.relu(jnp.concatenate([h, agg], axis=1) @ mlp_w[l] + mlp_b[l])
                mu = h.mean(axis=0)
                var = h.var(axis=0)
                h = (h - mu) * jax.lax.rsqrt(var + BN_EPS) * bn_g[l] + bn_b[l]
                if l != N_LAYERS - 1:
                    h = jax.nn.relu(h)
            return h
        return _mpnn(x, edge_index, edge_attr, mlp_w, mlp_b, ew1, ew2, bn_g, bn_b)

    def _L0_ffn_ref(x, Wr, W1s, b1s, W2s, b2s, W1p, b1p, W2p, b2p):
        import jax, jax.numpy as jnp
        import numpy as np
        B, S, D, F, E, K = (8, 128, 256, 1024, 8, 2)
        gelu = lambda t: jax.nn.gelu(t, approximate=False)
        shared = gelu(x @ W1s + b1s) @ W2s + b2s
        rw = jax.nn.softmax(x @ Wr, axis=-1)
        topw, topi = jax.lax.top_k(rw, K)
        topw = topw / jnp.sum(topw, axis=-1, keepdims=True)
        mask = jnp.sum(jax.nn.one_hot(topi, E, dtype=topw.dtype) * topw[..., None], axis=-2)
        h = gelu(jnp.einsum('bsd,edf->bsef', x, W1p) + b1p)
        priv = jnp.einsum('bsef,efd->bsed', h, W2p) + b2p
        routed = jnp.einsum('bsed,bse->bsd', priv, mask)
        return shared + routed
    edge_index = jnp.stack([src, dst])
    x = x + _L0_gnn_ref(_layernorm(x, axis=-1), edge_index, edge_attr_4, L0_gnn_mlp_w, L0_gnn_mlp_b, L0_gnn_ew1, L0_gnn_ew2, L0_gnn_bn_g, L0_gnn_bn_b)
    x = x + _L0_ffn_ref(_layernorm(x, axis=-1)[None], L0_ffn_Wr, L0_ffn_W1s, L0_ffn_b1s, L0_ffn_W2s, L0_ffn_b2s, L0_ffn_W1p, L0_ffn_b1p, L0_ffn_W2p, L0_ffn_b2p)[0]
    return x

_drawn_inputs = setup_inputs


def setup_inputs(seed=0):
    import zlib

    import numpy as np

    out = dict(_drawn_inputs(seed))
    spreads = {'L0_gnn_mlp_b': (0.0, 0.1),
     'L0_gnn_bn_g': (1.0, 0.2),
     'L0_gnn_bn_b': (0.0, 0.1),
     'L0_ffn_b1s': (0.0, 0.358),
     'L0_ffn_b2s': (0.0, 0.1),
     'L0_ffn_b1p': (0.0, 0.474),
     'L0_ffn_b2p': (0.0, 0.1)}
    factors = {}
    for name, (base, spread) in spreads.items():
        noise = np.random.default_rng([zlib.crc32(name.encode()), seed]).standard_normal(out[name].shape)
        drawn = base * np.exp(spread * noise) if base else spread * noise
        out[name] = jnp.asarray(drawn.astype(out[name].dtype))
    for name, factor in factors.items():
        out[name] = (out[name] * factor).astype(out[name].dtype)
    return out
```

```python
from contextlib import ExitStack

import concourse.bass as bass
from concourse import mybir

F32 = mybir.dt.float32
BF16 = mybir.dt.bfloat16
I32 = mybir.dt.int32
ALU = mybir.AluOpType
ACT = mybir.ActivationFunctionType
AX_X = mybir.AxisListType.X
ds = bass.ds

P = 128
K = 4
GG = 4
EPS = 1e-5
FAR = 1000000


def build(nc, x, src, dst, attr, mlp_w, mlp_b, ew1, ew2, bn_g, bn_b,
          wr, w1s, b1s, w2s, b2s, w1p, b1p, w2p, b2p, out):
    N, D = x.shape
    E = src.shape[0]
    L = mlp_w.shape[0]
    X = wr.shape[1]
    F = w1s.shape[1]
    A = attr.shape[1]
    KD = D // P
    KF = F // P
    NT = -(-N // P)
    LAST = N - (NT - 1) * P
    NP = NT * P
    NC = -(-E // P)
    CB = -(-NC // P)
    COLS = CB * P
    FULLC = E // P
    REST = E - FULLC * P
    MAXG = -(-NC // K) + GG
    MING = 3
    W0 = D + 1
    TB = 2
    TOK = TB * P
    EACH = -(-N // TOK)
    MAXB = 2 * N // TOK + X
    assert KD == 2 and NC + K * (MING + GG) < COLS and REST > 0 and L >= 3
    assert (NT - 1) % 4 == 0 and NT * X <= 512

    rows0 = nc.dram_tensor("rows0", (NP, W0), F32).ap()
    rows = nc.dram_tensor("rows", (NP, D), F32).ap()
    expert_in = nc.dram_tensor("expert_in", ((MAXB + 1) * TOK, D), F32).ap()
    expert_out = nc.dram_tensor("expert_out", (MAXB * TOK, D), F32).ap()

    with ExitStack() as ctx:
        def sb(name, shape, dt=F32):
            return ctx.enter_context(nc.sbuf_tensor(name, shape, dt))

        def sem(name):
            return ctx.enter_context(nc.semaphore(name))

        bank = ctx.enter_context(nc.psum_tensor("bank", [P, 8, 512], F32))

        feat_t = sb("feat_t", [P, KD, NP])
        resid = sb("resid", [P, NT, D])
        ident = sb("ident", [P, P])
        iota_row = sb("iota_row", [P, P])
        dinv = sb("dinv", [P, NT])
        zero = sb("zero", [1, 512], BF16)
        ln_stats = sb("ln_stats", [P, NT, 6])
        ln_mv = sb("ln_mv", [P, NT, 2])
        ln_rstd = sb("ln_rstd", [P, NT])
        ln_std = sb("ln_std", [P, NT])

        arena = sb("arena", [P, COLS * (2 + A) + 1024])
        src_col = arena[:, 0:COLS].bitcast(I32)
        dst_col = arena[:, COLS:2 * COLS]
        attr_col = arena[:, 2 * COLS:(2 + A) * COLS].rearrange("p (c a) -> p c a", a=A)
        iota_bf = arena[:, (2 + A) * COLS:(2 + A) * COLS + P // 2].bitcast(BF16)

        SET = KD * F + KF * D
        sets = sb("sets", [P, 3 * SET])

        def w1_set(s):
            return sets[:, s * SET:s * SET + KD * F].rearrange("p (k f) -> p k f", k=KD)

        def w2_set(s):
            return sets[:, s * SET + KD * F:(s + 1) * SET].rearrange("p (c d) -> p c d", c=KF)

        pools = [[sets[:, :], 3 * SET, 0], [feat_t[:, :, :].rearrange("p k n -> p (k n)"), KD * NP, 0]]

        def stage(n):
            pool = next(q for q in pools if q[2] + n <= q[1])
            pool[2] += n
            return pool[0][:, pool[2] - n:pool[2]]

        dst_int = stage(COLS).bitcast(I32).rearrange("p (b e) -> p b e", b=CB)
        src_int = stage(COLS).bitcast(I32).rearrange("p (b e) -> p b e", b=CB)
        dst_f = stage(COLS).rearrange("p (b e) -> p b e", b=CB)
        src_f = stage(COLS).rearrange("p (b e) -> p b e", b=CB)
        attr_in = stage(COLS * A).rearrange("p (b e a) -> p b e a", b=CB, a=A)
        c_lo = stage(CB)
        c_hi = stage(CB)
        tile_at = stage(NT)
        tile_at_end = stage(NT)
        chunk_up = stage(CB)
        chunk_down = stage(CB)
        act_lo = stage(NT * CB).rearrange("p (t b) -> p t b", t=NT)
        act_hi = stage(NT * CB).rearrange("p (t b) -> p t b", t=NT)
        bounds = stage(2 * NT)
        bounds_all = stage(2 * NT)
        first_f = stage(NT)
        some = stage(NT)
        first_m = stage(NT)
        span = stage(NT)
        span_i = stage(NT).bitcast(I32)
        groups_i = stage(NT).bitcast(I32)
        groups_f = stage(NT)
        groups_m = stage(NT)
        dst_ii = stage(COLS).bitcast(I32)
        lo_i = stage(COLS).bitcast(I32)
        hi_i = stage(COLS).bitcast(I32)
        lo_b = stage(COLS // 2).bitcast(BF16)
        hi_b = stage(COLS // 2).bitcast(BF16)
        deg = stage(NT)
        deg1 = stage(NT)
        deg_root = stage(NT)
        deg_inv = stage(NT)
        deg_some = stage(NT)
        CG = 8
        hot_lo = [stage(CG * P // 2).bitcast(BF16).rearrange("p (c n) -> p c n", c=CG) for _ in range(2)]
        hot_hi = [stage(CG * 64 // 2).bitcast(BF16).rearrange("p (c n) -> p c n", c=CG) for _ in range(2)]

        plan = sb("plan", [1, 2 * NT + 1], I32)
        plan_first = plan[:, 0:NT]
        plan_groups = plan[:, NT:2 * NT]
        plan_total = plan[:, 2 * NT:2 * NT + 1]
        neg_base = sb("neg_base", [P, NT])

        normed = sb("normed", [P, 2, D])
        row_out = sb("row_out", [P, 2, 4, D])
        row0_out = row_out[:, :, :, :].rearrange("p a b d -> p (a b d)")[:, 0:2 * (W0 + 7)].rearrange(
            "p (a d) -> p a d", a=2)[:, :, 0:W0]

        edges_in = sem("edges_in")
        padded = sem("padded")
        consts = sem("consts")
        as_float = sem("as_float")
        turned = sem("turned")
        placed = sem("placed")
        prep_v = sem("prep_v")
        reduce_in = sem("reduce_in")
        reduce_out = sem("reduce_out")
        hot_ready = sem("hot_ready")
        counted = sem("counted")
        root_in = sem("root_in")
        root_out = sem("root_out")
        x_in = sem("x_in")
        pre_p = sem("pre_p")

        def edge_parts(flat, tile, w):
            full = FULLC // P
            a = full * P * P
            b = FULLC * P
            r = FULLC - full * P
            if w == 1:
                yield flat[0:a].rearrange("(k p e) -> p k e", p=P, e=P), tile[:, 0:full, :]
                yield flat[a:b].rearrange("(p e) -> p e", e=P), tile[0:r, full, :]
                yield flat[b:E].rearrange("(p e) -> p e", p=1), tile[r:r + 1, full, 0:REST]
            else:
                yield (flat[0:a, :].rearrange("(k p e) a -> p k (e a)", p=P, e=P),
                       tile[:, 0:full, :, :].rearrange("p k e a -> p k (e a)"))
                yield (flat[a:b, :].rearrange("(p e) a -> p (e a)", e=P),
                       tile[0:r, full, :, :].rearrange("p e a -> p (e a)"))
                yield (flat[b:E, :].rearrange("(p e) a -> p (e a)", p=1),
                       tile[r:r + 1, full, 0:REST, :].rearrange("p e a -> p (e a)"))

        def turns():
            for b in range(CB):
                yield "dst", b, 0
            for b in range(CB):
                yield "src", b, 0
            for a in range(A):
                for b in range(CB):
                    yield "attr", b, a

        TURNS = list(turns())

        def loop(engine, n, body):
            body(0)
            with engine.Fori(1, n) as i:
                body(i)

        def wait_past(engine, what, value):
            if not isinstance(value, int) or value > 0:
                engine.wait_ge(what, value)

        def tile_stats(dve, done):
            assert NT % 7 == 0
            with dve.Fori(0, NT // 7) as i:
                for u in range(7):
                    dve.bn_stats(ln_stats[:, ds(i * 7 + u, 1), :].rearrange("p a s -> p (a s)"),
                                 resid[:, ds(i * 7 + u, 1), :].rearrange("p a d -> p (a d)")).then_inc(done, 1)

        def tile(ap, t):
            return ap[:, ds(t, 1), :].rearrange("p a s -> p (a s)")

        def nodes(t, n=1):
            return ds(t * P, n * P)

        with nc.Block() as block:
            @block.sync
            def _(sp):
                sp.wait_ge(padded, 3)
                for d, s in [*edge_parts(dst, dst_int, 1), *edge_parts(src, src_int, 1),
                             *edge_parts(attr, attr_in, A)]:
                    sp.dma_start(s, d).then_inc(edges_in, 16)
                sp.wait_ge(edges_in, 16 * 9)
                sp.wait_ge(x_in, 32)

            @block.gpsimd
            def _(pool):
                pool.memset(ident[:], 0.0).then_inc(pre_p, 1)
                pool.wait_ge(pre_p, 1)
                pool.affine_select(out=ident[:], in_=ident[:], compare_op=ALU.not_equal, fill=1.0, base=0,
                                   pattern=[[-1, P]], channel_multiplier=1).then_inc(consts, 1)
                imp = dict(allow_small_or_imprecise_dtypes=True)
                pool.iota(iota_row[:], [[1, P]], 0, 0, **imp).then_inc(consts, 1)
                pool.iota(iota_bf, [[1, P]], 0, 0, **imp).then_inc(consts, 1)
                pool.iota(tile_at, [[P, NT]], 0, 0, **imp).then_inc(consts, 1)
                pool.iota(tile_at_end, [[P, NT]], P, 0, **imp).then_inc(consts, 1)
                pool.iota(neg_base[:], [[-P, NT]], 0, 0, **imp).then_inc(consts, 1)
                pool.iota(chunk_up, [[P, CB]], 1, 1, **imp).then_inc(consts, 1)
                pool.iota(chunk_down, [[-P, CB]], COLS, -1, **imp).then_inc(consts, 1)
                pool.memset(resid[:, NT - 1, :], 0.0).then_inc(pre_p, 1)
                pool.wait_ge(pre_p, 2)
                full = (NT - 1) * P
                pool.dma_start(resid[:, 0:NT - 1, :],
                               x[0:full, :].rearrange("(t p) d -> p t d", p=P)).then_inc(x_in, 16)
                pool.dma_start(resid[0:LAST, NT - 1, :], x[full:N, :]).then_inc(x_in, 16)
                pool.wait_ge(reduce_in, 1)
                pool.partition_all_reduce(bounds_all, bounds, P, bass.bass_isa.ReduceOp.max)\
                    .then_inc(reduce_out, 1)

            @block.vector
            def _(dve):
                n = [0]

                def link(ins):
                    n[0] += 1
                    ins.then_inc(prep_v, 1)
                    dve.wait_ge(prep_v, n[0])

                dve.memset(dst_int, FAR).then_inc(padded, 1)
                dve.memset(src_int, 0).then_inc(padded, 1)
                dve.memset(attr_in, 0.0).then_inc(padded, 1)
                dve.memset(zero[:], 0.0).then_inc(padded, 1)
                dve.wait_ge(edges_in, 16 * 9)
                dve.tensor_copy(dst_f, dst_int).then_inc(as_float, 1)
                dve.tensor_copy(src_f, src_int).then_inc(as_float, 1)
                dve.wait_ge(as_float, 2)
                dve.tensor_reduce(c_lo, dst_f, AX_X, ALU.min)
                link(dve.tensor_reduce(c_hi, dst_f, AX_X, ALU.max))
                dve.wait_ge(consts, 8)
                dve.tensor_tensor(act_lo, c_lo.unsqueeze(1).to_broadcast([P, NT, CB]),
                                  tile_at_end.unsqueeze(2).to_broadcast([P, NT, CB]), ALU.is_lt)
                link(dve.tensor_tensor(act_hi, c_hi.unsqueeze(1).to_broadcast([P, NT, CB]),
                                       tile_at.unsqueeze(2).to_broadcast([P, NT, CB]), ALU.is_ge))
                link(dve.tensor_tensor(act_lo, act_lo, act_hi, ALU.mult))
                link(dve.tensor_tensor(act_hi, act_lo, chunk_up.unsqueeze(1).to_broadcast([P, NT, CB]), ALU.mult))
                link(dve.tensor_tensor(act_lo, act_lo, chunk_down.unsqueeze(1).to_broadcast([P, NT, CB]),
                                       ALU.mult))
                link(dve.tensor_reduce(bounds[:, 0:NT], act_lo, AX_X, ALU.max))
                dve.tensor_reduce(bounds[:, NT:2 * NT], act_hi, AX_X, ALU.max).then_inc(reduce_in, 1)

                def place(i):
                    what, b, a = TURNS[i]
                    dve.wait_ge(turned, i + 1)
                    got = bank[:, i % 4, 0:P]
                    col = slice(b * P, (b + 1) * P)
                    to = {"dst": dst_col[:, col], "src": src_col[:, col], "attr": attr_col[:, col, a]}[what]
                    dve.tensor_copy(to, got).then_inc(placed, 1)

                for i in range(2 * CB):
                    place(i)
                dve.wait_ge(placed, 2 * CB)
                link(dve.tensor_copy(dst_ii, dst_col))
                dve.tensor_scalar(lo_i, dst_ii, P - 1, None, ALU.bitwise_and)
                link(dve.tensor_scalar(hi_i, dst_ii, 7, None, ALU.arith_shift_right))
                dve.tensor_copy(lo_b, lo_i)
                link(dve.tensor_copy(hi_b, hi_i))
                with dve.Fori(0, COLS // (2 * CG)) as i:
                    for h in range(2):
                        dve.wait_ge(counted, 2 * i + h + 1)
                        c = i * (2 * CG) + h * CG
                        dve.tensor_tensor(hot_lo[h], iota_bf.unsqueeze(1).to_broadcast([P, CG, P]),
                                          lo_b[:, ds(c, CG)].unsqueeze(2).to_broadcast([P, CG, P]), ALU.is_equal)
                        dve.tensor_tensor(hot_hi[h][:, :, 0:NT],
                                          iota_bf[:, 0:NT].unsqueeze(1).to_broadcast([P, CG, NT]),
                                          hi_b[:, ds(c, CG)].unsqueeze(2).to_broadcast([P, CG, NT]),
                                          ALU.is_equal).then_inc(hot_ready, 1)
                for i in range(2 * CB, len(TURNS)):
                    place(i)
                dve.wait_ge(reduce_out, 1)
                dve.tensor_scalar(first_f, bounds_all[:, 0:NT], -1.0, float(COLS), ALU.mult, ALU.add)
                link(dve.tensor_scalar(some, bounds_all[:, 0:NT], 0.0, None, ALU.is_gt))
                link(dve.tensor_tensor(first_m, first_f, some, ALU.mult))
                dve.tensor_copy(plan_first, first_m[0:1, :])
                link(dve.scalar_tensor_tensor(span, bounds_all[:, NT:2 * NT], float(K - 1), first_m,
                                              ALU.add, ALU.subtract))
                link(dve.tensor_copy(span_i, span))
                link(dve.tensor_scalar(groups_i, span_i, K.bit_length() - 1, None, ALU.arith_shift_right))
                link(dve.tensor_copy(groups_f, groups_i))
                link(dve.tensor_scalar(groups_m, groups_f, float(MING), None, ALU.max))
                link(dve.tensor_reduce(span[:, 0:1], groups_m, AX_X, ALU.add, negate=True))
                link(dve.tensor_copy(span_i[:, 0:1], span[:, 0:1]))
                link(dve.tensor_scalar(groups_i[:, 0:1], span_i[:, 0:1], GG - 1, None, ALU.bitwise_and))
                link(dve.tensor_copy(groups_f[:, 0:1], groups_i[:, 0:1]))
                link(dve.tensor_tensor(groups_m[:, NT - 1:NT], groups_m[:, NT - 1:NT], groups_f[:, 0:1], ALU.add))
                dve.tensor_copy(plan_groups, groups_m[0:1, :])
                link(dve.tensor_tensor(span[:, 1:2], groups_f[:, 0:1], span[:, 0:1], ALU.subtract))
                link(dve.tensor_scalar(span[:, 2:3], span[:, 1:2], 1.0 / GG, None, ALU.mult))
                dve.tensor_copy(plan_total, span[0:1, 2:3])
                dve.wait_ge(counted, COLS // CG + 3)
                link(dve.tensor_copy(deg, bank[:, 4, 0:NT]))
                dve.tensor_scalar(deg_some, deg, 0.0, None, ALU.is_gt)
                dve.tensor_scalar(deg1, deg, 1.0, None, ALU.max).then_inc(root_in, 1)
                dve.wait_ge(x_in, 32)
                tile_stats(dve, prep_v)
                n[0] += NT
                dve.wait_ge(prep_v, n[0])
                for t in range(NT):
                    last = dve.bn_aggr(ln_mv[:, t, :], ln_stats[:, t, :])
                link(last)
                dve.tensor_scalar(ln_std[:], ln_mv[:, :, 1], EPS, None, ALU.add).then_inc(root_in, 1)
                dve.wait_ge(root_out, 2)
                link(dve.reciprocal(deg_inv, deg_root))
                dve.tensor_tensor(dinv[:], deg_inv, deg_some, ALU.mult)
                dve.reciprocal(ln_rstd[:], ln_std[:])

            @block.scalar
            def _(act):
                act.wait_ge(root_in, 1)
                act.activation(deg_root, deg1, ACT.Sqrt).then_inc(root_out, 1)
                act.wait_ge(root_in, 2)
                act.activation(ln_std[:], ln_std[:], ACT.Sqrt).then_inc(root_out, 1)

            @block.tensor
            def _(pe):
                pe.wait_ge(as_float, 2)
                pe.wait_ge(consts, 1)

                def turn(i):
                    what, b, a = TURNS[i]
                    if i >= 4:
                        pe.wait_ge(placed, i - 3)
                    of = {"dst": dst_f[:, b, :], "src": src_f[:, b, :], "attr": attr_in[:, b, :, a]}[what]
                    pe.transpose(bank[:, i % 4, 0:P], of, ident[:]).then_inc(turned, 1)

                for i in range(2 * CB):
                    turn(i)
                pe.sem_inc(counted, 2)
                pe.wait_ge(padded, 4)
                pe.matmul(bank[:, 4, 0:NT], zero[:, 0:P], zero[:, 0:NT], start=True, stop=False)
                with pe.Fori(0, COLS // (2 * CG)) as i:
                    for h in range(2):
                        pe.wait_ge(hot_ready, 2 * i + h + 1)
                        for c in range(CG):
                            mm = pe.matmul(bank[:, 4, 0:NT], hot_lo[h][:, c, :], hot_hi[h][:, c, 0:NT],
                                           start=False, stop=False)
                        mm.then_inc(counted, 1)
                pe.matmul(bank[:, 4, 0:NT], zero[:, 0:P], zero[:, 0:NT], start=False, stop=True)\
                    .then_inc(counted, 1)
                for i in range(2 * CB, len(TURNS)):
                    turn(i)


        mix_w = sb("mix_w", [P, 2 * KD, D])
        edge_w = sb("edge_w", [P, KD, A])
        layer_b = sb("layer_b", [P, L, KD])
        layer_g = sb("layer_g", [P, L, KD])
        layer_s = sb("layer_s", [P, L, KD])
        gate = sem("gate")

        def gated(engine):
            engine.sem_inc(gate, 1)

        class Norm:

            def __init__(self, name):
                self.ready = sem(name + "_ready")
                self.turned = sem(name + "_turned")
                self.placed = sem(name + "_placed")

            @staticmethod
            def tiles(engine, body):
                with engine.Fori(0, NT // 4) as i:
                    for u in range(4):
                        body(i * 4 + u, u % 2)
                body(NT - 1, 0)

            def vector(self, dve, slot_free=None):
                def normalise(t, s):
                    dve.wait_ge(self.turned, t + 1)
                    if slot_free:
                        dve.wait_ge(slot_free, t + 1)
                    dve.tensor_scalar(normed[:, s, :], tile(resid, t), ln_mv[:, ds(t, 1), 0], ln_rstd[:, ds(t, 1)],
                                      ALU.subtract, ALU.mult).then_inc(self.ready, 1)

                def place(t, s):
                    dve.wait_ge(self.turned, t + 3)
                    dve.tensor_copy(feat_t[:, :, nodes(t)],
                                    bank[:, s, 0:D].rearrange("p (k n) -> p k n", k=KD)).then_inc(self.placed, 1)

                dve.sem_inc(self.placed, 2)
                normalise(0, 0)
                with dve.Fori(0, NT // 4) as i:
                    for u in range(4):
                        normalise(i * 4 + u + 1, (u + 1) % 2)
                        place(i * 4 + u, u % 2)
                place(NT - 1, 0)

            def tensor(self, pe):
                def turn(t, s):
                    pe.wait_ge(self.ready, t + 1)
                    pe.wait_ge(self.placed, t + 1)
                    for k in range(KD):
                        mm = pe.transpose(bank[:, s, k * P:(k + 1) * P], normed[:, s, k * P:(k + 1) * P], ident[:])
                    mm.then_inc(self.turned, 1)

                pe.sem_inc(self.turned, 2)
                self.tiles(pe, turn)

        first_norm = Norm("norm")
        row0_ready = sem("row0_ready")
        row0_stored = [sem(f"row0_stored{i}") for i in range(2)]
        params_in = sem("params_in")
        edge_w_zero = sem("edge_w_zero")

        with nc.Block() as block:
            @block.sync
            def _(sp):
                with nc.allow_non_contiguous_dma(reason="a few hundred parameters"):
                    sp.dma_start(layer_b[:], mlp_b.rearrange("l (k p) -> p l k", p=P)).then_inc(params_in, 16)
                    sp.dma_start(layer_g[:], bn_g.rearrange("l (k p) -> p l k", p=P)).then_inc(params_in, 16)
                    sp.dma_start(layer_s[:], bn_b.rearrange("l (k p) -> p l k", p=P)).then_inc(params_in, 16)

                def store(t, s):
                    sp.wait_ge(row0_ready, t + 3)
                    gated(sp)
                    sp.dma_start(rows0[nodes(t), :], row0_out[:, s, :]).then_inc(row0_stored[s], 16)

                Norm.tiles(sp, store)
                sp.wait_ge(params_in, 48)
                sp.wait_ge(row0_stored[0], 16 * (NT // 2 + 1))
                sp.wait_ge(row0_stored[1], 16 * (NT // 2))

            @block.vector
            def _(dve):
                dve.memset(edge_w[:], 0.0).then_inc(edge_w_zero, 1)
                first_norm.vector(dve, row0_ready)

            @block.scalar
            def _(act):
                def scale(t, s, seen):
                    act.wait_ge(first_norm.ready, t + 1)
                    wait_past(act, row0_stored[s], seen)
                    act.activation(row0_out[:, s, 0:D], normed[:, s, :], ACT.Copy, scale=dinv[:, ds(t, 1)])
                    act.activation(row0_out[:, s, D:W0], dinv[:, ds(t, 1)], ACT.Copy).then_inc(row0_ready, 1)

                act.sem_inc(row0_ready, 2)

                def four(i):
                    for u in range(4):
                        scale(i * 4 + u, u % 2, (i * 2 + u // 2) * 16)

                loop(act, NT // 4, four)
                scale(NT - 1, 0, NT // 2 * 16)

            @block.tensor
            def _(pe):
                first_norm.tensor(pe)


        room = [0]

        def graph(n):
            room[0] += n
            assert room[0] <= 3 * SET
            return sets[:, room[0] - n:room[0]]

        got = graph(K * 264).rearrange("p (j d) -> p j d", j=K)
        hot = graph(K * P).rearrange("p (j n) -> p j n", j=K)
        index = sb("index", [P, K], I32)
        summed = sb("summed", [P, D + 1 + A])
        edge_sum = sb("edge_sum", [P, NT, A])
        summed_t = sb("summed_t", [P, KD, P])
        edge_sum_t = sb("edge_sum_t", [A, P])
        edge_mix = sb("edge_mix", [A, D])
        bn_rec = graph(KD * NT * 6).rearrange("p (k t s) -> p k t s", k=KD, s=6)
        bn_mv = sb("bn_mv", [P, KD, 2])
        bn_var = sb("bn_var", [P, KD])
        bn_std = sb("bn_std", [P, KD])
        bn_inv = sb("bn_inv", [P, KD])
        bn_scale = sb("bn_scale", [P, KD])
        bn_prod = sb("bn_prod", [P, KD])
        bn_shift = sb("bn_shift", [P, KD])
        BT = 4
        NB = NT // BT + 1
        applied = graph(2 * KD * BT * P).rearrange("p (s k n) -> p s k n", s=2, k=KD)

        WA = W0 + A

        layer_in = sem("layer_in")
        mix_ready = sem("mix_ready")
        mix_made = sem("mix_made")
        index_ready = sem("index_ready")
        gathered = [sem(f"gathered{j}") for j in range(K)]
        hot_in = sem("hot_in")
        chunk_done = sem("chunk_done")
        sum_done = sem("sum_done")
        sum_taken = sem("sum_taken")
        sum_turned = sem("sum_turned")
        sum_placed = sem("sum_placed")
        mixed = sem("mixed")
        mixed_taken = sem("mixed_taken")
        attr_kept = sem("attr_kept")
        stats_v = sem("stats_v")
        var_ready = sem("var_ready")
        std_ready = sem("std_ready")
        coeffs = sem("coeffs")
        coeffs2 = sem("coeffs2")
        applied_ready = sem("applied_ready")
        applied_turned = sem("applied_turned")
        applied_kept = sem("applied_kept")
        row_turned = sem("row_turned")
        row_taken = sem("row_taken")
        block_rows = sem("block_rows")
        rows_stored = [sem(f"rows_stored{i}") for i in range(2)]

        def in_layers(engine, body):
            body(0, True, False)
            with engine.Fori(1, L - 1) as l:
                body(l, False, False)
            body(L - 1, False, True)

        def in_blocks(engine, body):
            def two(v):
                for par in range(2):
                    body(v * 2 + par, par, BT, v)

            loop(engine, NB // 2, two)
            body(NB - 1, 0, 1, NB // 2)

        def counter(engine, name):
            r = engine.alloc_register(name)
            engine.reg_mov(r, 0)
            return r

        MAX_ALL = L * NT * MAXG

        with nc.Block() as block:
            @block.sync
            def _(sp):
                def layer(l, first, final):
                    sp.wait_ge(mixed, l * NT + 1)
                    gated(sp)
                    with nc.allow_non_contiguous_dma(reason="the edge weights by features: 4 columns"):
                        sp.dma_start(mix_w[:], mlp_w[ds(l, 1), :, :].rearrange("a (k p) n -> p (a k) n", p=P))\
                            .then_inc(layer_in, 16)
                        sp.dma_start(edge_w[:, 0, A - 1:A], ew1[ds(l, 1), :, :].rearrange("a b p -> p (a b)"))\
                            .then_inc(layer_in, 16)
                        sp.dma_start(edge_w[:, 1, 0:A - 1], ew2[ds(l, 1), :, :].rearrange("a j p -> p (a j)"))\
                            .then_inc(layer_in, 16)
                    if final:
                        return

                    def store(i, par, nt, v):
                        sp.wait_ge(block_rows, l * NB + i + 1)
                        gated(sp)
                        sp.dma_start(rows[nodes(i * BT, nt), :].rearrange("(t p) d -> p t d", p=P),
                                     row_out[:, par, 0:nt, :]).then_inc(rows_stored[par], 16)

                    in_blocks(sp, store)

                in_layers(sp, layer)

            @block.gpsimd
            def _(pool):
                g = counter(pool, "pool_group")
                steps = pool.value_load(plan_total, min_val=1, max_val=NT * MAXG)

                def layer(l, first, final):
                    if not first:
                        pool.wait_ge(rows_stored[0], l * (16 * (NB // 2 + 1)))
                        pool.wait_ge(rows_stored[1], l * (16 * (NB // 2)))
                        gated(pool)
                    width = W0 if first else D
                    with pool.Fori(0, steps):
                        for u in range(GG):
                            now = pool.snap(g, min_val=0, max_val=MAX_ALL)
                            for j in range(K):
                                pool.wait_ge(index_ready, now * K + j + 1)
                                pool.wait_ge(chunk_done, now * K + j + 1)
                                gated(pool)
                                pool.indirect_dma_start(
                                    got[:, j, 0:width], None, rows0 if first else rows,
                                    bass.IndirectOffsetOnAxis(ap=index[:, j:j + 1], axis=0)).then_inc(gathered[j], 16)
                            pool.reg_add(g, g, 1)
                    if final:
                        return

                    def keep(i, par, nt, v):
                        pool.wait_ge(applied_ready, l * NB + i + 1)
                        gated(pool)
                        pool.tensor_copy(feat_t[:, :, nodes(i * BT, nt)], applied[:, par, :, 0:nt * P])\
                            .then_inc(applied_kept, 1)

                    in_blocks(pool, keep)

                pool.sem_inc(applied_kept, 2)
                in_layers(pool, layer)

            @block.scalar
            def _(act):
                g = counter(act, "act_group")
                col = counter(act, "act_column")

                def indices():
                    now = act.snap(g, min_val=0, max_val=MAX_ALL)
                    c = act.snap(col, min_val=0, max_val=COLS - K)
                    for j in range(K):
                        act.wait_ge(chunk_done, now * K + j + 1)
                        act.activation(index[:, j:j + 1], src_col[:, ds(c + j, 1)], ACT.Copy).then_inc(index_ready, 1)
                    act.reg_add(g, g, 1)
                    act.reg_add(col, col, K)

                def layer(l, first, final):
                    width = W0 + A if first else D

                    def take(t):
                        q = l * NT + t
                        act.wait_ge(sum_done, q + 1)
                        act.wait_ge(sum_turned, q + 1)
                        act.activation(summed[:, 0:width], tile(bank, t % 2)[:, 0:width], ACT.Copy,
                                       scale=dinv[:, ds(t, 1)]).then_inc(sum_taken, 1)
                        if first:
                            act.wait_ge(sum_taken, q + 3)
                            act.activation(tile(edge_sum, t), summed[:, W0:WA], ACT.Copy).then_inc(attr_kept, 1)
                        else:
                            act.activation(summed[:, W0:WA], tile(edge_sum, t), ACT.Copy).then_inc(attr_kept, 1)

                    def relu(t):
                        act.wait_ge(mixed, l * NT + t + 2)
                        for k in range(KD):
                            last = act.activation(feat_t[:, k, nodes(t)], bank[:, 3, k * P:(k + 1) * P], ACT.Relu,
                                                  bias=layer_b[:, ds(l, 1), k])
                        last.then_inc(mixed_taken, 1)

                    def start(t):
                        c = act.value_load(plan_first[:, ds(t, 1)], min_val=0, max_val=NC)
                        act.reg_mov(col, c)
                        return act.value_load(plan_groups[:, ds(t, 1)], min_val=MING, max_val=MAXG)

                    act.wait_ge(mix_ready, l + 1)
                    act.activation(edge_mix[:], bank[0:A, 4, 0:D], ACT.Copy).then_inc(mix_made, 1)
                    n = start(0)
                    with act.Fori(0, n):
                        indices()
                    with act.Fori(1, NT) as t:
                        n = start(t)
                        indices()
                        take(t - 1)
                        indices()
                        with act.Fori(2, n):
                            indices()
                        relu(t - 1)
                    take(NT - 1)
                    relu(NT - 1)
                    act.wait_ge(var_ready, l + 1)
                    act.activation(bn_std[:], bn_var[:], ACT.Sqrt).then_inc(std_ready, 1)
                    act.wait_ge(coeffs, l + 1)

                    def apply(i, par, nt, v):
                        b = l * NB + i
                        act.wait_ge(applied_turned, b + 1)
                        act.wait_ge(applied_kept, b + 1)
                        for k in range(KD):
                            last = act.activation(applied[:, par, k, 0:nt * P], feat_t[:, k, nodes(i * BT, nt)],
                                                  ACT.Identity if final else ACT.Relu,
                                                  bias=bn_shift[:, k:k + 1], scale=bn_scale[:, k:k + 1])
                        last.then_inc(applied_ready, 1)
                        if final:
                            act.sem_inc(applied_kept, 1)

                    in_blocks(act, apply)

                act.sem_inc(sum_taken, 2)
                act.sem_inc(mixed_taken, 1)
                in_layers(act, layer)

            @block.vector
            def _(dve):
                g = counter(dve, "dve_group")
                col = counter(dve, "dve_column")
                CHAIN = 4

                def layer(l, first, final):
                    def hots(t):
                        now = dve.snap(g, min_val=0, max_val=MAX_ALL)
                        c = dve.snap(col, min_val=0, max_val=COLS - K)
                        for j in range(K):
                            dve.wait_ge(chunk_done, now * K + j + 1)
                            ins = dve.tensor_scalar(hot[:, j, :], iota_row[:], dst_col[:, ds(c + j, 1)],
                                                    neg_base[:, ds(t, 1)], ALU.subtract, ALU.is_equal)
                            if first:
                                dve.wait_ge(gathered[j], now * 16 + 16)
                                ins = dve.tensor_scalar(got[:, j, W0:WA], tile(attr_col, c + j),
                                                        got[:, j, D:W0], None, ALU.mult)
                            ins.then_inc(hot_in, 1)
                        dve.reg_add(g, g, 1)
                        dve.reg_add(col, col, K)

                    def place(t):
                        q = l * NT + t
                        dve.wait_ge(sum_turned, q + 2)
                        dve.wait_ge(mixed, q + 1)
                        dve.tensor_copy(summed_t[:], bank[:, 2, 0:D].rearrange("p (k n) -> p k n", k=KD))
                        dve.tensor_copy(edge_sum_t[:], bank[0:A, 2, D:D + P]).then_inc(sum_placed, 1)

                    def stats(t, n):
                        dve.wait_ge(mixed_taken, l * NT + t + 2)
                        for k in range(KD):
                            last = dve.bn_stats(bn_rec[:, k, ds(t, 1), :].rearrange("p a s -> p (a s)"),
                                                feat_t[:, k, ds(t * P, n)])
                        return last

                    def start(t):
                        c = dve.value_load(plan_first[:, ds(t, 1)], min_val=0, max_val=NC)
                        dve.reg_mov(col, c)
                        return dve.value_load(plan_groups[:, ds(t, 1)], min_val=MING, max_val=MAXG)

                    n = start(0)
                    with dve.Fori(0, n):
                        hots(0)
                    with dve.Fori(1, NT) as t:
                        n = start(t)
                        hots(t)
                        hots(t)
                        place(t - 1)
                        with dve.Fori(2, n):
                            hots(t)
                        stats(t - 1, P)
                    place(NT - 1)
                    links = [0]

                    def link(ins):
                        links[0] += 1
                        ins.then_inc(stats_v, 1)
                        dve.wait_ge(stats_v, l * CHAIN + links[0])

                    link(stats(NT - 1, LAST))
                    gated(dve)
                    for k in range(KD):
                        last = dve.bn_aggr(bn_mv[:, k, :], bn_rec[:, k, :, :].rearrange("p t s -> p (t s)"))
                    link(last)
                    dve.tensor_scalar(bn_var[:], bn_mv[:, :, 1], EPS, None, ALU.add).then_inc(var_ready, 1)
                    dve.wait_ge(std_ready, l + 1)
                    link(dve.reciprocal(bn_inv[:], bn_std[:]))
                    link(dve.tensor_tensor(bn_scale[:], bn_inv[:], tile(layer_g, l), ALU.mult))
                    assert links[0] == CHAIN
                    dve.tensor_tensor(bn_prod[:], bn_mv[:, :, 0], bn_scale[:], ALU.mult).then_inc(coeffs2, 1)
                    dve.wait_ge(coeffs2, l + 1)
                    dve.tensor_tensor(bn_shift[:], tile(layer_s, l), bn_prod[:], ALU.subtract).then_inc(coeffs, 1)

                    def take(i, par, nt, v):
                        if not final:
                            wait_past(dve, rows_stored[par], l * (16 * (NB // 2 + 1 - par)) + v * 16)
                        for u in range(nt):
                            t = i * BT + u
                            dve.wait_ge(row_turned, l * NT + t + 1)
                            if final:
                                dve.tensor_tensor(tile(resid, t), bank[:, 5 + u % 2, 0:D], tile(resid, t), ALU.add)\
                                    .then_inc(row_taken, 1)
                            else:
                                last = dve.tensor_scalar(row_out[:, par, u, :], bank[:, 5 + u % 2, 0:D],
                                                         dinv[:, ds(t, 1)], None, ALU.mult)
                                last.then_inc(row_taken, 1)
                        if not final:
                            dve.wait_ge(row_taken, l * NT + i * BT + nt + 2)
                            dve.sem_inc(block_rows, 1)

                    in_blocks(dve, take)

                dve.sem_inc(row_taken, 2)
                dve.sem_inc(sum_placed, 1)
                in_layers(dve, layer)

            @block.tensor
            def _(pe):
                g = counter(pe, "pe_group")

                def layer(l, first, final):
                    width = W0 + A if first else D

                    def sums(t, opening=False):
                        now = pe.snap(g, min_val=0, max_val=MAX_ALL)
                        for j in range(K):
                            pe.wait_ge(gathered[j], now * 16 + 16)
                            pe.wait_ge(hot_in, now * K + j + 1)
                            pe.matmul(tile(bank, t % 2)[:, 0:width], hot[:, j, :], got[:, j, 0:width],
                                      start=opening and j == 0, stop=False).then_inc(chunk_done, 1)
                        pe.reg_add(g, g, 1)

                    def open_tile(t):
                        pe.wait_ge(sum_taken, l * NT + t + 1)
                        sums(t, True)

                    def close(t):
                        pe.matmul(tile(bank, t % 2)[:, 0:width], zero[:, 0:P], zero[:, 0:width],
                                  start=False, stop=True).then_inc(sum_done, 1)

                    def turn(t):
                        q = l * NT + t
                        pe.wait_ge(attr_kept, q + 1)
                        pe.wait_ge(sum_taken, q + 3)
                        pe.wait_ge(sum_placed, q + 1)
                        for k in range(KD):
                            pe.transpose(bank[:, 2, k * P:(k + 1) * P], summed[:, k * P:(k + 1) * P], ident[:])
                        pe.transpose(bank[0:A, 2, D:D + P], summed[:, W0:WA], ident[:]).then_inc(sum_turned, 1)

                    def mix(t):
                        q = l * NT + t
                        pe.wait_ge(sum_placed, q + 2)
                        pe.wait_ge(mixed_taken, q + 1)
                        for f in range(KD):
                            o = bank[:, 3, f * P:(f + 1) * P]
                            c = slice(f * P, (f + 1) * P)
                            for k in range(KD):
                                pe.matmul(o, mix_w[:, k, c], feat_t[:, k, nodes(t)], start=k == 0, stop=False)
                            for k in range(KD):
                                pe.matmul(o, mix_w[:, KD + k, c], summed_t[:, k, :], start=False, stop=False)
                            mm = pe.matmul(o, edge_mix[:, c], edge_sum_t[:], start=False, stop=True)
                        mm.then_inc(mixed, 1)

                    def rest(t, n, start):
                        with pe.Fori(start, n):
                            sums(t)
                        close(t)

                    def size(t):
                        return pe.value_load(plan_groups[:, ds(t, 1)], min_val=MING, max_val=MAXG)

                    pe.wait_ge(layer_in, (l + 1) * 48)
                    if not first:
                        pe.wait_ge(applied_kept, l * NB + 2)
                    for k in range(KD):
                        mm = pe.matmul(bank[0:A, 4, 0:D], edge_w[:, k, :], mix_w[:, KD + k, :],
                                       start=k == 0, stop=k == KD - 1)
                    mm.then_inc(mix_ready, 1)
                    pe.wait_ge(mix_made, l + 1)
                    gated(pe)
                    n = size(0)
                    open_tile(0)
                    rest(0, n, 1)
                    with pe.Fori(1, NT) as t:
                        n = size(t)
                        open_tile(t)
                        turn(t - 1)
                        sums(t)
                        mix(t - 1)
                        rest(t, n, 2)
                    turn(NT - 1)
                    mix(NT - 1)

                    def turn_block(i, par, nt, v):
                        pe.wait_ge(applied_ready, l * NB + i + 1)
                        for u in range(nt):
                            pe.wait_ge(row_taken, l * NT + i * BT + u + 1)
                            for k in range(KD):
                                mm = pe.transpose(bank[:, 5 + u % 2, k * P:(k + 1) * P],
                                                  applied[:, par, k, u * P:(u + 1) * P], ident[:])
                            mm.then_inc(row_turned, 1)
                        pe.wait_ge(row_turned, l * NT + i * BT + nt)
                        pe.sem_inc(applied_turned, 1)

                    in_blocks(pe, turn_block)

                pe.sem_inc(chunk_done, K)
                pe.sem_inc(sum_turned, 1)
                pe.sem_inc(mixed, 1)
                pe.sem_inc(applied_turned, 2)
                in_layers(pe, layer)


        route_w = sb("route_w", [P, KD, X])
        bias1 = sb("bias1", [P, (X + 1) * KF])
        slot_of = sb("slot_of", [P, NT, 2], I32)
        weight_of = sb("weight_of", [P, NT, 2])
        plan_x = sb("plan_x", [1, 2 * X + 1], I32)

        second_norm = Norm("norm2")
        stats2_v = sem("stats2_v")
        var2_ready = sem("var2_ready")
        std2_ready = sem("std2_ready")
        logits_done = sem("logits_done")
        route_w_in = sem("route_w_in")
        bias1_in = sem("bias1_in")
        bias1_turned = sem("bias1_turned")
        sets_in = sem("sets_in")

        free = [0]

        def room(n):
            free[0] += n
            assert free[0] <= arena.shape[1]
            return arena[:, free[0] - n:free[0]]

        bias1_rows = room(P)

        def load_set(engine, s, w1, w2, done):
            engine.dma_start(w1_set(s), w1).then_inc(done, 16)
            engine.dma_start(w2_set(s), w2).then_inc(done, 16)

        with nc.Block() as block:
            @block.sync
            def _(sp):
                sp.dma_start(route_w[:], wr.rearrange("(k p) e -> p k e", p=P)).then_inc(route_w_in, 16)
                sp.dma_start(bias1_rows[0:X * KF, :], b1p.rearrange("x (c p) -> (x c) p", p=P)).then_inc(bias1_in, 16)
                sp.dma_start(bias1_rows[X * KF:(X + 1) * KF, :], b1s.rearrange("(c p) -> c p", p=P))\
                    .then_inc(bias1_in, 16)
                load_set(sp, 2, w1s.rearrange("(k p) f -> p k f", p=P), w2s.rearrange("(c p) d -> p c d", p=P), sets_in)
                for e in range(2):
                    load_set(sp, e, w1p[e].rearrange("(k p) f -> p k f", p=P),
                             w2p[e].rearrange("(c p) d -> p c d", p=P), sets_in)
                sp.wait_ge(sets_in, 96)

            @block.vector
            def _(dve):
                tile_stats(dve, stats2_v)
                dve.wait_ge(stats2_v, NT)
                for t in range(NT):
                    last = dve.bn_aggr(ln_mv[:, t, :], ln_stats[:, t, :])
                last.then_inc(stats2_v, 1)
                dve.wait_ge(stats2_v, NT + 1)
                dve.tensor_scalar(ln_std[:], ln_mv[:, :, 1], EPS, None, ALU.add).then_inc(var2_ready, 1)
                dve.wait_ge(std2_ready, 1)
                dve.reciprocal(ln_rstd[:], ln_std[:]).then_inc(stats2_v, 1)
                dve.wait_ge(stats2_v, NT + 2)
                second_norm.vector(dve)
                dve.wait_ge(bias1_turned, 1)
                dve.tensor_copy(bias1[:], bank[:, 2, 0:(X + 1) * KF])

            @block.scalar
            def _(act):
                act.wait_ge(var2_ready, 1)
                act.activation(ln_std[:], ln_std[:], ACT.Sqrt).then_inc(std2_ready, 1)

            @block.tensor
            def _(pe):
                pe.wait_ge(bias1_in, 32)
                pe.transpose(bank[:, 2, 0:(X + 1) * KF], bias1_rows[0:(X + 1) * KF, :],
                             ident[0:(X + 1) * KF, 0:(X + 1) * KF]).then_inc(bias1_turned, 1)
                second_norm.tensor(pe)
                pe.wait_ge(route_w_in, 16)
                pe.wait_ge(second_norm.placed, NT + 2)
                for t in range(NT):
                    for k in range(KD):
                        mm = pe.matmul(bank[:, 7, t * X:(t + 1) * X], feat_t[:, k, t * P:(t + 1) * P],
                                       route_w[:, k, :], start=k == 0, stop=k == KD - 1)
                mm.then_inc(logits_done, 1)

        free[0] = 0

        def per_expert():
            return room(NT * X).rearrange("p (t e) -> p t e", e=X)

        def over_experts(v):
            return v.unsqueeze(2).to_broadcast([P, NT, X])

        logit, prob, prob2, score, pick1, pick2, place_all, until = (per_expert() for _ in range(8))
        top1, top2, most, total_p, real, node_no = (room(NT) for _ in range(6))
        order = room(X)
        region = room(X)
        counts = room(X)
        counts_up = room(X)
        counts_i = room(X).bitcast(I32)
        blocks_i = room(X).bitcast(I32)
        blocks_f = room(X)
        picks_b = room(NT * X // 2).bitcast(BF16)
        before = room(P // 2).bitcast(BF16)
        ones_b = room(P // 2).bitcast(BF16)

        route_c = sem("route_c")
        route_v = sem("route_v")
        shifted = sem("shifted")
        powers = sem("powers")
        picked = sem("picked")
        ranked = sem("ranked")

        with nc.Block() as block:
            @block.gpsimd
            def _(pool):
                imp = dict(allow_small_or_imprecise_dtypes=True)
                pool.iota(order, [[-1, X]], X, 0, **imp).then_inc(route_c, 1)
                pool.iota(node_no, [[P, NT]], 0, 1, **imp).then_inc(route_c, 1)
                pool.memset(ones_b, 1.0).then_inc(route_c, 1)
                pool.wait_ge(route_c, 3)
                pool.affine_select(out=before, in_=ones_b, compare_op=ALU.is_gt, fill=0.0, base=0,
                                   pattern=[[1, P]], channel_multiplier=-1).then_inc(route_c, 1)

            @block.scalar
            def _(act):
                act.wait_ge(shifted, 1)
                act.activation(prob, prob2, ACT.Exp).then_inc(powers, 1)

            @block.tensor
            def _(pe):
                pe.wait_ge(picked, 1)
                pe.wait_ge(route_c, 4)
                pe.matmul(bank[:, 5, 0:NT * X], before, picks_b, start=True, stop=True)
                pe.matmul(bank[:, 6, 0:NT * X], ones_b, picks_b, start=True, stop=True).then_inc(ranked, 1)

            @block.vector
            def _(dve):
                n = [0]

                def link(ins):
                    n[0] += 1
                    ins.then_inc(route_v, 1)
                    dve.wait_ge(route_v, n[0])

                dve.wait_ge(route_c, 4)
                link(dve.tensor_copy(logit, bank[:, 7, 0:NT * X].rearrange("p (t e) -> p t e", e=X)))
                link(dve.tensor_reduce(most, logit, AX_X, ALU.max))
                dve.tensor_tensor(prob2, logit, over_experts(most), ALU.subtract).then_inc(shifted, 1)
                dve.tensor_scalar(real, node_no, float(N), None, ALU.is_lt)
                dve.wait_ge(powers, 1)
                link(dve.tensor_reduce(total_p, prob, AX_X, ALU.add))
                link(dve.reciprocal(most, total_p))
                link(dve.tensor_tensor(prob, prob, over_experts(most), ALU.mult))

                def pick(probs, top, into):
                    link(dve.tensor_reduce(top, probs, AX_X, ALU.max))
                    link(dve.tensor_tensor(score, probs, over_experts(top), ALU.is_equal))
                    link(dve.tensor_tensor(score, score, order.unsqueeze(1).to_broadcast([P, NT, X]), ALU.mult))
                    link(dve.tensor_reduce(most, score, AX_X, ALU.max))
                    link(dve.tensor_tensor(into, score, over_experts(most), ALU.is_equal))

                pick(prob, top1, pick1)
                link(dve.scalar_tensor_tensor(prob2, pick1, -2.0, prob, ALU.mult, ALU.add))
                pick(prob2, top2, pick2)
                link(dve.tensor_tensor(total_p, top1, top2, ALU.add))
                link(dve.reciprocal(most, total_p))
                dve.tensor_tensor(weight_of[:, :, 0], top1, most, ALU.mult)
                dve.tensor_tensor(weight_of[:, :, 1], top2, most, ALU.mult)
                dve.tensor_tensor(pick1, pick1, over_experts(real), ALU.mult)
                link(dve.tensor_tensor(pick2, pick2, over_experts(real), ALU.mult))
                dve.tensor_tensor(picks_b.rearrange("p (t e) -> p t e", e=X), pick1, pick2, ALU.add)\
                    .then_inc(picked, 1)
                dve.wait_ge(ranked, 1)
                link(dve.tensor_copy(score, bank[:, 6, 0:NT * X].rearrange("p (t e) -> p t e", e=X)))
                dve.memset(top1, 1.0).then_inc(route_v, 1)
                n[0] += 1
                dve.wait_ge(route_v, n[0])
                for e in range(X):
                    last = dve.tensor_tensor_scan(until[:, :, e], top1, score[:, :, e], 0.0, ALU.mult, ALU.add)
                link(last)
                link(dve.tensor_tensor(place_all, until, score, ALU.subtract))
                link(dve.tensor_scalar(counts_up, until[:, NT - 1, :], float(TOK - 1), None, ALU.add))
                link(dve.tensor_copy(counts_i, counts_up))
                link(dve.tensor_scalar(blocks_i, counts_i, TOK.bit_length() - 1, None, ALU.arith_shift_right))
                link(dve.tensor_copy(blocks_f, blocks_i))
                link(dve.tensor_scalar(counts, blocks_f, 1.0, None, ALU.max))
                dve.tensor_copy(plan_x[:, X:2 * X], counts[0:1, :])
                link(dve.tensor_tensor_scan(blocks_f, top1[:, 0:X], counts, 0.0, ALU.mult, ALU.add))
                dve.tensor_scalar(plan_x[:, 2 * X:2 * X + 1], blocks_f[0:1, X - 1:X], float(TOK), None, ALU.mult)
                link(dve.tensor_tensor(counts_up, blocks_f, counts, ALU.subtract))
                link(dve.tensor_scalar(region, counts_up, float(TOK), None, ALU.mult))
                link(dve.tensor_tensor(counts, region, until[:, NT - 1, :], ALU.add))
                dve.tensor_copy(plan_x[:, 0:X], counts[0:1, :])
                link(dve.tensor_tensor(place_all, place_all, region.unsqueeze(1).to_broadcast([P, NT, X]), ALU.add))
                link(dve.tensor_tensor(place_all, place_all,
                                       bank[:, 5, 0:NT * X].rearrange("p (t e) -> p t e", e=X), ALU.add))
                dve.tensor_tensor(prob, place_all, pick1, ALU.mult)
                link(dve.tensor_tensor(prob2, place_all, pick2, ALU.mult))
                dve.tensor_reduce(top1, prob, AX_X, ALU.add)
                link(dve.tensor_reduce(top2, prob2, AX_X, ALU.add))
                dve.tensor_copy(slot_of[:, :, 0], top1)
                dve.tensor_copy(slot_of[:, :, 1], top2)


        free[0] = 0
        hidden = room(KF * TOK).rearrange("p (c n) -> p c n", c=KF)
        bias2 = room((X + 1) * D).rearrange("p (x d) -> p x d", d=D)
        block_in = room(TB * D).rearrange("p (u d) -> p u d", u=TB)
        block_out = room(TB * D).rearrange("p (u d) -> p u d", u=TB)
        block_t = normed
        send = row_out[:, 0, :, :]
        fetched = row_out
        send_at = sb("send_at", [P, 4, 2], I32)
        turned_rows = mix_w[:, :, :].rearrange("p (s k) n -> p s k n", s=2)

        bias2_in = sem("bias2_in")
        tail_zero = sem("tail_zero")
        tails_in = sem("tails_in")
        results_zero = sem("results_zero")

        def block_rows_of(ap, b):
            return ap[ds(b * TOK, TOK), :].rearrange("(u p) d -> p u d", p=P)

        send_ready = sem("send_ready")
        sent = [sem(f"sent{u}") for u in range(4)]
        bias_added = sem("bias_added")

        class Expert:

            def __init__(self, name):
                self.up_done = sem(name + "_up_done")
                self.hidden_ready = sem(name + "_hidden_ready")
                self.down_done = sem(name + "_down_done")
                self.sums_taken = sem(name + "_sums_taken")

            def tensor(self, pe, at, s, rows_in, nt, between=None):
                w1, w2 = w1_set(s), w2_set(s)

                def up(c):
                    pe.wait_ge(self.hidden_ready, at * KF + c + 1)
                    for k in range(KD):
                        mm = pe.matmul(bank[:, c % 4, 0:nt * P], w1[:, k, c * P:(c + 1) * P], rows_in(k),
                                       start=k == 0, stop=k == KD - 1)
                    mm.then_inc(self.up_done, 1)

                def down(c):
                    pe.wait_ge(self.hidden_ready, at * KF + c + 5)
                    if c == 0:
                        pe.wait_ge(self.sums_taken, at + 1)
                    for u in range(nt):
                        mm = pe.matmul(bank[:, 4 + u, 0:D], hidden[:, c, u * P:(u + 1) * P], w2[:, c, :],
                                       start=c == 0, stop=c == KF - 1)
                    mm.then_inc(self.down_done, 1)

                up(0)
                for c in range(1, KF):
                    up(c)
                    down(c - 1)
                    if between and c == KF // 2:
                        between()
                down(KF - 1)

            def scalar(self, act, at, bias, nt):
                for c in range(KF):
                    act.wait_ge(self.up_done, at * KF + c + 1)
                    act.wait_ge(self.down_done, at * KF + c + 1)
                    act.activation(hidden[:, c, 0:nt * P], bank[:, c % 4, 0:nt * P], ACT.Gelu,
                                   bias=bias(c)).then_inc(self.hidden_ready, 1)

        shared = Expert("shared")
        NS = NT // TB

        with nc.Block() as block:
            @block.sync
            def _(sp):
                sp.dma_start(bias2[:, X, :], b2s.partition_broadcast(P)).then_inc(bias2_in, 16)
                sp.dma_start(bias2[:, 0:X, :].rearrange("p x d -> p (x d)"),
                             b2p.rearrange("x d -> (x d)").partition_broadcast(P)).then_inc(bias2_in, 16)
                sp.wait_ge(tail_zero, 1)
                for e in range(X + 1):
                    at = e if e < X else 2 * X
                    n = sp.value_load(plan_x[:, at:at + 1], min_val=0, max_val=MAXB * TOK)
                    sp.dma_start(expert_in[ds(n, TOK), :].rearrange("(u p) d -> p u d", p=P), block_in)\
                        .then_inc(tails_in, 16)
                    sp.wait_ge(tails_in, 16 * (e + 1))
                with sp.Fori(0, MAXB) as b:
                    sp.dma_start(block_rows_of(expert_out, b), block_in).then_inc(results_zero, 16)
                sp.wait_ge(results_zero, 16 * MAXB)
                sp.wait_ge(bias2_in, 32)

            @block.gpsimd
            def _(pool):
                def scatter(t, u, p):
                    pool.wait_ge(send_ready, t + 1)
                    gated(pool)
                    for w in range(2):
                        pool.indirect_dma_start(expert_in, bass.IndirectOffsetOnAxis(ap=send_at[0:p, u, w:w + 1], axis=0),
                                                send[0:p, u, :], None).then_inc(sent[u], 16)

                pool.wait_ge(tails_in, 16 * (X + 1))
                with pool.Fori(0, NT // 4) as i:
                    for u in range(4):
                        scatter(i * 4 + u, u, P)
                scatter(NT - 1, 0, LAST)
                pool.wait_ge(sent[0], 32 * (NT // 4 + 1))
                for u in range(1, 4):
                    pool.wait_ge(sent[u], 32 * (NT // 4))

            @block.scalar
            def _(act):
                def bias(c):
                    return bias1[:, X * KF + c:X * KF + c + 1]

                act.sem_inc(shared.hidden_ready, 4)
                with act.Fori(0, NS) as b:
                    shared.scalar(act, b, bias, TB)
                shared.scalar(act, NS, bias, 1)

            @block.vector
            def _(dve):
                dve.memset(block_in, 0.0).then_inc(tail_zero, 1)
                dve.wait_ge(bias2_in, 32)

                def prepare(t, u, seen):
                    wait_past(dve, sent[u], seen)
                    dve.tensor_scalar(send[:, u, :], tile(resid, t), ln_mv[:, ds(t, 1), 0], ln_rstd[:, ds(t, 1)],
                                      ALU.subtract, ALU.mult)
                    dve.tensor_copy(send_at[:, u, :], tile(slot_of, t)).then_inc(send_ready, 1)
                    dve.tensor_tensor(tile(resid, t), tile(resid, t), bias2[:, X, :], ALU.add).then_inc(bias_added, 1)

                def take(b, nt):
                    dve.wait_ge(shared.down_done, b * KF + 2 * KF)
                    dve.wait_ge(bias_added, b * TB + nt)
                    for u in range(nt):
                        last = dve.tensor_tensor(tile(resid, b * TB + u), bank[:, 4 + u, 0:D],
                                                 tile(resid, b * TB + u), ALU.add)
                    last.then_inc(shared.sums_taken, 1)

                def four(i):
                    for u in range(4):
                        prepare(i * 4 + u, u, i * 32)
                    for h in range(2):
                        take(i * 2 + h, TB)

                dve.sem_inc(shared.sums_taken, 1)
                loop(dve, NT // 4, four)
                prepare(NT - 1, 0, 32 * (NT // 4))
                take(NS, 1)

            @block.tensor
            def _(pe):
                pe.sem_inc(shared.down_done, KF)
                with pe.Fori(0, NS) as b:
                    shared.tensor(pe, b, 2, lambda k: feat_t[:, k, nodes(b * TB, TB)], TB)
                shared.tensor(pe, NS, 2, lambda k: feat_t[:, k, nodes(NT - 1)], 1)

        routed = Expert("routed")
        rows_in = sem("rows_in")
        rows_turned = sem("rows_turned")
        rows_placed = sem("rows_placed")
        out_stored = sem("out_stored")
        out_free = sem("out_free")
        expert_done = sem("expert_done")
        weights_in = [sem(f"weights_in{s}") for s in range(2)]
        set_ready = [sem(f"set_ready{s}") for s in range(2)]
        def experts(engine, name, body, before=None, after=None):
            r = counter(engine, name)
            with engine.Fori(0, X // 2) as v:
                for s in range(2):
                    e = v * 2 + s
                    if before:
                        before(e, s, v)
                    n = engine.value_load(plan_x[:, ds(e + X, 1)], min_val=1, max_val=EACH)
                    with engine.Fori(0, n):
                        at = engine.snap(r, min_val=0, max_val=MAXB - 1)
                        body(e, s, at)
                        engine.reg_add(r, r, 1)
                    if after:
                        after()
            return engine.snap(r, min_val=0, max_val=MAXB)

        with nc.Block() as block:
            @block.sync
            def _(sp):
                def load(at):
                    sp.wait_ge(rows_turned, at + 1)
                    gated(sp)
                    sp.dma_start(block_in, block_rows_of(expert_in, at)).then_inc(rows_in, 16)

                def body(e, s, at):
                    load(at + 1)
                    sp.wait_ge(routed.sums_taken, at + 2)
                    gated(sp)
                    sp.dma_start(block_rows_of(expert_out, at), block_out).then_inc(out_stored, 16)
                    sp.wait_ge(out_stored, at * 16 + 16)
                    sp.sem_inc(out_free, 1)

                sp.sem_inc(out_free, 1)
                load(0)
                at = experts(sp, "sp_blocks", body)
                sp.wait_ge(rows_in, at * 16 + 16)
                gated(sp)

            @block.gpsimd
            def _(pool):
                for s in range(2):
                    pool.sem_inc(set_ready[s], 1)
                with pool.Fori(0, X // 2 - 1) as v:
                    for s in range(2):
                        pool.wait_ge(expert_done, v * 2 + s + 1)
                        gated(pool)
                        e = v * 2 + (s + 2)
                        load_set(pool, s, w1p[ds(e, 1), :, :].rearrange("a (k p) f -> p (a k) f", p=P),
                                 w2p[ds(e, 1), :, :].rearrange("a (c p) d -> p (a c) d", p=P), weights_in[s])
                        pool.wait_ge(weights_in[s], v * 32 + 32)
                        pool.sem_inc(set_ready[s], 1)

            @block.scalar
            def _(act):
                def body(e, s, at):
                    routed.scalar(act, at, lambda c: bias1[:, ds(e * KF + c, 1)], TB)

                act.sem_inc(routed.hidden_ready, 4)
                experts(act, "act_blocks", body)

            @block.vector
            def _(dve):
                def place(at):
                    dve.wait_ge(rows_turned, at + 2)
                    dve.tensor_copy(turned_rows[:, ds(at % 2, 1), :, :].rearrange("p a k n -> p (a k) n"),
                                    bank[:, 6, :].rearrange("p (k n) -> p k n", k=KD)).then_inc(rows_placed, 1)

                def body(e, s, at):
                    place(at + 1)
                    dve.wait_ge(routed.down_done, at * KF + 2 * KF)
                    dve.wait_ge(out_free, at + 1)
                    for u in range(TB):
                        last = dve.tensor_tensor(block_out[:, u, :], bank[:, 4 + u, 0:D], tile(bias2, e), ALU.add)
                    last.then_inc(routed.sums_taken, 1)

                dve.sem_inc(rows_placed, 1)
                dve.sem_inc(routed.sums_taken, 1)
                place(0)
                experts(dve, "dve_blocks", body)

            @block.tensor
            def _(pe):
                def turn(at):
                    pe.wait_ge(rows_in, at * 16 + 16)
                    pe.wait_ge(rows_placed, at + 1)
                    for k in range(KD):
                        for u in range(TB):
                            mm = pe.transpose(bank[:, 6, (k * TB + u) * P:(k * TB + u + 1) * P],
                                              block_in[:, u, k * P:(k + 1) * P], ident[:])
                    mm.then_inc(rows_turned, 1)

                def before(e, s, v):
                    pe.wait_ge(set_ready[s], v + 1)
                    gated(pe)

                def body(e, s, at):
                    pe.wait_ge(rows_placed, at + 2)
                    slot = turned_rows[:, ds(at % 2, 1), :, :].rearrange("p a k n -> p (a k) n")
                    routed.tensor(pe, at, s, lambda k: slot[:, k, :], TB, between=lambda: turn(at + 1))

                pe.sem_inc(routed.down_done, KF)
                pe.sem_inc(rows_turned, 1)
                turn(0)
                experts(pe, "pe_blocks", body, before,
                        lambda: pe.matmul(bank[:, 7, 0:8], zero[:, 0:P], zero[:, 0:8], start=True, stop=True)
                        .then_inc(expert_done, 1))

        fetch_at = send_at
        fetch_ready = sem("fetch_ready")
        fetched_in = [sem(f"fetched_in{u}") for u in range(4)]
        half_added = sem("half_added")
        added = sem("added")
        stored = [sem(f"stored{u}") for u in range(4)]

        def fours(engine, body):
            def four(i):
                for u in range(4):
                    body(i * 4 + u, u, i, P)

            loop(engine, NT // 4, four)
            body(NT - 1, 0, NT // 4, LAST)

        with nc.Block() as block:
            @block.sync
            def _(sp):
                def store(t, u, i, p):
                    sp.wait_ge(added, t + 1)
                    gated(sp)
                    sp.dma_start(out[ds(t * P, p), :], tile(resid, t)[0:p, :]).then_inc(stored[u], 16)

                fours(sp, store)
                sp.wait_ge(stored[0], 16 * (NT // 4 + 1))
                for u in range(1, 4):
                    sp.wait_ge(stored[u], 16 * (NT // 4))

            @block.gpsimd
            def _(pool):
                def fetch(t, u, i, p):
                    pool.wait_ge(fetch_ready, t + 1)
                    wait_past(pool, added, i * 4)
                    gated(pool)
                    for w in range(2):
                        pool.indirect_dma_start(
                            fetched[:, w, u, :], None, expert_out,
                            bass.IndirectOffsetOnAxis(ap=fetch_at[:, u, w:w + 1], axis=0)).then_inc(fetched_in[u], 16)

                fours(pool, fetch)

            @block.scalar
            def _(act):
                def indices(t, u, i, p):
                    wait_past(act, fetched_in[u], i * 32)
                    act.activation(fetch_at[:, u, :], tile(slot_of, t), ACT.Copy).then_inc(fetch_ready, 1)

                fours(act, indices)

            @block.vector
            def _(dve):
                def add(t, u, i, p):
                    dve.wait_ge(fetched_in[u], i * 32 + 32)
                    for w in range(2):
                        dve.scalar_tensor_tensor(tile(resid, t), fetched[:, w, u, :], tile(weight_of, t)[:, w:w + 1],
                                                 tile(resid, t), ALU.mult, ALU.add)\
                            .then_inc([half_added, added][w], 1)
                        if w == 0:
                            dve.wait_ge(half_added, t + 1)

                fours(dve, add)


_INS = ['x', 'src', 'dst', 'edge_attr_4', 'L0_gnn_mlp_w', 'L0_gnn_mlp_b', 'L0_gnn_ew1', 'L0_gnn_ew2',
        'L0_gnn_bn_g', 'L0_gnn_bn_b', 'L0_ffn_Wr', 'L0_ffn_W1s', 'L0_ffn_b1s', 'L0_ffn_W2s', 'L0_ffn_b2s',
        'L0_ffn_W1p', 'L0_ffn_b1p', 'L0_ffn_W2p', 'L0_ffn_b2p']
_OUTS = [((6250, 256), 'float32')]


def kernel(**inputs):
    import numpy as _np
    import concourse.bacc as _bacc
    from concourse import mybir as _mybir
    from concourse.bass_utils import run_bass_kernel_spmd as _run

    nc = _bacc.Bacc("TRN2", target_bir_lowering=False, num_devices=1)
    arrays, args = {}, []
    for name in _INS:
        a = _np.ascontiguousarray(inputs[name])
        arrays[f"in_{name}_dram"] = a
        args.append(nc.dram_tensor(f"in_{name}_dram", a.shape, _mybir.dt.from_np(a.dtype), kind="ExternalInput").ap())
    for i, (shape, dtype) in enumerate(_OUTS):
        dt = _mybir.dt.from_np(_np.dtype(dtype))
        args.append(nc.dram_tensor(f"out_{i}_dram", shape, dt, kind="ExternalOutput").ap())
    build(nc, *args)
    r = _run(nc, [arrays], core_ids=[0])
    got = tuple(r.results[0][f"out_{i}_dram"] for i in range(len(_OUTS)))
    return got[0]
```

```python
from contextlib import ExitStack

import concourse.bass as bass
from concourse import mybir

F32 = mybir.dt.float32
BF16 = mybir.dt.bfloat16
I32 = mybir.dt.int32
ALU = mybir.AluOpType
ACT = mybir.ActivationFunctionType
AX_X = mybir.AxisListType.X
ds = bass.ds

P = 128
K = 8
GG = 2
MINS = 1
EPS = 1e-5
FAR = 1000000


def build(nc, x, src, dst, attr, mlp_w, mlp_b, ew1, ew2, bn_g, bn_b,
          wr, w1s, b1s, w2s, b2s, w1p, b1p, w2p, b2p, out):
    N, D = x.shape
    E = src.shape[0]
    L = mlp_w.shape[0]
    X = wr.shape[1]
    F = w1s.shape[1]
    A = attr.shape[1]
    KD = D // P
    KF = F // P
    NT = -(-N // P)
    LAST = N - (NT - 1) * P
    NP = NT * P
    NC = -(-E // P)
    CB = -(-NC // P)
    COLS = CB * P
    FULLC = E // P
    REST = E - FULLC * P
    MAXG = -(-NC // K) + GG + 1
    W0 = D + 1
    TB = 2
    TOK = TB * P
    EACH = -(-N // TOK)
    MAXB = 2 * N // TOK + X
    assert KD == 2 and NC + K * (MINS + GG + 1) < COLS and REST > 0 and L >= 3
    assert (NT - 1) % 4 == 0 and NT * X <= 512

    rows0 = nc.dram_tensor("rows0", (NP, W0), F32).ap()
    rows = nc.dram_tensor("rows", (NP, D), F32).ap()
    expert_in = nc.dram_tensor("expert_in", ((MAXB + 1) * TOK, D), F32).ap()
    expert_out = nc.dram_tensor("expert_out", (MAXB * TOK, D), F32).ap()

    with ExitStack() as ctx:
        def sb(name, shape, dt=F32):
            return ctx.enter_context(nc.sbuf_tensor(name, shape, dt))

        def sem(name):
            return ctx.enter_context(nc.semaphore(name))

        bank = ctx.enter_context(nc.psum_tensor("bank", [P, 8, 512], F32))

        feat_t = sb("feat_t", [P, KD, NP])
        resid = sb("resid", [P, NT, D])
        ident = sb("ident", [P, P])
        iota_row = sb("iota_row", [P, P])
        dinv = sb("dinv", [P, NT])
        zero = sb("zero", [1, 512], BF16)
        ln_stats = sb("ln_stats", [P, NT, 6])
        ln_mv = sb("ln_mv", [P, NT, 2])
        ln_rstd = sb("ln_rstd", [P, NT])
        ln_std = sb("ln_std", [P, NT])

        arena = sb("arena", [P, COLS * (2 + A) + 1024])
        src_col = arena[:, 0:COLS].bitcast(I32)
        dst_col = arena[:, COLS:2 * COLS]
        attr_col = arena[:, 2 * COLS:(2 + A) * COLS].rearrange("p (c a) -> p c a", a=A)
        iota_bf = arena[:, (2 + A) * COLS:(2 + A) * COLS + P // 2].bitcast(BF16)

        SET = KD * F + KF * D
        sets = sb("sets", [P, 3 * SET])

        def w1_set(s):
            return sets[:, s * SET:s * SET + KD * F].rearrange("p (k f) -> p k f", k=KD)

        def w2_set(s):
            return sets[:, s * SET + KD * F:(s + 1) * SET].rearrange("p (c d) -> p c d", c=KF)

        pools = [[sets[:, :], 3 * SET, 0], [feat_t[:, :, :].rearrange("p k n -> p (k n)"), KD * NP, 0]]

        def stage(n):
            pool = next(q for q in pools if q[2] + n <= q[1])
            pool[2] += n
            return pool[0][:, pool[2] - n:pool[2]]

        dst_int = stage(COLS).bitcast(I32).rearrange("p (b e) -> p b e", b=CB)
        src_int = stage(COLS).bitcast(I32).rearrange("p (b e) -> p b e", b=CB)
        dst_f = stage(COLS).rearrange("p (b e) -> p b e", b=CB)
        src_f = stage(COLS).rearrange("p (b e) -> p b e", b=CB)
        attr_in = stage(COLS * A).rearrange("p (b e a) -> p b e a", b=CB, a=A)
        c_lo = stage(CB)
        c_hi = stage(CB)
        tile_at = stage(NT)
        tile_at_end = stage(NT)
        chunk_up = stage(CB)
        chunk_down = stage(CB)
        act_lo = stage(NT * CB).rearrange("p (t b) -> p t b", t=NT)
        act_hi = stage(NT * CB).rearrange("p (t b) -> p t b", t=NT)
        bounds = stage(2 * NT)
        bounds_all = stage(2 * NT)
        first_c, last_c, first_g, last_g, wide, shares, start_g, end_g, before_last, base_2 = (
            stage(NT) for _ in range(10))
        first_i, last_i = (stage(NT).bitcast(I32) for _ in range(2))
        some = stage(NT)
        total = stage(4)
        total_i = stage(4).bitcast(I32)
        dst_ii = stage(COLS).bitcast(I32)
        lo_i = stage(COLS).bitcast(I32)
        hi_i = stage(COLS).bitcast(I32)
        lo_b = stage(COLS // 2).bitcast(BF16)
        hi_b = stage(COLS // 2).bitcast(BF16)
        deg = stage(NT)
        deg1 = stage(NT)
        deg_root = stage(NT)
        deg_inv = stage(NT)
        deg_some = stage(NT)
        CG = 8
        hot_lo = [stage(CG * P // 2).bitcast(BF16).rearrange("p (c n) -> p c n", c=CG) for _ in range(2)]
        hot_hi = [stage(CG * 64 // 2).bitcast(BF16).rearrange("p (c n) -> p c n", c=CG) for _ in range(2)]

        plan = sb("plan", [1, 2 * NT + 1], I32)
        plan_first = plan[:, 0:NT]
        plan_groups = plan[:, NT:2 * NT]
        plan_total = plan[:, 2 * NT:2 * NT + 1]
        neg_base = sb("neg_base", [P, NT])
        neg_base_2 = sb("neg_base_2", [P, NT])

        normed = sb("normed", [P, 2, D])
        row_out = sb("row_out", [P, 2, 4, D])
        row0_out = row_out[:, :, :, :].rearrange("p a b d -> p (a b d)")[:, 0:2 * (W0 + 7)].rearrange(
            "p (a d) -> p a d", a=2)[:, :, 0:W0]

        edges_in = sem("edges_in")
        padded = sem("padded")
        consts = sem("consts")
        as_float = sem("as_float")
        turned = sem("turned")
        placed = sem("placed")
        prep_v = sem("prep_v")
        reduce_in = sem("reduce_in")
        reduce_out = sem("reduce_out")
        hot_ready = sem("hot_ready")
        counted = sem("counted")
        root_in = sem("root_in")
        root_out = sem("root_out")
        x_in = sem("x_in")
        pre_p = sem("pre_p")

        def edge_parts(flat, tile, w):
            full = FULLC // P
            a = full * P * P
            b = FULLC * P
            r = FULLC - full * P
            if w == 1:
                yield flat[0:a].rearrange("(k p e) -> p k e", p=P, e=P), tile[:, 0:full, :]
                yield flat[a:b].rearrange("(p e) -> p e", e=P), tile[0:r, full, :]
                yield flat[b:E].rearrange("(p e) -> p e", p=1), tile[r:r + 1, full, 0:REST]
            else:
                yield (flat[0:a, :].rearrange("(k p e) a -> p k (e a)", p=P, e=P),
                       tile[:, 0:full, :, :].rearrange("p k e a -> p k (e a)"))
                yield (flat[a:b, :].rearrange("(p e) a -> p (e a)", e=P),
                       tile[0:r, full, :, :].rearrange("p e a -> p (e a)"))
                yield (flat[b:E, :].rearrange("(p e) a -> p (e a)", p=1),
                       tile[r:r + 1, full, 0:REST, :].rearrange("p e a -> p (e a)"))

        def turns():
            for b in range(CB):
                yield "dst", b, 0
            for b in range(CB):
                yield "src", b, 0
            for a in range(A):
                for b in range(CB):
                    yield "attr", b, a

        TURNS = list(turns())

        def loop(engine, n, body):
            body(0)
            with engine.Fori(1, n) as i:
                body(i)

        def wait_past(engine, what, value):
            if not isinstance(value, int) or value > 0:
                engine.wait_ge(what, value)

        def tile_stats(dve, done):
            assert NT % 7 == 0
            with dve.Fori(0, NT // 7) as i:
                for u in range(7):
                    dve.bn_stats(ln_stats[:, ds(i * 7 + u, 1), :].rearrange("p a s -> p (a s)"),
                                 resid[:, ds(i * 7 + u, 1), :].rearrange("p a d -> p (a d)")).then_inc(done, 1)

        def tile(ap, t):
            return ap[:, ds(t, 1), :].rearrange("p a s -> p (a s)")

        def nodes(t, n=1):
            return ds(t * P, n * P)

        with nc.Block() as block:
            @block.sync
            def _(sp):
                sp.wait_ge(padded, 3)
                for d, s in [*edge_parts(dst, dst_int, 1), *edge_parts(src, src_int, 1),
                             *edge_parts(attr, attr_in, A)]:
                    sp.dma_start(s, d).then_inc(edges_in, 16)
                sp.wait_ge(edges_in, 16 * 9)
                sp.wait_ge(x_in, 32)

            @block.gpsimd
            def _(pool):
                pool.memset(ident[:], 0.0).then_inc(pre_p, 1)
                pool.wait_ge(pre_p, 1)
                pool.affine_select(out=ident[:], in_=ident[:], compare_op=ALU.not_equal, fill=1.0, base=0,
                                   pattern=[[-1, P]], channel_multiplier=1).then_inc(consts, 1)
                imp = dict(allow_small_or_imprecise_dtypes=True)
                pool.iota(iota_row[:], [[1, P]], 0, 0, **imp).then_inc(consts, 1)
                pool.iota(iota_bf, [[1, P]], 0, 0, **imp).then_inc(consts, 1)
                pool.iota(tile_at, [[P, NT]], 0, 0, **imp).then_inc(consts, 1)
                pool.iota(tile_at_end, [[P, NT]], P, 0, **imp).then_inc(consts, 1)
                pool.iota(neg_base[:], [[-P, NT]], 0, 0, **imp).then_inc(consts, 1)
                pool.iota(base_2, [[-P, NT]], -P - FAR, 0, **imp).then_inc(consts, 1)
                pool.iota(chunk_up, [[P, CB]], 1, 1, **imp).then_inc(consts, 1)
                pool.iota(chunk_down, [[-P, CB]], COLS, -1, **imp).then_inc(consts, 1)
                pool.memset(resid[:, NT - 1, :], 0.0).then_inc(pre_p, 1)
                pool.wait_ge(pre_p, 2)
                full = (NT - 1) * P
                pool.dma_start(resid[:, 0:NT - 1, :],
                               x[0:full, :].rearrange("(t p) d -> p t d", p=P)).then_inc(x_in, 16)
                pool.dma_start(resid[0:LAST, NT - 1, :], x[full:N, :]).then_inc(x_in, 16)
                pool.wait_ge(reduce_in, 1)
                pool.partition_all_reduce(bounds_all, bounds, P, bass.bass_isa.ReduceOp.max)\
                    .then_inc(reduce_out, 1)

            @block.vector
            def _(dve):
                n = [0]

                def link(ins):
                    n[0] += 1
                    ins.then_inc(prep_v, 1)
                    dve.wait_ge(prep_v, n[0])

                dve.memset(dst_int, FAR).then_inc(padded, 1)
                dve.memset(src_int, 0).then_inc(padded, 1)
                dve.memset(attr_in, 0.0).then_inc(padded, 1)
                dve.memset(zero[:], 0.0).then_inc(padded, 1)
                dve.wait_ge(edges_in, 16 * 9)
                dve.tensor_copy(dst_f, dst_int).then_inc(as_float, 1)
                dve.tensor_copy(src_f, src_int).then_inc(as_float, 1)
                dve.wait_ge(as_float, 2)
                dve.tensor_reduce(c_lo, dst_f, AX_X, ALU.min)
                link(dve.tensor_reduce(c_hi, dst_f, AX_X, ALU.max))
                dve.wait_ge(consts, 9)
                dve.tensor_tensor(act_lo, c_lo.unsqueeze(1).to_broadcast([P, NT, CB]),
                                  tile_at_end.unsqueeze(2).to_broadcast([P, NT, CB]), ALU.is_lt)
                link(dve.tensor_tensor(act_hi, c_hi.unsqueeze(1).to_broadcast([P, NT, CB]),
                                       tile_at.unsqueeze(2).to_broadcast([P, NT, CB]), ALU.is_ge))
                link(dve.tensor_tensor(act_lo, act_lo, act_hi, ALU.mult))
                link(dve.tensor_tensor(act_hi, act_lo, chunk_up.unsqueeze(1).to_broadcast([P, NT, CB]), ALU.mult))
                link(dve.tensor_tensor(act_lo, act_lo, chunk_down.unsqueeze(1).to_broadcast([P, NT, CB]),
                                       ALU.mult))
                link(dve.tensor_reduce(bounds[:, 0:NT], act_lo, AX_X, ALU.max))
                dve.tensor_reduce(bounds[:, NT:2 * NT], act_hi, AX_X, ALU.max).then_inc(reduce_in, 1)

                def place(i):
                    what, b, a = TURNS[i]
                    dve.wait_ge(turned, i + 1)
                    got = bank[:, i % 4, 0:P]
                    col = slice(b * P, (b + 1) * P)
                    to = {"dst": dst_col[:, col], "src": src_col[:, col], "attr": attr_col[:, col, a]}[what]
                    dve.tensor_copy(to, got).then_inc(placed, 1)

                for i in range(2 * CB):
                    place(i)
                dve.wait_ge(placed, 2 * CB)
                link(dve.tensor_copy(dst_ii, dst_col))
                dve.tensor_scalar(lo_i, dst_ii, P - 1, None, ALU.bitwise_and)
                link(dve.tensor_scalar(hi_i, dst_ii, 7, None, ALU.arith_shift_right))
                dve.tensor_copy(lo_b, lo_i)
                link(dve.tensor_copy(hi_b, hi_i))
                with dve.Fori(0, COLS // (2 * CG)) as i:
                    for h in range(2):
                        dve.wait_ge(counted, 2 * i + h + 1)
                        c = i * (2 * CG) + h * CG
                        dve.tensor_tensor(hot_lo[h], iota_bf.unsqueeze(1).to_broadcast([P, CG, P]),
                                          lo_b[:, ds(c, CG)].unsqueeze(2).to_broadcast([P, CG, P]), ALU.is_equal)
                        dve.tensor_tensor(hot_hi[h][:, :, 0:NT],
                                          iota_bf[:, 0:NT].unsqueeze(1).to_broadcast([P, CG, NT]),
                                          hi_b[:, ds(c, CG)].unsqueeze(2).to_broadcast([P, CG, NT]),
                                          ALU.is_equal).then_inc(hot_ready, 1)
                for i in range(2 * CB, len(TURNS)):
                    place(i)
                dve.wait_ge(reduce_out, 1)
                dve.tensor_scalar(first_c, bounds_all[:, 0:NT], -1.0, float(COLS), ALU.mult, ALU.add)
                dve.tensor_scalar(last_c, bounds_all[:, NT:2 * NT], -1.0, 0.0, ALU.add, ALU.max)
                link(dve.tensor_scalar(some, bounds_all[:, 0:NT], 0.0, None, ALU.is_gt))
                dve.tensor_copy(last_i, last_c)
                link(dve.tensor_tensor(first_i, first_c, some, ALU.mult))
                shift = K.bit_length() - 1
                dve.tensor_scalar(last_i, last_i, shift, None, ALU.arith_shift_right)
                link(dve.tensor_scalar(first_i, first_i, shift, None, ALU.arith_shift_right))
                dve.tensor_copy(last_g, last_i)
                link(dve.tensor_copy(first_g, first_i))
                link(dve.tensor_tensor(wide, last_g, first_g, ALU.subtract))
                link(dve.tensor_scalar(wide, wide, float(MINS + 1), None, ALU.is_ge))
                dve.memset(shares, 0.0)
                link(dve.tensor_tensor(start_g[:, 0:NT - 1], first_g[:, 1:NT], last_g[:, 0:NT - 1], ALU.is_equal))
                link(dve.tensor_tensor(shares[:, 0:NT - 1], start_g[:, 0:NT - 1], wide[:, 0:NT - 1], ALU.mult))
                dve.tensor_tensor(start_g[:, 1:NT], first_g[:, 1:NT], shares[:, 0:NT - 1], ALU.add)
                link(dve.tensor_copy(start_g[:, 0:1], first_g[:, 0:1]))
                dve.tensor_tensor(base_2, base_2, shares, ALU.mult)
                link(dve.tensor_scalar(before_last, start_g, float(MINS), None, ALU.add))
                dve.tensor_scalar(neg_base_2[:], base_2, float(FAR), None, ALU.add)
                link(dve.tensor_tensor(end_g, before_last, last_g, ALU.max))
                link(dve.tensor_tensor(before_last, end_g, start_g, ALU.subtract))
                link(dve.tensor_reduce(total[:, 0:1], before_last, AX_X, ALU.add))
                link(dve.tensor_scalar(total[:, 1:2], total[:, 0:1], -1.0, float(-NT), ALU.mult, ALU.add))
                link(dve.tensor_copy(total_i[:, 0:1], total[:, 1:2]))
                link(dve.tensor_scalar(total_i[:, 1:2], total_i[:, 0:1], GG - 1, None, ALU.bitwise_and))
                link(dve.tensor_copy(total[:, 2:3], total_i[:, 1:2]))
                link(dve.tensor_tensor(before_last[:, NT - 1:NT], before_last[:, NT - 1:NT], total[:, 2:3], ALU.add))
                dve.tensor_copy(plan_groups, before_last[0:1, :])
                link(dve.tensor_tensor(total[:, 3:4], total[:, 2:3], total[:, 1:2], ALU.subtract))
                dve.tensor_scalar(plan_total, total[0:1, 3:4], 1.0 / GG, None, ALU.mult)
                dve.tensor_scalar(plan_first, start_g[0:1, :], float(K), None, ALU.mult)
                dve.wait_ge(counted, COLS // CG + 3)
                link(dve.tensor_copy(deg, bank[:, 4, 0:NT]))
                dve.tensor_scalar(deg_some, deg, 0.0, None, ALU.is_gt)
                dve.tensor_scalar(deg1, deg, 1.0, None, ALU.max).then_inc(root_in, 1)
                dve.wait_ge(x_in, 32)
                tile_stats(dve, prep_v)
                n[0] += NT
                dve.wait_ge(prep_v, n[0])
                for t in range(NT):
                    last = dve.bn_aggr(ln_mv[:, t, :], ln_stats[:, t, :])
                link(last)
                dve.tensor_scalar(ln_std[:], ln_mv[:, :, 1], EPS, None, ALU.add).then_inc(root_in, 1)
                dve.wait_ge(root_out, 2)
                link(dve.reciprocal(deg_inv, deg_root))
                dve.tensor_tensor(dinv[:], deg_inv, deg_some, ALU.mult)
                dve.reciprocal(ln_rstd[:], ln_std[:])

            @block.scalar
            def _(act):
                act.wait_ge(root_in, 1)
                act.activation(deg_root, deg1, ACT.Sqrt).then_inc(root_out, 1)
                act.wait_ge(root_in, 2)
                act.activation(ln_std[:], ln_std[:], ACT.Sqrt).then_inc(root_out, 1)

            @block.tensor
            def _(pe):
                pe.wait_ge(as_float, 2)
                pe.wait_ge(consts, 1)

                def turn(i):
                    what, b, a = TURNS[i]
                    if i >= 4:
                        pe.wait_ge(placed, i - 3)
                    of = {"dst": dst_f[:, b, :], "src": src_f[:, b, :], "attr": attr_in[:, b, :, a]}[what]
                    pe.transpose(bank[:, i % 4, 0:P], of, ident[:]).then_inc(turned, 1)

                for i in range(2 * CB):
                    turn(i)
                pe.sem_inc(counted, 2)
                pe.wait_ge(padded, 4)
                pe.matmul(bank[:, 4, 0:NT], zero[:, 0:P], zero[:, 0:NT], start=True, stop=False)
                with pe.Fori(0, COLS // (2 * CG)) as i:
                    for h in range(2):
                        pe.wait_ge(hot_ready, 2 * i + h + 1)
                        for c in range(CG):
                            mm = pe.matmul(bank[:, 4, 0:NT], hot_lo[h][:, c, :], hot_hi[h][:, c, 0:NT],
                                           start=False, stop=False)
                        mm.then_inc(counted, 1)
                pe.matmul(bank[:, 4, 0:NT], zero[:, 0:P], zero[:, 0:NT], start=False, stop=True)\
                    .then_inc(counted, 1)
                for i in range(2 * CB, len(TURNS)):
                    turn(i)


        mix_w = sb("mix_w", [P, 2 * KD, D])
        edge_w = sb("edge_w", [P, KD, A])
        layer_b = sb("layer_b", [P, L, KD])
        layer_g = sb("layer_g", [P, L, KD])
        layer_s = sb("layer_s", [P, L, KD])
        chunk_end = sem("chunk_end")
        gate = sem("gate")

        def gated(engine):
            engine.sem_inc(gate, 1)

        class Norm:

            def __init__(self, name):
                self.ready = sem(name + "_ready")
                self.turned = sem(name + "_turned")
                self.placed = sem(name + "_placed")

            @staticmethod
            def tiles(engine, body):
                with engine.Fori(0, NT // 4) as i:
                    for u in range(4):
                        body(i * 4 + u, u % 2)
                body(NT - 1, 0)

            def vector(self, dve, slot_free=None):
                def normalise(t, s):
                    dve.wait_ge(self.turned, t + 1)
                    if slot_free:
                        dve.wait_ge(slot_free, t + 1)
                    dve.tensor_scalar(normed[:, s, :], tile(resid, t), ln_mv[:, ds(t, 1), 0], ln_rstd[:, ds(t, 1)],
                                      ALU.subtract, ALU.mult).then_inc(self.ready, 1)

                def place(t, s):
                    dve.wait_ge(self.turned, t + 3)
                    dve.tensor_copy(feat_t[:, :, nodes(t)],
                                    bank[:, s, 0:D].rearrange("p (k n) -> p k n", k=KD)).then_inc(self.placed, 1)

                dve.sem_inc(self.placed, 2)
                normalise(0, 0)
                with dve.Fori(0, NT // 4) as i:
                    for u in range(4):
                        normalise(i * 4 + u + 1, (u + 1) % 2)
                        place(i * 4 + u, u % 2)
                place(NT - 1, 0)

            def tensor(self, pe):
                def turn(t, s):
                    pe.wait_ge(self.ready, t + 1)
                    pe.wait_ge(self.placed, t + 1)
                    for k in range(KD):
                        mm = pe.transpose(bank[:, s, k * P:(k + 1) * P], normed[:, s, k * P:(k + 1) * P], ident[:])
                    mm.then_inc(self.turned, 1)

                pe.sem_inc(self.turned, 2)
                self.tiles(pe, turn)

        first_norm = Norm("norm")
        row0_ready = sem("row0_ready")
        row0_stored = [sem(f"row0_stored{i}") for i in range(2)]
        params_in = sem("params_in")
        edge_w_zero = sem("edge_w_zero")

        with nc.Block() as block:
            @block.sync
            def _(sp):
                with nc.allow_non_contiguous_dma(reason="a few hundred parameters"):
                    sp.dma_start(layer_b[:], mlp_b.rearrange("l (k p) -> p l k", p=P)).then_inc(params_in, 16)
                    sp.dma_start(layer_g[:], bn_g.rearrange("l (k p) -> p l k", p=P)).then_inc(params_in, 16)
                    sp.dma_start(layer_s[:], bn_b.rearrange("l (k p) -> p l k", p=P)).then_inc(params_in, 16)

                def store(t, s):
                    sp.wait_ge(row0_ready, t + 3)
                    gated(sp)
                    sp.dma_start(rows0[nodes(t), :], row0_out[:, s, :]).then_inc(row0_stored[s], 16)

                Norm.tiles(sp, store)
                sp.wait_ge(params_in, 48)
                sp.wait_ge(row0_stored[0], 16 * (NT // 2 + 1))
                sp.wait_ge(row0_stored[1], 16 * (NT // 2))

            @block.vector
            def _(dve):
                dve.memset(edge_w[:], 0.0).then_inc(edge_w_zero, 1)
                first_norm.vector(dve, row0_ready)

            @block.scalar
            def _(act):
                def scale(t, s, seen):
                    act.wait_ge(first_norm.ready, t + 1)
                    wait_past(act, row0_stored[s], seen)
                    act.activation(row0_out[:, s, 0:D], normed[:, s, :], ACT.Copy, scale=dinv[:, ds(t, 1)])
                    act.activation(row0_out[:, s, D:W0], dinv[:, ds(t, 1)], ACT.Copy).then_inc(row0_ready, 1)

                act.sem_inc(row0_ready, 2)

                def four(i):
                    for u in range(4):
                        scale(i * 4 + u, u % 2, (i * 2 + u // 2) * 16)

                loop(act, NT // 4, four)
                scale(NT - 1, 0, NT // 2 * 16)

            @block.tensor
            def _(pe):
                first_norm.tensor(pe)


        room = [0]

        def graph(n):
            room[0] += n
            assert room[0] <= 3 * SET
            return sets[:, room[0] - n:room[0]]

        got = graph(K * 264).rearrange("p (j d) -> p j d", j=K)
        hot = graph(K * P).rearrange("p (j n) -> p j n", j=K)
        hot_2 = graph(K * P).rearrange("p (j n) -> p j n", j=K)
        index = sb("index", [P, K], I32)
        summed = sb("summed", [P, D + 1 + A])
        edge_sum = sb("edge_sum", [P, NT, A])
        summed_t = sb("summed_t", [P, KD, P])
        edge_sum_t = sb("edge_sum_t", [A, P])
        edge_mix = sb("edge_mix", [A, D])
        bn_rec = graph(KD * NT * 6).rearrange("p (k t s) -> p k t s", k=KD, s=6)
        bn_mv = sb("bn_mv", [P, KD, 2])
        bn_var = sb("bn_var", [P, KD])
        bn_std = sb("bn_std", [P, KD])
        bn_inv = sb("bn_inv", [P, KD])
        bn_scale = sb("bn_scale", [P, KD])
        bn_prod = sb("bn_prod", [P, KD])
        bn_shift = sb("bn_shift", [P, KD])
        new_rows = graph(4 * 4 * D).rearrange("p (s t d) -> p s t d", s=4, t=4)
        BT = 4
        NB = NT // BT + 1
        NPAIR = NT // 2 + 1

        WA = W0 + A

        layer_in = sem("layer_in")
        mix_ready = sem("mix_ready")
        mix_made = sem("mix_made")
        index_ready = sem("index_ready")
        gathered = [sem(f"gathered{j}") for j in range(K)]
        hot_in = sem("hot_in")
        chunk_done = sem("chunk_done")
        sum_done = sem("sum_done")
        sum_taken = sem("sum_taken")
        sum_turned = sem("sum_turned")
        sum_placed = sem("sum_placed")
        mixed = sem("mixed")
        mixed_taken = sem("mixed_taken")
        attr_kept = sem("attr_kept")
        stats_v = sem("stats_v")
        var_ready = sem("var_ready")
        std_ready = sem("std_ready")
        coeffs = sem("coeffs")
        coeffs2 = sem("coeffs2")
        applied = sem("applied")
        row_turned = sem("row_turned")
        row_taken = sem("row_taken")
        rows_stored = [sem(f"rows_stored{i}") for i in range(4)]

        def in_layers(engine, body):
            body(0, True, False)
            with engine.Fori(1, L - 1) as l:
                body(l, False, False)
            body(L - 1, False, True)

        def in_blocks(engine, body):
            def four(v):
                for s in range(4):
                    body(v * 4 + s, s, BT, v)

            loop(engine, NB // 4, four)
            body(NB - 1, 0, 1, NB // 4)

        def counter(engine, name):
            r = engine.alloc_register(name)
            engine.reg_mov(r, 0)
            return r

        MAX_ALL = L * NT * MAXG

        with nc.Block() as block:
            @block.sync
            def _(sp):
                def load(l):
                    with nc.allow_non_contiguous_dma(reason="the edge weights by features: 4 columns"):
                        sp.dma_start(mix_w[:], mlp_w[ds(l, 1), :, :].rearrange("a (k p) n -> p (a k) n", p=P))\
                            .then_inc(layer_in, 16)
                        sp.dma_start(edge_w[:, 0, A - 1:A], ew1[ds(l, 1), :, :].rearrange("a b p -> p (a b)"))\
                            .then_inc(layer_in, 16)
                        sp.dma_start(edge_w[:, 1, 0:A - 1], ew2[ds(l, 1), :, :].rearrange("a j p -> p (a j)"))\
                            .then_inc(layer_in, 16)
                def layer(l, first, final):
                    if final:
                        return
                    sp.wait_ge(mixed, (l + 1) * NT + 1)
                    gated(sp)
                    load(l + 1)

                    def store(i, s, nt, v):
                        sp.wait_ge(row_taken, l * NPAIR + i * (BT // 2) + (nt + 1) // 2 + 4)
                        gated(sp)
                        sp.dma_start(rows[nodes(i * BT, nt), :].rearrange("(t p) d -> p t d", p=P),
                                     new_rows[:, s, 0:nt, :]).then_inc(rows_stored[s], 16)

                    in_blocks(sp, store)

                load(0)
                in_layers(sp, layer)

            @block.gpsimd
            def _(pool):
                g = counter(pool, "pool_group")
                steps = pool.value_load(plan_total, min_val=1, max_val=NT * MAXG)

                def layer(l, first, final):
                    if not first:
                        for s in range(4):
                            pool.wait_ge(rows_stored[s], l * (16 * (NB // 4 + (s == 0))))
                        gated(pool)
                    width = W0 if first else D
                    with pool.Fori(0, steps):
                        for u in range(GG):
                            now = pool.snap(g, min_val=0, max_val=MAX_ALL)
                            for j in range(K):
                                pool.wait_ge(index_ready, now * K + j + 1)
                                gated(pool)
                                pool.indirect_dma_start(
                                    got[:, j, 0:width], None, rows0 if first else rows,
                                    bass.IndirectOffsetOnAxis(ap=index[:, j:j + 1], axis=0)).then_inc(gathered[j], 16)
                            pool.reg_add(g, g, 1)

                in_layers(pool, layer)

            @block.scalar
            def _(act):
                g = counter(act, "act_group")
                col = counter(act, "act_column")

                def indices():
                    now = act.snap(g, min_val=0, max_val=MAX_ALL)
                    c = act.snap(col, min_val=0, max_val=COLS - K)
                    for j in range(K):
                        act.wait_ge(chunk_done, now * K + j + 1)
                        act.activation(index[:, j:j + 1], src_col[:, ds(c + j, 1)], ACT.Copy).then_inc(index_ready, 1)
                    act.reg_add(g, g, 1)
                    act.reg_add(col, col, K)

                def layer(l, first, final):
                    width = W0 + A if first else D

                    def take(t):
                        q = l * NT + t
                        act.wait_ge(sum_done, q + 1)
                        act.wait_ge(sum_turned, q + 1)
                        act.activation(summed[:, 0:width], tile(bank, t % 2)[:, 0:width], ACT.Copy,
                                       scale=dinv[:, ds(t, 1)]).then_inc(sum_taken, 1)
                        if first:
                            act.wait_ge(sum_taken, q + 3)
                            act.activation(tile(edge_sum, t), summed[:, W0:WA], ACT.Copy).then_inc(attr_kept, 1)
                        else:
                            act.activation(summed[:, W0:WA], tile(edge_sum, t), ACT.Copy).then_inc(attr_kept, 1)

                    def relu(t):
                        act.wait_ge(mixed, l * NT + t + 2)
                        gated(act)
                        for k in range(KD):
                            last = act.activation(feat_t[:, k, nodes(t)], bank[:, 3, k * P:(k + 1) * P], ACT.Relu,
                                                  bias=layer_b[:, ds(l, 1), k])
                        last.then_inc(mixed_taken, 1)

                    def start(t):
                        c = act.value_load(plan_first[:, ds(t, 1)], min_val=0, max_val=COLS)
                        act.reg_mov(col, c)
                        return act.value_load(plan_groups[:, ds(t, 1)], min_val=MINS, max_val=MAXG)

                    def tile_steps(t, past):
                        n = start(t)
                        with act.Fori(0, n):
                            indices()
                        if past >= 2:
                            relu(t - 2)
                        if past >= 1:
                            take(t - 1)
                        indices()

                    tile_steps(0, 0)
                    act.wait_ge(mix_ready, l + 1)
                    act.activation(edge_mix[:], bank[0:A, 4, 0:D], ACT.Copy).then_inc(mix_made, 1)
                    tile_steps(1, 1)
                    with act.Fori(2, NT) as t:
                        tile_steps(t, 2)
                    relu(NT - 2)
                    take(NT - 1)
                    relu(NT - 1)
                    act.wait_ge(var_ready, l + 1)
                    act.activation(bn_std[:], bn_var[:], ACT.Sqrt).then_inc(std_ready, 1)
                    act.wait_ge(coeffs, l + 1)

                    def apply(i, s, nt, v):
                        for k in range(KD):
                            span = feat_t[:, k, nodes(i * BT, nt)]
                            last = act.activation(span, span, ACT.Identity if final else ACT.Relu,
                                                  bias=bn_shift[:, k:k + 1], scale=bn_scale[:, k:k + 1])
                        last.then_inc(applied, 1)

                    in_blocks(act, apply)

                act.sem_inc(sum_taken, 2)
                act.sem_inc(mixed_taken, 1)
                in_layers(act, layer)

            @block.vector
            def _(dve):
                g = counter(dve, "dve_group")
                col = counter(dve, "dve_column")
                CHAIN = 4

                def layer(l, first, final):
                    def hots(t, shared):
                        now = dve.snap(g, min_val=0, max_val=MAX_ALL)
                        c = dve.snap(col, min_val=0, max_val=COLS - K)
                        for j in range(K):
                            dve.wait_ge(chunk_done, now * K + j + 1)
                            ins = dve.tensor_scalar(hot[:, j, :], iota_row[:], dst_col[:, ds(c + j, 1)],
                                                    neg_base[:, ds(t, 1)], ALU.subtract, ALU.is_equal)
                            if shared:
                                ins = dve.tensor_scalar(hot_2[:, j, :], iota_row[:], dst_col[:, ds(c + j, 1)],
                                                        neg_base_2[:, ds(t, 1)], ALU.subtract, ALU.is_equal)
                            if first:
                                dve.wait_ge(gathered[j], now * 16 + 16)
                                ins = dve.tensor_scalar(got[:, j, W0:WA], tile(attr_col, c + j),
                                                        got[:, j, D:W0], None, ALU.mult)
                            ins.then_inc(hot_in, 1)
                        dve.reg_add(g, g, 1)
                        dve.reg_add(col, col, K)

                    def place(t):
                        q = l * NT + t
                        dve.wait_ge(sum_turned, q + 2)
                        dve.wait_ge(mixed, q + 1)
                        dve.tensor_copy(summed_t[:], bank[:, 2, 0:D].rearrange("p (k n) -> p k n", k=KD))
                        dve.tensor_copy(edge_sum_t[:], bank[0:A, 2, D:D + P]).then_inc(sum_placed, 1)

                    def stats(t, n):
                        dve.wait_ge(mixed_taken, l * NT + t + 2)
                        for k in range(KD):
                            last = dve.bn_stats(bn_rec[:, k, ds(t, 1), :].rearrange("p a s -> p (a s)"),
                                                feat_t[:, k, ds(t * P, n)])
                        return last

                    def start(t):
                        c = dve.value_load(plan_first[:, ds(t, 1)], min_val=0, max_val=COLS)
                        dve.reg_mov(col, c)
                        return dve.value_load(plan_groups[:, ds(t, 1)], min_val=MINS, max_val=MAXG)

                    def tile_steps(t, past):
                        n = start(t)
                        with dve.Fori(0, n):
                            hots(t, False)
                        hots(t, True)
                        if past >= 1:
                            place(t - 1)
                        if past >= 2:
                            stats(t - 2, P)

                    tile_steps(0, 0)
                    tile_steps(1, 1)
                    with dve.Fori(2, NT) as t:
                        tile_steps(t, 2)
                    place(NT - 1)
                    stats(NT - 2, P)
                    links = [0]

                    def link(ins):
                        links[0] += 1
                        ins.then_inc(stats_v, 1)
                        dve.wait_ge(stats_v, l * CHAIN + links[0])

                    link(stats(NT - 1, LAST))
                    gated(dve)
                    for k in range(KD):
                        last = dve.bn_aggr(bn_mv[:, k, :], bn_rec[:, k, :, :].rearrange("p t s -> p (t s)"))
                    link(last)
                    dve.tensor_scalar(bn_var[:], bn_mv[:, :, 1], EPS, None, ALU.add).then_inc(var_ready, 1)
                    dve.wait_ge(std_ready, l + 1)
                    link(dve.reciprocal(bn_inv[:], bn_std[:]))
                    link(dve.tensor_tensor(bn_scale[:], bn_inv[:], tile(layer_g, l), ALU.mult))
                    assert links[0] == CHAIN
                    dve.tensor_tensor(bn_prod[:], bn_mv[:, :, 0], bn_scale[:], ALU.mult).then_inc(coeffs2, 1)
                    dve.wait_ge(coeffs2, l + 1)
                    dve.tensor_tensor(bn_shift[:], tile(layer_s, l), bn_prod[:], ALU.subtract).then_inc(coeffs, 1)

                    def take(i, s, nt, v):
                        if not final:
                            wait_past(dve, rows_stored[s], l * (16 * (NB // 4 + (s == 0))) + v * 16)
                        for u in range(0, nt, 2):
                            t = i * BT + u
                            w = min(2, nt - u)
                            dve.wait_ge(row_turned, l * NPAIR + i * (BT // 2) + u // 2 + 1)
                            turned_rows = bank[:, 4 + (2 * s + u // 2) % 4, 0:w * D].rearrange("p (t d) -> p t d", t=w)
                            if final:
                                here = resid[:, ds(t, w), :]
                                dve.tensor_tensor(here, turned_rows, here, ALU.add).then_inc(row_taken, 1)
                            else:
                                dve.tensor_tensor(new_rows[:, s, u:u + w, :], turned_rows,
                                                  dinv[:, ds(t, w)].unsqueeze(2).to_broadcast([P, w, D]), ALU.mult)\
                                    .then_inc(row_taken, 1)

                    in_blocks(dve, take)

                dve.sem_inc(row_taken, 4)
                dve.sem_inc(sum_placed, 1)
                in_layers(dve, layer)

            @block.tensor
            def _(pe):
                g = counter(pe, "pe_group")

                def layer(l, first, final):
                    width = W0 + A if first else D

                    def into(t):
                        return tile(bank, t % 2)[:, 0:width]

                    def sums(t, last=False, more=()):
                        now = pe.snap(g, min_val=0, max_val=MAX_ALL)
                        if last:
                            pe.wait_ge(sum_taken, l * NT + t + 2)
                        for j in range(K):
                            pe.wait_ge(gathered[j], now * 16 + 16)
                            pe.wait_ge(hot_in, now * K + j + 1)
                            mm = pe.matmul(into(t), hot[:, j, :], got[:, j, 0:width], start=False,
                                           stop=last and j == K - 1)
                            if last and j == K - 1:
                                mm.then_inc(sum_done, 1)
                            if last:
                                mm = pe.matmul(into(t + 1), hot_2[:, j, :], got[:, j, 0:width], start=j == 0,
                                               stop=False)
                            mm.then_inc(chunk_done, 1)
                            if j in more:
                                more[j]()
                        pe.reg_add(g, g, 1)

                    def turn(t):
                        q = l * NT + t
                        pe.wait_ge(attr_kept, q + 1)
                        pe.wait_ge(sum_taken, q + 3)
                        pe.wait_ge(sum_placed, q + 1)
                        for k in range(KD):
                            pe.transpose(bank[:, 2, k * P:(k + 1) * P], summed[:, k * P:(k + 1) * P], ident[:])
                        pe.transpose(bank[0:A, 2, D:D + P], summed[:, W0:WA], ident[:]).then_inc(sum_turned, 1)

                    def mix(t, f):
                        q = l * NT + t
                        if f == 0:
                            pe.wait_ge(sum_placed, q + 2)
                            pe.wait_ge(mixed_taken, q + 1)
                        o = bank[:, 3, f * P:(f + 1) * P]
                        c = slice(f * P, (f + 1) * P)
                        for k in range(KD):
                            pe.matmul(o, mix_w[:, k, c], feat_t[:, k, nodes(t)], start=k == 0, stop=False)
                        for k in range(KD):
                            pe.matmul(o, mix_w[:, KD + k, c], summed_t[:, k, :], start=False, stop=False)
                        mm = pe.matmul(o, edge_mix[:, c], edge_sum_t[:], start=False, stop=True)
                        if f == KD - 1:
                            mm.then_inc(mixed, 1)

                    pe.wait_ge(layer_in, (l + 1) * 48)
                    if not first:
                        pe.wait_ge(applied, l * NB)
                    pe.wait_ge(row_taken, l * NPAIR + 4)
                    for k in range(KD):
                        mm = pe.matmul(bank[0:A, 4, 0:D], edge_w[:, k, :], mix_w[:, KD + k, :],
                                       start=k == 0, stop=k == KD - 1)
                    mm.then_inc(mix_ready, 1)

                    def tile_steps(t, past):
                        n = pe.value_load(plan_groups[:, ds(t, 1)], min_val=MINS, max_val=MAXG)
                        with pe.Fori(0, n):
                            sums(t)
                        sums(t, True, {0: lambda: turn(t - 1), 2: lambda: mix(t - 1, 0), 4: lambda: mix(t - 1, 1)}
                             if past else ())

                    pe.matmul(into(0), zero[:, 0:P], zero[:, 0:width], start=True, stop=False)
                    tile_steps(0, 0)
                    pe.wait_ge(mix_made, l + 1)
                    gated(pe)
                    with pe.Fori(1, NT) as t:
                        tile_steps(t, 1)
                    pe.matmul(into(NT), zero[:, 0:P], zero[:, 0:width], start=False, stop=True).then_inc(chunk_end, 1)
                    turn(NT - 1)
                    mix(NT - 1, 0)
                    mix(NT - 1, 1)

                    for i in range(NB):
                        pe.wait_ge(applied, l * NB + i + 1)
                        for t in range(i * BT, min(i * BT + BT, NT), 2):
                            pe.wait_ge(row_taken, l * NPAIR + t // 2 + 1)
                            for u in range(min(2, NT - t)):
                                for k in range(KD):
                                    mm = pe.transpose(bank[:, 4 + t // 2 % 4, ds(u * D + k * P, P)],
                                                      feat_t[:, k, (t + u) * P:(t + u + 1) * P], ident[:])
                            mm.then_inc(row_turned, 1)

                pe.sem_inc(chunk_done, K)
                pe.sem_inc(sum_turned, 1)
                pe.sem_inc(mixed, 1)
                in_layers(pe, layer)


        route_w = sb("route_w", [P, KD, X])
        bias1 = sb("bias1", [P, (X + 1) * KF])
        slot_of = sb("slot_of", [P, NT, 2], I32)
        weight_of = sb("weight_of", [P, NT, 2])
        plan_x = sb("plan_x", [1, 2 * X + 1], I32)

        second_norm = Norm("norm2")
        stats2_v = sem("stats2_v")
        var2_ready = sem("var2_ready")
        std2_ready = sem("std2_ready")
        logits_done = sem("logits_done")
        route_w_in = sem("route_w_in")
        bias1_in = sem("bias1_in")
        bias1_turned = sem("bias1_turned")
        sets_in = sem("sets_in")

        free = [0]

        def room(n):
            free[0] += n
            assert free[0] <= arena.shape[1]
            return arena[:, free[0] - n:free[0]]

        bias1_rows = room(P)

        def load_set(engine, s, w1, w2, done):
            engine.dma_start(w1_set(s), w1).then_inc(done, 16)
            engine.dma_start(w2_set(s), w2).then_inc(done, 16)

        with nc.Block() as block:
            @block.sync
            def _(sp):
                sp.dma_start(route_w[:], wr.rearrange("(k p) e -> p k e", p=P)).then_inc(route_w_in, 16)
                sp.dma_start(bias1_rows[0:X * KF, :], b1p.rearrange("x (c p) -> (x c) p", p=P)).then_inc(bias1_in, 16)
                sp.dma_start(bias1_rows[X * KF:(X + 1) * KF, :], b1s.rearrange("(c p) -> c p", p=P))\
                    .then_inc(bias1_in, 16)
                load_set(sp, 2, w1s.rearrange("(k p) f -> p k f", p=P), w2s.rearrange("(c p) d -> p c d", p=P), sets_in)
                for e in range(2):
                    load_set(sp, e, w1p[e].rearrange("(k p) f -> p k f", p=P),
                             w2p[e].rearrange("(c p) d -> p c d", p=P), sets_in)
                sp.wait_ge(sets_in, 96)

            @block.vector
            def _(dve):
                tile_stats(dve, stats2_v)
                dve.wait_ge(stats2_v, NT)
                for t in range(NT):
                    last = dve.bn_aggr(ln_mv[:, t, :], ln_stats[:, t, :])
                last.then_inc(stats2_v, 1)
                dve.wait_ge(stats2_v, NT + 1)
                dve.tensor_scalar(ln_std[:], ln_mv[:, :, 1], EPS, None, ALU.add).then_inc(var2_ready, 1)
                dve.wait_ge(std2_ready, 1)
                dve.reciprocal(ln_rstd[:], ln_std[:]).then_inc(stats2_v, 1)
                dve.wait_ge(stats2_v, NT + 2)
                second_norm.vector(dve)
                dve.wait_ge(bias1_turned, 1)
                dve.tensor_copy(bias1[:], bank[:, 2, 0:(X + 1) * KF])

            @block.scalar
            def _(act):
                act.wait_ge(var2_ready, 1)
                act.activation(ln_std[:], ln_std[:], ACT.Sqrt).then_inc(std2_ready, 1)

            @block.tensor
            def _(pe):
                pe.wait_ge(bias1_in, 32)
                pe.transpose(bank[:, 2, 0:(X + 1) * KF], bias1_rows[0:(X + 1) * KF, :],
                             ident[0:(X + 1) * KF, 0:(X + 1) * KF]).then_inc(bias1_turned, 1)
                second_norm.tensor(pe)
                pe.wait_ge(route_w_in, 16)
                pe.wait_ge(second_norm.placed, NT + 2)
                for t in range(NT):
                    for k in range(KD):
                        mm = pe.matmul(bank[:, 7, t * X:(t + 1) * X], feat_t[:, k, t * P:(t + 1) * P],
                                       route_w[:, k, :], start=k == 0, stop=k == KD - 1)
                mm.then_inc(logits_done, 1)

        free[0] = 0

        def per_expert():
            return room(NT * X).rearrange("p (t e) -> p t e", e=X)

        def over_experts(v):
            return v.unsqueeze(2).to_broadcast([P, NT, X])

        logit, prob, prob2, score, pick1, pick2, place_all, until = (per_expert() for _ in range(8))
        top1, top2, most, total_p, real, node_no = (room(NT) for _ in range(6))
        order = room(X)
        region = room(X)
        counts = room(X)
        counts_up = room(X)
        counts_i = room(X).bitcast(I32)
        blocks_i = room(X).bitcast(I32)
        blocks_f = room(X)
        picks_b = room(NT * X // 2).bitcast(BF16)
        before = room(P // 2).bitcast(BF16)
        ones_b = room(P // 2).bitcast(BF16)

        route_c = sem("route_c")
        route_v = sem("route_v")
        shifted = sem("shifted")
        powers = sem("powers")
        picked = sem("picked")
        ranked = sem("ranked")

        with nc.Block() as block:
            @block.gpsimd
            def _(pool):
                imp = dict(allow_small_or_imprecise_dtypes=True)
                pool.iota(order, [[-1, X]], X, 0, **imp).then_inc(route_c, 1)
                pool.iota(node_no, [[P, NT]], 0, 1, **imp).then_inc(route_c, 1)
                pool.memset(ones_b, 1.0).then_inc(route_c, 1)
                pool.wait_ge(route_c, 3)
                pool.affine_select(out=before, in_=ones_b, compare_op=ALU.is_gt, fill=0.0, base=0,
                                   pattern=[[1, P]], channel_multiplier=-1).then_inc(route_c, 1)

            @block.scalar
            def _(act):
                act.wait_ge(shifted, 1)
                act.activation(prob, prob2, ACT.Exp).then_inc(powers, 1)

            @block.tensor
            def _(pe):
                pe.wait_ge(picked, 1)
                pe.wait_ge(route_c, 4)
                pe.matmul(bank[:, 5, 0:NT * X], before, picks_b, start=True, stop=True)
                pe.matmul(bank[:, 6, 0:NT * X], ones_b, picks_b, start=True, stop=True).then_inc(ranked, 1)

            @block.vector
            def _(dve):
                n = [0]

                def link(ins):
                    n[0] += 1
                    ins.then_inc(route_v, 1)
                    dve.wait_ge(route_v, n[0])

                dve.wait_ge(route_c, 4)
                link(dve.tensor_copy(logit, bank[:, 7, 0:NT * X].rearrange("p (t e) -> p t e", e=X)))
                link(dve.tensor_reduce(most, logit, AX_X, ALU.max))
                dve.tensor_tensor(prob2, logit, over_experts(most), ALU.subtract).then_inc(shifted, 1)
                dve.tensor_scalar(real, node_no, float(N), None, ALU.is_lt)
                dve.wait_ge(powers, 1)
                link(dve.tensor_reduce(total_p, prob, AX_X, ALU.add))
                link(dve.reciprocal(most, total_p))
                link(dve.tensor_tensor(prob, prob, over_experts(most), ALU.mult))

                def pick(probs, top, into):
                    link(dve.tensor_reduce(top, probs, AX_X, ALU.max))
                    link(dve.tensor_tensor(score, probs, over_experts(top), ALU.is_equal))
                    link(dve.tensor_tensor(score, score, order.unsqueeze(1).to_broadcast([P, NT, X]), ALU.mult))
                    link(dve.tensor_reduce(most, score, AX_X, ALU.max))
                    link(dve.tensor_tensor(into, score, over_experts(most), ALU.is_equal))

                pick(prob, top1, pick1)
                link(dve.scalar_tensor_tensor(prob2, pick1, -2.0, prob, ALU.mult, ALU.add))
                pick(prob2, top2, pick2)
                link(dve.tensor_tensor(total_p, top1, top2, ALU.add))
                link(dve.reciprocal(most, total_p))
                dve.tensor_tensor(weight_of[:, :, 0], top1, most, ALU.mult)
                dve.tensor_tensor(weight_of[:, :, 1], top2, most, ALU.mult)
                dve.tensor_tensor(pick1, pick1, over_experts(real), ALU.mult)
                link(dve.tensor_tensor(pick2, pick2, over_experts(real), ALU.mult))
                dve.tensor_tensor(picks_b.rearrange("p (t e) -> p t e", e=X), pick1, pick2, ALU.add)\
                    .then_inc(picked, 1)
                dve.wait_ge(ranked, 1)
                link(dve.tensor_copy(score, bank[:, 6, 0:NT * X].rearrange("p (t e) -> p t e", e=X)))
                dve.memset(top1, 1.0).then_inc(route_v, 1)
                n[0] += 1
                dve.wait_ge(route_v, n[0])
                for e in range(X):
                    last = dve.tensor_tensor_scan(until[:, :, e], top1, score[:, :, e], 0.0, ALU.mult, ALU.add)
                link(last)
                link(dve.tensor_tensor(place_all, until, score, ALU.subtract))
                link(dve.tensor_scalar(counts_up, until[:, NT - 1, :], float(TOK - 1), None, ALU.add))
                link(dve.tensor_copy(counts_i, counts_up))
                link(dve.tensor_scalar(blocks_i, counts_i, TOK.bit_length() - 1, None, ALU.arith_shift_right))
                link(dve.tensor_copy(blocks_f, blocks_i))
                link(dve.tensor_scalar(counts, blocks_f, 1.0, None, ALU.max))
                dve.tensor_copy(plan_x[:, X:2 * X], counts[0:1, :])
                link(dve.tensor_tensor_scan(blocks_f, top1[:, 0:X], counts, 0.0, ALU.mult, ALU.add))
                dve.tensor_scalar(plan_x[:, 2 * X:2 * X + 1], blocks_f[0:1, X - 1:X], float(TOK), None, ALU.mult)
                link(dve.tensor_tensor(counts_up, blocks_f, counts, ALU.subtract))
                link(dve.tensor_scalar(region, counts_up, float(TOK), None, ALU.mult))
                link(dve.tensor_tensor(counts, region, until[:, NT - 1, :], ALU.add))
                dve.tensor_copy(plan_x[:, 0:X], counts[0:1, :])
                link(dve.tensor_tensor(place_all, place_all, region.unsqueeze(1).to_broadcast([P, NT, X]), ALU.add))
                link(dve.tensor_tensor(place_all, place_all,
                                       bank[:, 5, 0:NT * X].rearrange("p (t e) -> p t e", e=X), ALU.add))
                dve.tensor_tensor(prob, place_all, pick1, ALU.mult)
                link(dve.tensor_tensor(prob2, place_all, pick2, ALU.mult))
                dve.tensor_reduce(top1, prob, AX_X, ALU.add)
                link(dve.tensor_reduce(top2, prob2, AX_X, ALU.add))
                dve.tensor_copy(slot_of[:, :, 0], top1)
                dve.tensor_copy(slot_of[:, :, 1], top2)


        free[0] = 0
        hidden = room(KF * TOK).rearrange("p (c n) -> p c n", c=KF)
        bias2 = room((X + 1) * D).rearrange("p (x d) -> p x d", d=D)
        block_in = room(TB * D).rearrange("p (u d) -> p u d", u=TB)
        block_out = room(TB * D).rearrange("p (u d) -> p u d", u=TB)
        block_t = normed
        send = row_out[:, 0, :, :]
        fetched = row_out
        send_at = sb("send_at", [P, 4, 2], I32)
        turned_rows = mix_w[:, :, :].rearrange("p (s k) n -> p s k n", s=2)

        bias2_in = sem("bias2_in")
        tail_zero = sem("tail_zero")
        tails_in = sem("tails_in")
        results_zero = sem("results_zero")

        def block_rows_of(ap, b):
            return ap[ds(b * TOK, TOK), :].rearrange("(u p) d -> p u d", p=P)

        send_ready = sem("send_ready")
        sent = [sem(f"sent{u}") for u in range(4)]
        bias_added = sem("bias_added")

        class Expert:

            def __init__(self, name):
                self.up_done = sem(name + "_up_done")
                self.hidden_ready = sem(name + "_hidden_ready")
                self.down_done = sem(name + "_down_done")
                self.sums_taken = sem(name + "_sums_taken")

            def tensor(self, pe, at, s, rows_in, nt, between=None):
                w1, w2 = w1_set(s), w2_set(s)

                def up(c):
                    pe.wait_ge(self.hidden_ready, at * KF + c + 1)
                    for k in range(KD):
                        mm = pe.matmul(bank[:, c % 4, 0:nt * P], w1[:, k, c * P:(c + 1) * P], rows_in(k),
                                       start=k == 0, stop=k == KD - 1)
                    mm.then_inc(self.up_done, 1)

                def down(c):
                    pe.wait_ge(self.hidden_ready, at * KF + c + 5)
                    if c == 0:
                        pe.wait_ge(self.sums_taken, at + 1)
                    for u in range(nt):
                        mm = pe.matmul(bank[:, 4 + u, 0:D], hidden[:, c, u * P:(u + 1) * P], w2[:, c, :],
                                       start=c == 0, stop=c == KF - 1)
                    mm.then_inc(self.down_done, 1)

                up(0)
                for c in range(1, KF):
                    up(c)
                    down(c - 1)
                    if between and c == KF // 2:
                        between()
                down(KF - 1)

            def scalar(self, act, at, bias, nt):
                for c in range(KF):
                    act.wait_ge(self.up_done, at * KF + c + 1)
                    act.wait_ge(self.down_done, at * KF + c + 1)
                    act.activation(hidden[:, c, 0:nt * P], bank[:, c % 4, 0:nt * P], ACT.Gelu,
                                   bias=bias(c)).then_inc(self.hidden_ready, 1)

        shared = Expert("shared")
        NS = NT // TB
        NS1 = NS // 2
        assert NS1 == NT // 4 and NS == 2 * NS1

        def shared_bias(c):
            return bias1[:, X * KF + c:X * KF + c + 1]

        def take_shared(dve, b, nt):
            dve.wait_ge(shared.down_done, b * KF + 2 * KF)
            for u in range(nt):
                last = dve.tensor_tensor(tile(resid, b * TB + u), bank[:, 4 + u, 0:D],
                                         tile(resid, b * TB + u), ALU.add)
            last.then_inc(shared.sums_taken, 1)

        with nc.Block() as block:
            @block.sync
            def _(sp):
                sp.dma_start(bias2[:, X, :], b2s.partition_broadcast(P)).then_inc(bias2_in, 16)
                sp.dma_start(bias2[:, 0:X, :].rearrange("p x d -> p (x d)"),
                             b2p.rearrange("x d -> (x d)").partition_broadcast(P)).then_inc(bias2_in, 16)
                sp.wait_ge(tail_zero, 1)
                for e in range(X + 1):
                    at = e if e < X else 2 * X
                    n = sp.value_load(plan_x[:, at:at + 1], min_val=0, max_val=MAXB * TOK)
                    sp.dma_start(expert_in[ds(n, TOK), :].rearrange("(u p) d -> p u d", p=P), block_in)\
                        .then_inc(tails_in, 16)
                    sp.wait_ge(tails_in, 16 * (e + 1))
                with sp.Fori(0, MAXB) as b:
                    sp.dma_start(block_rows_of(expert_out, b), block_in).then_inc(results_zero, 16)
                sp.wait_ge(results_zero, 16 * MAXB)
                sp.wait_ge(bias2_in, 32)

            @block.gpsimd
            def _(pool):
                def scatter(t, u, p):
                    pool.wait_ge(send_ready, t + 1)
                    gated(pool)
                    for w in range(2):
                        pool.indirect_dma_start(expert_in, bass.IndirectOffsetOnAxis(ap=send_at[0:p, u, w:w + 1], axis=0),
                                                send[0:p, u, :], None).then_inc(sent[u], 16)

                pool.wait_ge(tails_in, 16 * (X + 1))
                with pool.Fori(0, NT // 4) as i:
                    for u in range(4):
                        scatter(i * 4 + u, u, P)
                scatter(NT - 1, 0, LAST)
                pool.wait_ge(sent[0], 32 * (NT // 4 + 1))
                for u in range(1, 4):
                    pool.wait_ge(sent[u], 32 * (NT // 4))

            @block.scalar
            def _(act):
                act.sem_inc(shared.hidden_ready, 4)
                with act.Fori(0, NS1) as b:
                    shared.scalar(act, b, shared_bias, TB)

            @block.vector
            def _(dve):
                dve.memset(block_in, 0.0).then_inc(tail_zero, 1)
                dve.wait_ge(bias2_in, 32)

                def prepare(t, u, seen):
                    wait_past(dve, sent[u], seen)
                    dve.tensor_scalar(send[:, u, :], tile(resid, t), ln_mv[:, ds(t, 1), 0], ln_rstd[:, ds(t, 1)],
                                      ALU.subtract, ALU.mult)
                    dve.tensor_copy(send_at[:, u, :], tile(slot_of, t)).then_inc(send_ready, 1)
                    dve.tensor_tensor(tile(resid, t), tile(resid, t), bias2[:, X, :], ALU.add).then_inc(bias_added, 1)

                def four(i):
                    for u in range(4):
                        prepare(i * 4 + u, u, i * 32)
                    dve.wait_ge(bias_added, i * 4 + 4)
                    take_shared(dve, i, TB)

                dve.sem_inc(shared.sums_taken, 1)
                loop(dve, NT // 4, four)
                prepare(NT - 1, 0, 32 * (NT // 4))

            @block.tensor
            def _(pe):
                pe.sem_inc(shared.down_done, KF)
                with pe.Fori(0, NS1) as b:
                    shared.tensor(pe, b, 2, lambda k: feat_t[:, k, nodes(b * TB, TB)], TB)

        routed = Expert("routed")
        rows_in = sem("rows_in")
        rows_turned = sem("rows_turned")
        rows_placed = sem("rows_placed")
        out_stored = sem("out_stored")
        out_free = sem("out_free")
        expert_done = sem("expert_done")
        weights_in = [sem(f"weights_in{s}") for s in range(2)]
        set_ready = [sem(f"set_ready{s}") for s in range(2)]
        def experts(engine, name, body, before=None, after=None):
            r = counter(engine, name)
            with engine.Fori(0, X // 2) as v:
                for s in range(2):
                    e = v * 2 + s
                    if before:
                        before(e, s, v)
                    n = engine.value_load(plan_x[:, ds(e + X, 1)], min_val=1, max_val=EACH)
                    with engine.Fori(0, n):
                        at = engine.snap(r, min_val=0, max_val=MAXB - 1)
                        body(e, s, at)
                        engine.reg_add(r, r, 1)
                    if after:
                        after()
            return engine.snap(r, min_val=0, max_val=MAXB)

        with nc.Block() as block:
            @block.sync
            def _(sp):
                def load(at):
                    sp.wait_ge(rows_turned, at + 1)
                    gated(sp)
                    sp.dma_start(block_in, block_rows_of(expert_in, at)).then_inc(rows_in, 16)

                def body(e, s, at):
                    load(at + 1)
                    sp.wait_ge(routed.sums_taken, at + 2)
                    gated(sp)
                    sp.dma_start(block_rows_of(expert_out, at), block_out).then_inc(out_stored, 16)
                    sp.wait_ge(out_stored, at * 16 + 16)
                    sp.sem_inc(out_free, 1)

                sp.sem_inc(out_free, 1)
                load(0)
                at = experts(sp, "sp_blocks", body)
                sp.wait_ge(rows_in, at * 16 + 16)
                gated(sp)

            @block.gpsimd
            def _(pool):
                for s in range(2):
                    pool.sem_inc(set_ready[s], 1)
                with pool.Fori(0, X // 2 - 1) as v:
                    for s in range(2):
                        pool.wait_ge(expert_done, v * 2 + s + 1)
                        gated(pool)
                        e = v * 2 + (s + 2)
                        load_set(pool, s, w1p[ds(e, 1), :, :].rearrange("a (k p) f -> p (a k) f", p=P),
                                 w2p[ds(e, 1), :, :].rearrange("a (c p) d -> p (a c) d", p=P), weights_in[s])
                        pool.wait_ge(weights_in[s], v * 32 + 32)
                        pool.sem_inc(set_ready[s], 1)

            @block.scalar
            def _(act):
                def body(e, s, at):
                    routed.scalar(act, at, lambda c: bias1[:, ds(e * KF + c, 1)], TB)

                act.sem_inc(routed.hidden_ready, 4)
                experts(act, "act_blocks", body)

            @block.vector
            def _(dve):
                def place(at):
                    dve.wait_ge(rows_turned, at + 2)
                    dve.tensor_copy(turned_rows[:, ds(at % 2, 1), :, :].rearrange("p a k n -> p (a k) n"),
                                    bank[:, 6, :].rearrange("p (k n) -> p k n", k=KD)).then_inc(rows_placed, 1)

                def body(e, s, at):
                    place(at + 1)
                    dve.wait_ge(routed.down_done, at * KF + 2 * KF)
                    dve.wait_ge(out_free, at + 1)
                    for u in range(TB):
                        last = dve.tensor_tensor(block_out[:, u, :], bank[:, 4 + u, 0:D], tile(bias2, e), ALU.add)
                    last.then_inc(routed.sums_taken, 1)

                dve.sem_inc(rows_placed, 1)
                dve.sem_inc(routed.sums_taken, 1)
                place(0)
                experts(dve, "dve_blocks", body)

            @block.tensor
            def _(pe):
                def turn(at):
                    pe.wait_ge(rows_in, at * 16 + 16)
                    pe.wait_ge(rows_placed, at + 1)
                    for k in range(KD):
                        for u in range(TB):
                            mm = pe.transpose(bank[:, 6, (k * TB + u) * P:(k * TB + u + 1) * P],
                                              block_in[:, u, k * P:(k + 1) * P], ident[:])
                    mm.then_inc(rows_turned, 1)

                def before(e, s, v):
                    pe.wait_ge(set_ready[s], v + 1)
                    gated(pe)

                def body(e, s, at):
                    pe.wait_ge(rows_placed, at + 2)
                    slot = turned_rows[:, ds(at % 2, 1), :, :].rearrange("p a k n -> p (a k) n")
                    routed.tensor(pe, at, s, lambda k: slot[:, k, :], TB, between=lambda: turn(at + 1))

                pe.sem_inc(routed.down_done, KF)
                pe.sem_inc(rows_turned, 1)
                turn(0)
                experts(pe, "pe_blocks", body, before,
                        lambda: pe.matmul(bank[:, 7, 0:8], zero[:, 0:P], zero[:, 0:8], start=True, stop=True)
                        .then_inc(expert_done, 1))

        fetch_at = send_at
        fetch_ready = sem("fetch_ready")
        fetched_in = [sem(f"fetched_in{u}") for u in range(4)]
        half_added = sem("half_added")
        added = sem("added")
        stored = [sem(f"stored{u}") for u in range(4)]

        def fours(engine, body):
            def four(i):
                for u in range(4):
                    body(i * 4 + u, u, i, P)

            loop(engine, NT // 4, four)
            body(NT - 1, 0, NT // 4, LAST)

        with nc.Block() as block:
            @block.sync
            def _(sp):
                def store(t, u, i, p):
                    sp.wait_ge(added, t + 1)
                    gated(sp)
                    sp.dma_start(out[ds(t * P, p), :], tile(resid, t)[0:p, :]).then_inc(stored[u], 16)

                fours(sp, store)
                sp.wait_ge(stored[0], 16 * (NT // 4 + 1))
                for u in range(1, 4):
                    sp.wait_ge(stored[u], 16 * (NT // 4))

            @block.gpsimd
            def _(pool):
                def fetch(t, u, i, p):
                    pool.wait_ge(fetch_ready, t + 1)
                    wait_past(pool, added, i * 4)
                    gated(pool)
                    for w in range(2):
                        pool.indirect_dma_start(
                            fetched[:, w, u, :], None, expert_out,
                            bass.IndirectOffsetOnAxis(ap=fetch_at[:, u, w:w + 1], axis=0)).then_inc(fetched_in[u], 16)

                fours(pool, fetch)

            @block.scalar
            def _(act):
                def indices(t, u, i):
                    wait_past(act, fetched_in[u], i * 32)
                    act.activation(fetch_at[:, u, :], tile(slot_of, t), ACT.Copy).then_inc(fetch_ready, 1)

                def four(i):
                    for u in range(4):
                        indices(i * 4 + u, u, i)
                    shared.scalar(act, i + NS1, shared_bias, TB)

                loop(act, NT // 4, four)
                indices(NT - 1, 0, NT // 4)
                shared.scalar(act, NS, shared_bias, 1)

            @block.vector
            def _(dve):
                def add(t, u, i):
                    dve.wait_ge(fetched_in[u], i * 32 + 32)
                    for w in range(2):
                        dve.scalar_tensor_tensor(tile(resid, t), fetched[:, w, u, :], tile(weight_of, t)[:, w:w + 1],
                                                 tile(resid, t), ALU.mult, ALU.add)\
                            .then_inc([half_added, added][w], 1)
                        if w == 0:
                            dve.wait_ge(half_added, t + 1)

                def four(i):
                    take_shared(dve, i + NS1, TB)
                    dve.wait_ge(shared.sums_taken, i + NS1 + 2)
                    for u in range(4):
                        add(i * 4 + u, u, i)

                loop(dve, NT // 4, four)
                take_shared(dve, NS, 1)
                dve.wait_ge(shared.sums_taken, NS + 2)
                add(NT - 1, 0, NT // 4)

            @block.tensor
            def _(pe):
                with pe.Fori(NS1, NS) as b:
                    shared.tensor(pe, b, 2, lambda k: feat_t[:, k, nodes(b * TB, TB)], TB)
                shared.tensor(pe, NS, 2, lambda k: feat_t[:, k, nodes(NT - 1)], 1)


_INS = ['x', 'src', 'dst', 'edge_attr_4', 'L0_gnn_mlp_w', 'L0_gnn_mlp_b', 'L0_gnn_ew1', 'L0_gnn_ew2',
        'L0_gnn_bn_g', 'L0_gnn_bn_b', 'L0_ffn_Wr', 'L0_ffn_W1s', 'L0_ffn_b1s', 'L0_ffn_W2s', 'L0_ffn_b2s',
        'L0_ffn_W1p', 'L0_ffn_b1p', 'L0_ffn_W2p', 'L0_ffn_b2p']
_OUTS = [((6250, 256), 'float32')]


def kernel(**inputs):
    import numpy as _np
    import concourse.bacc as _bacc
    from concourse import mybir as _mybir
    from concourse.bass_utils import run_bass_kernel_spmd as _run

    nc = _bacc.Bacc("TRN2", target_bir_lowering=False, num_devices=1)
    arrays, args = {}, []
    for name in _INS:
        a = _np.ascontiguousarray(inputs[name])
        arrays[f"in_{name}_dram"] = a
        args.append(nc.dram_tensor(f"in_{name}_dram", a.shape, _mybir.dt.from_np(a.dtype), kind="ExternalInput").ap())
    for i, (shape, dtype) in enumerate(_OUTS):
        dt = _mybir.dt.from_np(_np.dtype(dtype))
        args.append(nc.dram_tensor(f"out_{i}_dram", shape, dt, kind="ExternalOutput").ap())
    build(nc, *args)
    r = _run(nc, [arrays], core_ids=[0])
    got = tuple(r.results[0][f"out_{i}_dram"] for i in range(len(_OUTS)))
    return got[0]
```

```python
from contextlib import ExitStack

import concourse.bass as bass
from concourse import mybir

F32 = mybir.dt.float32
BF16 = mybir.dt.bfloat16
I32 = mybir.dt.int32
ALU = mybir.AluOpType
ACT = mybir.ActivationFunctionType
AX_X = mybir.AxisListType.X
ds = bass.ds

P = 128
K = 8
GG = 2
MINS = 1
EPS = 1e-5
FAR = 1000000


def build(nc, x, src, dst, attr, mlp_w, mlp_b, ew1, ew2, bn_g, bn_b,
          wr, w1s, b1s, w2s, b2s, w1p, b1p, w2p, b2p, out):
    N, D = x.shape
    E = src.shape[0]
    L = mlp_w.shape[0]
    X = wr.shape[1]
    F = w1s.shape[1]
    A = attr.shape[1]
    KD = D // P
    KF = F // P
    NT = -(-N // P)
    LAST = N - (NT - 1) * P
    NP = NT * P
    NC = -(-E // P)
    CB = -(-NC // P)
    COLS = CB * P
    FULLC = E // P
    REST = E - FULLC * P
    MAXG = -(-NC // K) + GG + 1
    W0 = D + 1
    TB = 2
    TOK = TB * P
    EACH = -(-N // TOK)
    MAXB = 2 * N // TOK + X
    assert KD == 2 and NC + K * (MINS + GG + 1) < COLS and REST > 0 and L >= 3
    assert (NT - 1) % 4 == 0 and NT * X <= 512

    rows0 = nc.dram_tensor("rows0", (NP, W0), F32).ap()
    rows = nc.dram_tensor("rows", (NP, D), F32).ap()
    expert_in = nc.dram_tensor("expert_in", ((MAXB + 1) * TOK, D), F32).ap()
    expert_out = nc.dram_tensor("expert_out", (MAXB * TOK, D), F32).ap()

    with ExitStack() as ctx:
        def sb(name, shape, dt=F32):
            return ctx.enter_context(nc.sbuf_tensor(name, shape, dt))

        def sem(name):
            return ctx.enter_context(nc.semaphore(name))

        bank = ctx.enter_context(nc.psum_tensor("bank", [P, 8, 512], F32))

        feat_t = sb("feat_t", [P, KD, NP])
        resid = sb("resid", [P, NT, D])
        ident = sb("ident", [P, P])
        iota_row = sb("iota_row", [P, P])
        dinv = sb("dinv", [P, NT])
        zero = sb("zero", [1, 512], BF16)
        ln_stats = sb("ln_stats", [P, NT, 6])
        ln_mv = sb("ln_mv", [P, NT, 2])
        ln_rstd = sb("ln_rstd", [P, NT])
        ln_std = sb("ln_std", [P, NT])
        ln_shift = sb("ln_shift", [P, NT])

        arena = sb("arena", [P, COLS * (2 + A) + 1024])
        src_col = arena[:, 0:COLS].bitcast(I32)
        dst_col = arena[:, COLS:2 * COLS]
        attr_col = arena[:, 2 * COLS:(2 + A) * COLS].rearrange("p (c a) -> p c a", a=A)
        iota_bf = arena[:, (2 + A) * COLS:(2 + A) * COLS + P // 2].bitcast(BF16)

        SET = KD * F + KF * D
        sets = sb("sets", [P, 3 * SET])

        def w1_set(s):
            return sets[:, s * SET:s * SET + KD * F].rearrange("p (k f) -> p k f", k=KD)

        def w2_set(s):
            return sets[:, s * SET + KD * F:(s + 1) * SET].rearrange("p (c d) -> p c d", c=KF)

        staged = [0]

        def stage(n):
            staged[0] += n
            assert staged[0] <= 3 * SET
            return sets[:, staged[0] - n:staged[0]]

        dst_int = stage(COLS).bitcast(I32).rearrange("p (b e) -> p b e", b=CB)
        src_int = stage(COLS).bitcast(I32).rearrange("p (b e) -> p b e", b=CB)
        dst_f = stage(COLS).rearrange("p (b e) -> p b e", b=CB)
        src_f = stage(COLS).rearrange("p (b e) -> p b e", b=CB)
        dst_ii = stage(COLS).bitcast(I32)
        row0_out = sets[:, 0:4 * 4 * (W0 + 3)].rearrange("p (s t d) -> p s t d", s=4, t=4)
        assert staged[0] >= 4 * 4 * (W0 + 3)
        attr_in = stage(COLS * A).rearrange("p (b e a) -> p b e a", b=CB, a=A)
        c_lo = stage(CB)
        c_hi = stage(CB)
        tile_at = stage(NT)
        tile_at_end = stage(NT)
        chunk_up = stage(CB)
        chunk_down = stage(CB)
        act_lo = stage(NT * CB).rearrange("p (t b) -> p t b", t=NT)
        act_hi = stage(NT * CB).rearrange("p (t b) -> p t b", t=NT)
        bounds = stage(2 * NT)
        bounds_all = stage(2 * NT)
        first_c, last_c, first_g, last_g, wide, shares, start_g, end_g, before_last, base_2 = (
            stage(NT) for _ in range(10))
        first_i, last_i = (stage(NT).bitcast(I32) for _ in range(2))
        some = stage(NT)
        total = stage(4)
        total_i = stage(4).bitcast(I32)
        lo_i = src_int.rearrange("p b e -> p (b e)")
        hi_i = dst_int.rearrange("p b e -> p (b e)")
        lo_b = stage(COLS // 2).bitcast(BF16)
        hi_b = stage(COLS // 2).bitcast(BF16)
        hi_half = stage(COLS)
        deg_steps = stage(NT + 1)
        deg = stage(NT)
        deg1 = stage(NT)
        deg_root = stage(NT)
        deg_inv = stage(NT)
        deg_some = stage(NT)
        CG = 8
        RADIX = NT + 1
        row_out = sb("row_out", [P, 2, 4, D])
        count_room = row_out[:, :, :, :].rearrange("p a b d -> p (a b d)").bitcast(BF16)
        hot_lo = [count_room[:, i * CG * P:(i + 1) * CG * P].rearrange("p (c n) -> p c n", c=CG) for i in range(2)]
        step_hi, hot_hi = (count_room[:, 2 * CG * P + i * CG * 64:2 * CG * P + (i + 1) * CG * 64].rearrange(
            "p (c n) -> p c n", c=CG) for i in range(2))
        assert RADIX <= 64
        row0_scale = stage(NT)
        row0_shift = stage(NT)

        plan = sb("plan", [1, 2 * NT + 1], I32)
        plan_first = plan[:, 0:NT]
        plan_groups = plan[:, NT:2 * NT]
        plan_total = plan[:, 2 * NT:2 * NT + 1]
        neg_base = sb("neg_base", [P, NT])
        neg_base_2 = sb("neg_base_2", [P, NT])

        normed = sb("normed", [P, 2, D])

        edges_in = sem("edges_in")
        attr_loaded = sem("attr_loaded")
        padded = sem("padded")
        consts = sem("consts")
        as_float = sem("as_float")
        turned = sem("turned")
        placed = sem("placed")
        prep_v = sem("prep_v")
        reduce_in = sem("reduce_in")
        reduce_out = sem("reduce_out")
        hot_ready = sem("hot_ready")
        step_ready = sem("step_ready")
        ln_ready = sem("ln_ready")
        gate = sem("gate")
        counted = sem("counted")
        root_in = sem("root_in")
        step_in = sem("step_in")
        root_out = sem("root_out")
        x_in = [sem(f"x_in{i}") for i in range(2)]
        HALF = NT // 14 * 7 + 7
        pre_p = sem("pre_p")

        def edge_parts(flat, tile, w):
            full = FULLC // P
            a = full * P * P
            b = FULLC * P
            r = FULLC - full * P
            if w == 1:
                yield flat[0:a].rearrange("(k p e) -> p k e", p=P, e=P), tile[:, 0:full, :]
                yield flat[a:b].rearrange("(p e) -> p e", e=P), tile[0:r, full, :]
                yield flat[b:E].rearrange("(p e) -> p e", p=1), tile[r:r + 1, full, 0:REST]
            else:
                yield (flat[0:a, :].rearrange("(k p e) a -> p k (e a)", p=P, e=P),
                       tile[:, 0:full, :, :].rearrange("p k e a -> p k (e a)"))
                yield (flat[a:b, :].rearrange("(p e) a -> p (e a)", e=P),
                       tile[0:r, full, :, :].rearrange("p e a -> p (e a)"))
                yield (flat[b:E, :].rearrange("(p e) a -> p (e a)", p=1),
                       tile[r:r + 1, full, 0:REST, :].rearrange("p e a -> p (e a)"))

        def turns():
            for b in range(CB):
                yield "dst", b, 0
            for b in range(CB):
                yield "src", b, 0
            for a in range(A):
                for b in range(CB):
                    yield "attr", b, a

        TURNS = list(turns())

        def turn_edges(pe, i):
            what, b, a = TURNS[i]
            if i >= 4:
                pe.wait_ge(placed, i - 3)
            of = {"dst": dst_f[:, b, :], "src": src_f[:, b, :], "attr": attr_in[:, b, :, a]}[what]
            pe.transpose(bank[:, i % 4, 0:P], of, ident[:]).then_inc(turned, 1)

        def place_edges(dve, i):
            what, b, a = TURNS[i]
            dve.wait_ge(turned, i + 1)
            col = slice(b * P, (b + 1) * P)
            to = {"dst": dst_col[:, col], "src": src_col[:, col], "attr": attr_col[:, col, a]}[what]
            dve.tensor_copy(to, bank[:, i % 4, 0:P]).then_inc(placed, 1)

        def loop(engine, n, body):
            body(0)
            with engine.Fori(1, n) as i:
                body(i)

        def wait_past(engine, what, value):
            if not isinstance(value, int) or value > 0:
                engine.wait_ge(what, value)

        def tile_stats(dve, a, b, done):
            assert a % 7 == b % 7 == 0
            with dve.Fori(a // 7, b // 7) as i:
                for u in range(7):
                    dve.bn_stats(tile(ln_stats, i * 7 + u), tile(resid, i * 7 + u)).then_inc(done, 1)

        def tile(ap, t):
            return ap[:, ds(t, 1), :].rearrange("p a s -> p (a s)")

        def nodes(t, n=1):
            return ds(t * P, n * P)

        def gated(engine):
            engine.sem_inc(gate, 1)

        class Norm:

            def __init__(self, name, banks):
                self.banks = banks
                self.ready = sem(name + "_ready")
                self.turned = sem(name + "_turned")
                self.placed = sem(name + "_placed")

            def normalise(self, act, t, s):
                act.wait_ge(self.turned, t + 1)
                gated(act)
                act.activation(normed[:, s, :], tile(resid, t), ACT.Identity, bias=ln_shift[:, ds(t, 1)],
                               scale=ln_rstd[:, ds(t, 1)]).then_inc(self.ready, 1)

            def turn(self, pe, t, s):
                pe.wait_ge(self.ready, t + 1)
                pe.wait_ge(self.placed, t + 1)
                for k in range(KD):
                    mm = pe.transpose(bank[:, self.banks + s, k * P:(k + 1) * P], normed[:, s, k * P:(k + 1) * P],
                                      ident[:])
                mm.then_inc(self.turned, 1)

            def place(self, dve, t, s):
                dve.wait_ge(self.turned, t + 3)
                dve.tensor_copy(feat_t[:, :, nodes(t)],
                                bank[:, self.banks + s, 0:D].rearrange("p (k n) -> p k n", k=KD))\
                    .then_inc(self.placed, 1)

        def tile_pairs(engine, body, rest=0):
            with engine.Fori(0, NT // 2) as i:
                for u in range(2):
                    body(i * 2 + u, u)
            for t in range(NT - 1, NT + rest):
                body(t, t % 2)

        first_norm = Norm("norm", 5)
        COUNT_STEPS = -(-NC // (2 * CG))
        assert COUNT_STEPS >= NT

        with nc.Block() as block:
            @block.sync
            def _(sp):
                sp.wait_ge(padded, 2)
                for d, s in [*edge_parts(dst, dst_int, 1), *edge_parts(src, src_int, 1)]:
                    sp.dma_start(s, d).then_inc(edges_in, 16)
                sp.wait_ge(padded, 3)
                for d, s in edge_parts(attr, attr_in, A):
                    sp.dma_start(s, d).then_inc(attr_loaded, 16)
                sp.wait_ge(edges_in, 16 * 6)
                sp.wait_ge(attr_loaded, 16 * 3)
                sp.wait_ge(x_in[0], 16)
                sp.wait_ge(x_in[1], 32)

            @block.gpsimd
            def _(pool):
                pool.memset(ident[:], 0.0).then_inc(pre_p, 1)
                pool.wait_ge(pre_p, 1)
                pool.affine_select(out=ident[:], in_=ident[:], compare_op=ALU.not_equal, fill=1.0, base=0,
                                   pattern=[[-1, P]], channel_multiplier=1).then_inc(consts, 1)
                imp = dict(allow_small_or_imprecise_dtypes=True)
                pool.iota(iota_row[:], [[1, P]], 0, 0, **imp).then_inc(consts, 1)
                pool.iota(iota_bf, [[1, P]], 0, 0, **imp).then_inc(consts, 1)
                pool.iota(tile_at, [[P, NT]], 0, 0, **imp).then_inc(consts, 1)
                pool.iota(tile_at_end, [[P, NT]], P, 0, **imp).then_inc(consts, 1)
                pool.iota(neg_base[:], [[-P, NT]], 0, 0, **imp).then_inc(consts, 1)
                pool.iota(base_2, [[-P, NT]], -P - FAR, 0, **imp).then_inc(consts, 1)
                pool.iota(chunk_up, [[P, CB]], 1, 1, **imp).then_inc(consts, 1)
                pool.iota(chunk_down, [[-P, CB]], COLS, -1, **imp).then_inc(consts, 1)
                pool.memset(resid[:, NT - 1, :], 0.0).then_inc(pre_p, 1)
                pool.wait_ge(pre_p, 2)
                full = (NT - 1) * P
                pool.wait_ge(edges_in, 16 * 6)
                for part, (a, b) in enumerate([(0, HALF), (HALF, NT - 1)]):
                    pool.dma_start(resid[:, a:b, :],
                                   x[a * P:b * P, :].rearrange("(t p) d -> p t d", p=P)).then_inc(x_in[part], 16)
                pool.dma_start(resid[0:LAST, NT - 1, :], x[full:N, :]).then_inc(x_in[1], 16)
                pool.wait_ge(reduce_in, 1)
                pool.partition_all_reduce(bounds_all, bounds, P, bass.bass_isa.ReduceOp.max)\
                    .then_inc(reduce_out, 1)

            @block.vector
            def _(dve):
                n = [0]

                def link(ins):
                    n[0] += 1
                    ins.then_inc(prep_v, 1)
                    dve.wait_ge(prep_v, n[0])

                dve.memset(dst_int, FAR).then_inc(padded, 1)
                dve.memset(src_int, 0).then_inc(padded, 1)
                dve.memset(attr_in, 0.0).then_inc(padded, 1)
                dve.memset(zero[:], 0.0).then_inc(padded, 1)
                dve.wait_ge(edges_in, 16 * 6)
                dve.tensor_copy(dst_f, dst_int).then_inc(as_float, 1)
                dve.tensor_copy(src_f, src_int).then_inc(as_float, 1)
                dve.wait_ge(as_float, 2)
                dve.tensor_reduce(c_lo, dst_f, AX_X, ALU.min)
                link(dve.tensor_reduce(c_hi, dst_f, AX_X, ALU.max))
                dve.wait_ge(consts, 9)
                dve.tensor_tensor(act_lo, c_lo.unsqueeze(1).to_broadcast([P, NT, CB]),
                                  tile_at_end.unsqueeze(2).to_broadcast([P, NT, CB]), ALU.is_lt)
                link(dve.tensor_tensor(act_hi, c_hi.unsqueeze(1).to_broadcast([P, NT, CB]),
                                       tile_at.unsqueeze(2).to_broadcast([P, NT, CB]), ALU.is_ge))
                link(dve.tensor_tensor(act_lo, act_lo, act_hi, ALU.mult))
                link(dve.tensor_tensor(act_hi, act_lo, chunk_up.unsqueeze(1).to_broadcast([P, NT, CB]), ALU.mult))
                link(dve.tensor_tensor(act_lo, act_lo, chunk_down.unsqueeze(1).to_broadcast([P, NT, CB]),
                                       ALU.mult))
                link(dve.tensor_reduce(bounds[:, 0:NT], act_lo, AX_X, ALU.max))
                dve.tensor_reduce(bounds[:, NT:2 * NT], act_hi, AX_X, ALU.max).then_inc(reduce_in, 1)

                for i in range(2 * CB):
                    place_edges(dve, i)
                dve.wait_ge(placed, 2 * CB)
                link(dve.tensor_copy(dst_ii, dst_col))
                dve.tensor_scalar(lo_i, dst_ii, P - 1, None, ALU.bitwise_and)
                link(dve.tensor_scalar(hi_i, dst_ii, 7, None, ALU.arith_shift_right))
                dve.tensor_copy(lo_b, lo_i)
                dve.tensor_copy(hi_b, hi_i)
                dve.tensor_scalar(hi_half, hi_i, 0.5, None, ALU.add).then_inc(step_in, 1)
                dve.wait_ge(x_in[0], 16)
                tile_stats(dve, 0, HALF, prep_v)
                dve.wait_ge(x_in[1], 32)
                tile_stats(dve, HALF, NT, prep_v)
                n[0] += NT
                dve.wait_ge(prep_v, n[0])
                for t in range(NT):
                    last = dve.bn_aggr(ln_mv[:, t, :], ln_stats[:, t, :])
                link(last)
                dve.tensor_scalar(ln_std[:], ln_mv[:, :, 1], EPS, None, ALU.add).then_inc(root_in, 1)
                dve.wait_ge(root_out, 1)
                link(dve.reciprocal(ln_rstd[:], ln_std[:]))
                dve.scalar_tensor_tensor(ln_shift[:], ln_mv[:, :, 0], -1.0, ln_rstd[:], ALU.mult, ALU.mult)\
                    .then_inc(ln_ready, 1)
                dve.sem_inc(first_norm.placed, 2)

                def count(t, s):
                    for h in range(2):
                        dve.wait_ge(counted, 2 * t + h + 1)
                        dve.tensor_tensor(hot_lo[h], iota_bf.unsqueeze(1).to_broadcast([P, CG, P]),
                                          lo_b[:, ds(t * (2 * CG) + h * CG, CG)].unsqueeze(2).to_broadcast([P, CG, P]),
                                          ALU.is_equal).then_inc(hot_ready, 1)
                    dve.tensor_tensor(hot_hi[:, :, 0:NT], iota_bf[:, 0:NT].unsqueeze(1).to_broadcast([P, CG, NT]),
                                      hi_b[:, ds(t * (2 * CG) + CG, CG)].unsqueeze(2).to_broadcast([P, CG, NT]),
                                      ALU.is_equal).then_inc(hot_ready, 1)
                    if not isinstance(t, int) or t < NT:
                        first_norm.place(dve, t, s)

                tile_pairs(dve, count, COUNT_STEPS - NT)
                dve.wait_ge(counted, 2 * COUNT_STEPS + 3)
                link(dve.tensor_copy(deg_steps, bank[:, 4, 0:RADIX]))
                link(dve.tensor_tensor(deg1, deg_steps[:, 0:NT], deg_steps[:, 1:RADIX], ALU.subtract))
                link(dve.scalar_tensor_tensor(deg, deg1, 0.5, bank[:, 7, 0:NT], ALU.mult, ALU.add))
                dve.tensor_scalar(deg_some, deg, 0.0, None, ALU.is_gt)
                dve.tensor_scalar(deg1, deg, 1.0, None, ALU.max).then_inc(root_in, 1)
                dve.wait_ge(root_out, 2)
                link(dve.reciprocal(deg_inv, deg_root))
                link(dve.tensor_tensor(dinv[:], deg_inv, deg_some, ALU.mult))
                dve.tensor_tensor(row0_scale, ln_rstd[:], dinv[:], ALU.mult)
                dve.tensor_tensor(row0_shift, ln_shift[:], dinv[:], ALU.mult)

            @block.scalar
            def _(act):
                act.wait_ge(root_in, 1)
                act.activation(ln_std[:], ln_std[:], ACT.Sqrt).then_inc(root_out, 1)
                act.wait_ge(ln_ready, 1)
                act.wait_ge(step_in, 1)

                def count(t, s):
                    if not isinstance(t, int) or t < NT:
                        first_norm.normalise(act, t, s)
                    act.wait_ge(counted, 2 * t + 1)
                    gated(act)
                    for c in range(CG):
                        last = act.activation(step_hi[:, c, 0:RADIX], iota_row[:, 0:RADIX], ACT.Sign,
                                              bias=hi_half[:, ds(t * (2 * CG) + c, 1)], scale=-1.0)
                    last.then_inc(step_ready, 1)

                tile_pairs(act, count, COUNT_STEPS - NT)
                act.wait_ge(root_in, 2)
                act.activation(deg_root, deg1, ACT.Sqrt).then_inc(root_out, 1)

            @block.tensor
            def _(pe):
                pe.wait_ge(as_float, 2)
                pe.wait_ge(consts, 1)

                for i in range(2 * CB):
                    turn_edges(pe, i)
                pe.sem_inc(counted, 2)
                pe.sem_inc(first_norm.turned, 2)
                pe.wait_ge(padded, 4)
                pe.matmul(bank[:, 4, 0:RADIX], zero[:, 0:P], zero[:, 0:RADIX], start=True, stop=False)
                pe.matmul(bank[:, 7, 0:NT], zero[:, 0:P], zero[:, 0:NT], start=True, stop=False)

                def count(t, s):
                    if not isinstance(t, int) or t < NT:
                        first_norm.turn(pe, t, s)
                    for h in range(2):
                        pe.wait_ge(hot_ready, 3 * t + 2 * h + 1)
                        if h == 0:
                            pe.wait_ge(step_ready, t + 1)
                        for c in range(CG):
                            mm = pe.matmul(bank[:, 4, 0:RADIX] if h == 0 else bank[:, 7, 0:NT], hot_lo[h][:, c, :],
                                           step_hi[:, c, 0:RADIX] if h == 0 else hot_hi[:, c, 0:NT],
                                           start=False, stop=False)
                        mm.then_inc(counted, 1)

                tile_pairs(pe, count, COUNT_STEPS - NT)
                pe.matmul(bank[:, 4, 0:RADIX], zero[:, 0:P], zero[:, 0:RADIX], start=False, stop=True)
                pe.matmul(bank[:, 7, 0:NT], zero[:, 0:P], zero[:, 0:NT], start=False, stop=True).then_inc(counted, 1)


        mix_w = sb("mix_w", [P, 2 * KD, D])
        edge_w = sb("edge_w", [P, KD, A])
        layer_b = sb("layer_b", [P, L, KD])
        layer_g = sb("layer_g", [P, L, KD])
        layer_s = sb("layer_s", [P, L, KD])
        chunk_end = sem("chunk_end")
        row0_a = sem("row0_a")
        row0_v = sem("row0_v")
        row0_stored = [sem(f"row0_stored{i}") for i in range(4)]
        params_in = sem("params_in")
        edge_w_zero = sem("edge_w_zero")

        plan_v = sem("plan_v")

        def in_fours(engine, body):
            def four(v):
                for s in range(4):
                    body(v * 4 + s, s, 4, v)

            loop(engine, NT // 16, four)
            body(NT // 4, 0, 1, NT // 16)

        with nc.Block() as block:
            @block.sync
            def _(sp):
                with nc.allow_non_contiguous_dma(reason="a few hundred parameters"):
                    sp.dma_start(layer_b[:], mlp_b.rearrange("l (k p) -> p l k", p=P)).then_inc(params_in, 16)
                    sp.dma_start(layer_g[:], bn_g.rearrange("l (k p) -> p l k", p=P)).then_inc(params_in, 16)
                    sp.dma_start(layer_s[:], bn_b.rearrange("l (k p) -> p l k", p=P)).then_inc(params_in, 16)

                def store(i, s, nt, v):
                    sp.wait_ge(row0_v, i + 1)
                    sp.wait_ge(row0_a, i + 1)
                    gated(sp)
                    sp.dma_start(rows0[nodes(i * 4, nt), :].rearrange("(t p) d -> p t d", p=P),
                                 row0_out[:, s, 0:nt, 0:W0]).then_inc(row0_stored[s], 16)

                in_fours(sp, store)
                sp.wait_ge(params_in, 48)
                for s in range(4):
                    sp.wait_ge(row0_stored[s], 16 * (NT // 16 + (s == 0)))

            @block.vector
            def _(dve):
                n = [0]

                def link(ins):
                    n[0] += 1
                    ins.then_inc(plan_v, 1)
                    dve.wait_ge(plan_v, n[0])

                def scale(i, s, nt, v):
                    wait_past(dve, row0_stored[s], v * 16)
                    for u in range(2, nt):
                        dve.tensor_scalar(row0_out[:, s, u, 0:D], tile(resid, i * 4 + u),
                                          row0_scale[:, ds(i * 4 + u, 1)], row0_shift[:, ds(i * 4 + u, 1)],
                                          ALU.mult, ALU.add)
                    dve.tensor_copy(row0_out[:, s, 0:nt, D:W0], dinv[:, ds(i * 4, nt)].unsqueeze(2))\
                        .then_inc(row0_v, 1)

                in_fours(dve, scale)
                dve.memset(edge_w[:], 0.0).then_inc(edge_w_zero, 1)
                for i in range(2 * CB, len(TURNS)):
                    place_edges(dve, i)
                dve.wait_ge(reduce_out, 1)
                dve.tensor_scalar(first_c, bounds_all[:, 0:NT], -1.0, float(COLS), ALU.mult, ALU.add)
                dve.tensor_scalar(last_c, bounds_all[:, NT:2 * NT], -1.0, 0.0, ALU.add, ALU.max)
                link(dve.tensor_scalar(some, bounds_all[:, 0:NT], 0.0, None, ALU.is_gt))
                dve.tensor_copy(last_i, last_c)
                link(dve.tensor_tensor(first_i, first_c, some, ALU.mult))
                shift = K.bit_length() - 1
                dve.tensor_scalar(last_i, last_i, shift, None, ALU.arith_shift_right)
                link(dve.tensor_scalar(first_i, first_i, shift, None, ALU.arith_shift_right))
                dve.tensor_copy(last_g, last_i)
                link(dve.tensor_copy(first_g, first_i))
                link(dve.tensor_tensor(wide, last_g, first_g, ALU.subtract))
                link(dve.tensor_scalar(wide, wide, float(MINS + 1), None, ALU.is_ge))
                dve.memset(shares, 0.0)
                link(dve.tensor_tensor(start_g[:, 0:NT - 1], first_g[:, 1:NT], last_g[:, 0:NT - 1], ALU.is_equal))
                link(dve.tensor_tensor(shares[:, 0:NT - 1], start_g[:, 0:NT - 1], wide[:, 0:NT - 1], ALU.mult))
                dve.tensor_tensor(start_g[:, 1:NT], first_g[:, 1:NT], shares[:, 0:NT - 1], ALU.add)
                link(dve.tensor_copy(start_g[:, 0:1], first_g[:, 0:1]))
                dve.tensor_tensor(base_2, base_2, shares, ALU.mult)
                link(dve.tensor_scalar(before_last, start_g, float(MINS), None, ALU.add))
                dve.tensor_scalar(neg_base_2[:], base_2, float(FAR), None, ALU.add)
                link(dve.tensor_tensor(end_g, before_last, last_g, ALU.max))
                link(dve.tensor_tensor(before_last, end_g, start_g, ALU.subtract))
                link(dve.tensor_reduce(total[:, 0:1], before_last, AX_X, ALU.add))
                link(dve.tensor_scalar(total[:, 1:2], total[:, 0:1], -1.0, float(-NT), ALU.mult, ALU.add))
                link(dve.tensor_copy(total_i[:, 0:1], total[:, 1:2]))
                link(dve.tensor_scalar(total_i[:, 1:2], total_i[:, 0:1], GG - 1, None, ALU.bitwise_and))
                link(dve.tensor_copy(total[:, 2:3], total_i[:, 1:2]))
                link(dve.tensor_tensor(before_last[:, NT - 1:NT], before_last[:, NT - 1:NT], total[:, 2:3], ALU.add))
                dve.tensor_copy(plan_groups, before_last[0:1, :])
                link(dve.tensor_tensor(total[:, 3:4], total[:, 2:3], total[:, 1:2], ALU.subtract))
                dve.tensor_scalar(plan_total, total[0:1, 3:4], 1.0 / GG, None, ALU.mult)
                dve.tensor_scalar(plan_first, start_g[0:1, :], float(K), None, ALU.mult)

            @block.scalar
            def _(act):
                def scale(i, s, nt, v):
                    wait_past(act, row0_stored[s], v * 16)
                    if not isinstance(v, int):
                        gated(act)
                    for u in range(min(nt, 2)):
                        last = act.activation(row0_out[:, s, u, 0:D], tile(resid, i * 4 + u), ACT.Identity,
                                              bias=row0_shift[:, ds(i * 4 + u, 1)],
                                              scale=row0_scale[:, ds(i * 4 + u, 1)])
                    last.then_inc(row0_a, 1)

                in_fours(act, scale)

            @block.tensor
            def _(pe):
                for i in range(2 * CB, len(TURNS)):
                    turn_edges(pe, i)


        room = [0]

        def graph(n):
            room[0] += n
            assert room[0] <= 3 * SET
            return sets[:, room[0] - n:room[0]]

        got = graph(K * 264).rearrange("p (j d) -> p j d", j=K)
        hot = graph(K * P).rearrange("p (j n) -> p j n", j=K)
        hot_2 = graph(K * P).rearrange("p (j n) -> p j n", j=K)
        index = sb("index", [P, K], I32)
        summed = sb("summed", [P, D + 1 + A])
        edge_sum = sb("edge_sum", [P, NT, A])
        summed_t = sb("summed_t", [P, KD, P])
        edge_sum_t = sb("edge_sum_t", [A, P])
        edge_mix = sb("edge_mix", [A, D])
        bn_rec = graph(KD * NT * 6).rearrange("p (k t s) -> p k t s", k=KD, s=6)
        bn_mv = sb("bn_mv", [P, KD, 2])
        bn_var = sb("bn_var", [P, KD])
        bn_std = sb("bn_std", [P, KD])
        bn_inv = sb("bn_inv", [P, KD])
        bn_scale = sb("bn_scale", [P, KD])
        bn_prod = sb("bn_prod", [P, KD])
        bn_shift = sb("bn_shift", [P, KD])
        new_rows = graph(4 * 4 * D).rearrange("p (s t d) -> p s t d", s=4, t=4)
        BT = 4
        NB = NT // BT + 1
        NPAIR = NT // 2 + 1

        WA = W0 + A

        layer_in = sem("layer_in")
        mix_ready = sem("mix_ready")
        mix_made = sem("mix_made")
        index_ready = sem("index_ready")
        gathered = [sem(f"gathered{j}") for j in range(K)]
        hot_in = sem("hot_in")
        chunk_done = sem("chunk_done")
        sum_done = sem("sum_done")
        sum_taken = sem("sum_taken")
        sum_turned = sem("sum_turned")
        sum_placed = sem("sum_placed")
        mixed = sem("mixed")
        mixed_taken = sem("mixed_taken")
        attr_kept = sem("attr_kept")
        stats_v = sem("stats_v")
        var_ready = sem("var_ready")
        std_ready = sem("std_ready")
        stats2_v = sem("stats2_v")
        coeffs = sem("coeffs")
        coeffs2 = sem("coeffs2")
        applied = sem("applied")
        row_turned = sem("row_turned")
        row_taken = sem("row_taken")
        rows_stored = [sem(f"rows_stored{i}") for i in range(4)]

        def in_layers(engine, body):
            body(0, True, False)
            with engine.Fori(1, L - 1) as l:
                body(l, False, False)
            body(L - 1, False, True)

        def in_blocks(engine, body):
            def four(v):
                for s in range(4):
                    body(v * 4 + s, s, BT, v)

            loop(engine, NB // 4, four)
            body(NB - 1, 0, 1, NB // 4)

        def counter(engine, name):
            r = engine.alloc_register(name)
            engine.reg_mov(r, 0)
            return r

        MAX_ALL = L * NT * MAXG

        with nc.Block() as block:
            @block.sync
            def _(sp):
                def load(l):
                    with nc.allow_non_contiguous_dma(reason="the edge weights by features: 4 columns"):
                        sp.dma_start(mix_w[:], mlp_w[ds(l, 1), :, :].rearrange("a (k p) n -> p (a k) n", p=P))\
                            .then_inc(layer_in, 16)
                        sp.dma_start(edge_w[:, 0, A - 1:A], ew1[ds(l, 1), :, :].rearrange("a b p -> p (a b)"))\
                            .then_inc(layer_in, 16)
                        sp.dma_start(edge_w[:, 1, 0:A - 1], ew2[ds(l, 1), :, :].rearrange("a j p -> p (a j)"))\
                            .then_inc(layer_in, 16)
                def layer(l, first, final):
                    if final:
                        return
                    sp.wait_ge(mixed, (l + 1) * NT + 1)
                    gated(sp)
                    load(l + 1)

                    def store(i, s, nt, v):
                        sp.wait_ge(row_taken, l * NPAIR + i * (BT // 2) + (nt + 1) // 2 + 4)
                        gated(sp)
                        sp.dma_start(rows[nodes(i * BT, nt), :].rearrange("(t p) d -> p t d", p=P),
                                     new_rows[:, s, 0:nt, :]).then_inc(rows_stored[s], 16)

                    in_blocks(sp, store)

                load(0)
                in_layers(sp, layer)

            @block.gpsimd
            def _(pool):
                g = counter(pool, "pool_group")
                steps = pool.value_load(plan_total, min_val=1, max_val=NT * MAXG)

                def layer(l, first, final):
                    if not first:
                        for s in range(4):
                            pool.wait_ge(rows_stored[s], l * (16 * (NB // 4 + (s == 0))))
                        gated(pool)
                    width = W0 if first else D
                    with pool.Fori(0, steps):
                        for u in range(GG):
                            now = pool.snap(g, min_val=0, max_val=MAX_ALL)
                            for j in range(K):
                                pool.wait_ge(index_ready, now * K + j + 1)
                                gated(pool)
                                pool.indirect_dma_start(
                                    got[:, j, 0:width], None, rows0 if first else rows,
                                    bass.IndirectOffsetOnAxis(ap=index[:, j:j + 1], axis=0)).then_inc(gathered[j], 16)
                            pool.reg_add(g, g, 1)

                in_layers(pool, layer)

            @block.scalar
            def _(act):
                g = counter(act, "act_group")
                col = counter(act, "act_column")

                def indices():
                    now = act.snap(g, min_val=0, max_val=MAX_ALL)
                    c = act.snap(col, min_val=0, max_val=COLS - K)
                    for j in range(K):
                        act.wait_ge(chunk_done, now * K + j + 1)
                        act.activation(index[:, j:j + 1], src_col[:, ds(c + j, 1)], ACT.Copy).then_inc(index_ready, 1)
                    act.reg_add(g, g, 1)
                    act.reg_add(col, col, K)

                def layer(l, first, final):
                    width = W0 + A if first else D

                    def take(t):
                        q = l * NT + t
                        act.wait_ge(sum_done, q + 1)
                        act.wait_ge(sum_turned, q + 1)
                        act.activation(summed[:, 0:width], tile(bank, t % 2)[:, 0:width], ACT.Copy,
                                       scale=dinv[:, ds(t, 1)]).then_inc(sum_taken, 1)
                        if first:
                            act.wait_ge(sum_taken, q + 3)
                            act.activation(tile(edge_sum, t), summed[:, W0:WA], ACT.Copy).then_inc(attr_kept, 1)
                        else:
                            act.activation(summed[:, W0:WA], tile(edge_sum, t), ACT.Copy).then_inc(attr_kept, 1)

                    def relu(t):
                        act.wait_ge(mixed, l * NT + t + 2)
                        gated(act)
                        for k in range(KD):
                            last = act.activation(feat_t[:, k, nodes(t)], bank[:, 3, k * P:(k + 1) * P], ACT.Relu,
                                                  bias=layer_b[:, ds(l, 1), k])
                        last.then_inc(mixed_taken, 1)

                    def start(t):
                        c = act.value_load(plan_first[:, ds(t, 1)], min_val=0, max_val=COLS)
                        act.reg_mov(col, c)
                        return act.value_load(plan_groups[:, ds(t, 1)], min_val=MINS, max_val=MAXG)

                    def tile_steps(t, past):
                        n = start(t)
                        with act.Fori(0, n):
                            indices()
                        if past >= 2:
                            relu(t - 2)
                        if past >= 1:
                            take(t - 1)
                        indices()

                    tile_steps(0, 0)
                    act.wait_ge(mix_ready, l + 1)
                    act.activation(edge_mix[:], bank[0:A, 4, 0:D], ACT.Copy).then_inc(mix_made, 1)
                    tile_steps(1, 1)
                    with act.Fori(2, NT) as t:
                        tile_steps(t, 2)
                    relu(NT - 2)
                    take(NT - 1)
                    relu(NT - 1)
                    act.wait_ge(var_ready, l + 1)
                    act.activation(bn_std[:], bn_var[:], ACT.Sqrt).then_inc(std_ready, 1)
                    act.wait_ge(coeffs, l + 1)

                    def apply(i, s, nt, v):
                        for k in range(KD):
                            span = feat_t[:, k, nodes(i * BT, nt)]
                            last = act.activation(span, span, ACT.Identity if final else ACT.Relu,
                                                  bias=bn_shift[:, k:k + 1], scale=bn_scale[:, k:k + 1])
                        last.then_inc(applied, 1)

                    in_blocks(act, apply)

                act.sem_inc(sum_taken, 2)
                act.sem_inc(mixed_taken, 1)
                in_layers(act, layer)

            @block.vector
            def _(dve):
                g = counter(dve, "dve_group")
                col = counter(dve, "dve_column")
                CHAIN = 4

                def layer(l, first, final):
                    def hots(t, shared):
                        now = dve.snap(g, min_val=0, max_val=MAX_ALL)
                        c = dve.snap(col, min_val=0, max_val=COLS - K)
                        for j in range(K):
                            dve.wait_ge(chunk_done, now * K + j + 1)
                            ins = dve.tensor_scalar(hot[:, j, :], iota_row[:], dst_col[:, ds(c + j, 1)],
                                                    neg_base[:, ds(t, 1)], ALU.subtract, ALU.is_equal)
                            if shared:
                                ins = dve.tensor_scalar(hot_2[:, j, :], iota_row[:], dst_col[:, ds(c + j, 1)],
                                                        neg_base_2[:, ds(t, 1)], ALU.subtract, ALU.is_equal)
                            if first:
                                dve.wait_ge(gathered[j], now * 16 + 16)
                                ins = dve.tensor_scalar(got[:, j, W0:WA], tile(attr_col, c + j),
                                                        got[:, j, D:W0], None, ALU.mult)
                            ins.then_inc(hot_in, 1)
                        dve.reg_add(g, g, 1)
                        dve.reg_add(col, col, K)

                    def place(t):
                        q = l * NT + t
                        dve.wait_ge(sum_turned, q + 2)
                        dve.wait_ge(mixed, q + 1)
                        dve.tensor_copy(summed_t[:], bank[:, 2, 0:D].rearrange("p (k n) -> p k n", k=KD))
                        dve.tensor_copy(edge_sum_t[:], bank[0:A, 2, D:D + P]).then_inc(sum_placed, 1)

                    def stats(t, n):
                        dve.wait_ge(mixed_taken, l * NT + t + 2)
                        for k in range(KD):
                            last = dve.bn_stats(bn_rec[:, k, ds(t, 1), :].rearrange("p a s -> p (a s)"),
                                                feat_t[:, k, ds(t * P, n)])
                        return last

                    def start(t):
                        c = dve.value_load(plan_first[:, ds(t, 1)], min_val=0, max_val=COLS)
                        dve.reg_mov(col, c)
                        return dve.value_load(plan_groups[:, ds(t, 1)], min_val=MINS, max_val=MAXG)

                    def tile_steps(t, past):
                        n = start(t)
                        with dve.Fori(0, n):
                            hots(t, False)
                        hots(t, True)
                        if past >= 1:
                            place(t - 1)
                        if past >= 2:
                            stats(t - 2, P)

                    tile_steps(0, 0)
                    tile_steps(1, 1)
                    with dve.Fori(2, NT) as t:
                        tile_steps(t, 2)
                    place(NT - 1)
                    stats(NT - 2, P)
                    links = [0]

                    def link(ins):
                        links[0] += 1
                        ins.then_inc(stats_v, 1)
                        dve.wait_ge(stats_v, l * CHAIN + links[0])

                    link(stats(NT - 1, LAST))
                    gated(dve)
                    for k in range(KD):
                        last = dve.bn_aggr(bn_mv[:, k, :], bn_rec[:, k, :, :].rearrange("p t s -> p (t s)"))
                    link(last)
                    dve.tensor_scalar(bn_var[:], bn_mv[:, :, 1], EPS, None, ALU.add).then_inc(var_ready, 1)
                    dve.wait_ge(std_ready, l + 1)
                    link(dve.reciprocal(bn_inv[:], bn_std[:]))
                    link(dve.tensor_tensor(bn_scale[:], bn_inv[:], tile(layer_g, l), ALU.mult))
                    assert links[0] == CHAIN
                    dve.tensor_tensor(bn_prod[:], bn_mv[:, :, 0], bn_scale[:], ALU.mult).then_inc(coeffs2, 1)
                    dve.wait_ge(coeffs2, l + 1)
                    dve.tensor_tensor(bn_shift[:], tile(layer_s, l), bn_prod[:], ALU.subtract).then_inc(coeffs, 1)

                    def take(i, s, nt, v):
                        if not final:
                            wait_past(dve, rows_stored[s], l * (16 * (NB // 4 + (s == 0))) + v * 16)
                        for u in range(0, nt, 2):
                            t = i * BT + u
                            w = min(2, nt - u)
                            dve.wait_ge(row_turned, l * NPAIR + i * (BT // 2) + u // 2 + 1)
                            turned_rows = bank[:, 4 + (2 * s + u // 2) % 4, 0:w * D].rearrange("p (t d) -> p t d", t=w)
                            if final:
                                here = resid[:, ds(t, w), :]
                                dve.tensor_tensor(here, turned_rows, here, ALU.add).then_inc(row_taken, 1)
                                dve.wait_ge(row_taken, l * NPAIR + i * (BT // 2) + u // 2 + 5)
                                for v2 in range(w):
                                    dve.bn_stats(tile(ln_stats, t + v2), tile(resid, t + v2)).then_inc(stats2_v, 1)
                            else:
                                dve.tensor_tensor(new_rows[:, s, u:u + w, :], turned_rows,
                                                  dinv[:, ds(t, w)].unsqueeze(2).to_broadcast([P, w, D]), ALU.mult)\
                                    .then_inc(row_taken, 1)

                    in_blocks(dve, take)

                dve.sem_inc(row_taken, 4)
                dve.sem_inc(sum_placed, 1)
                in_layers(dve, layer)

            @block.tensor
            def _(pe):
                g = counter(pe, "pe_group")

                def layer(l, first, final):
                    width = W0 + A if first else D

                    def into(t):
                        return tile(bank, t % 2)[:, 0:width]

                    def sums(t, last=False, more=()):
                        now = pe.snap(g, min_val=0, max_val=MAX_ALL)
                        if last:
                            pe.wait_ge(sum_taken, l * NT + t + 2)
                        for j in range(K):
                            pe.wait_ge(gathered[j], now * 16 + 16)
                            pe.wait_ge(hot_in, now * K + j + 1)
                            mm = pe.matmul(into(t), hot[:, j, :], got[:, j, 0:width], start=False,
                                           stop=last and j == K - 1)
                            if last and j == K - 1:
                                mm.then_inc(sum_done, 1)
                            if last:
                                mm = pe.matmul(into(t + 1), hot_2[:, j, :], got[:, j, 0:width], start=j == 0,
                                               stop=False)
                            mm.then_inc(chunk_done, 1)
                            if j in more:
                                more[j]()
                        pe.reg_add(g, g, 1)

                    def turn(t):
                        q = l * NT + t
                        pe.wait_ge(attr_kept, q + 1)
                        pe.wait_ge(sum_taken, q + 3)
                        pe.wait_ge(sum_placed, q + 1)
                        for k in range(KD):
                            pe.transpose(bank[:, 2, k * P:(k + 1) * P], summed[:, k * P:(k + 1) * P], ident[:])
                        pe.transpose(bank[0:A, 2, D:D + P], summed[:, W0:WA], ident[:]).then_inc(sum_turned, 1)

                    def mix(t, f):
                        q = l * NT + t
                        if f == 0:
                            pe.wait_ge(sum_placed, q + 2)
                            pe.wait_ge(mixed_taken, q + 1)
                        o = bank[:, 3, f * P:(f + 1) * P]
                        c = slice(f * P, (f + 1) * P)
                        for k in range(KD):
                            pe.matmul(o, mix_w[:, k, c], feat_t[:, k, nodes(t)], start=k == 0, stop=False)
                        for k in range(KD):
                            pe.matmul(o, mix_w[:, KD + k, c], summed_t[:, k, :], start=False, stop=False)
                        mm = pe.matmul(o, edge_mix[:, c], edge_sum_t[:], start=False, stop=True)
                        if f == KD - 1:
                            mm.then_inc(mixed, 1)

                    pe.wait_ge(layer_in, (l + 1) * 48)
                    if not first:
                        pe.wait_ge(applied, l * NB)
                    pe.wait_ge(row_taken, l * NPAIR + 4)
                    for k in range(KD):
                        mm = pe.matmul(bank[0:A, 4, 0:D], edge_w[:, k, :], mix_w[:, KD + k, :],
                                       start=k == 0, stop=k == KD - 1)
                    mm.then_inc(mix_ready, 1)

                    def tile_steps(t, past):
                        n = pe.value_load(plan_groups[:, ds(t, 1)], min_val=MINS, max_val=MAXG)
                        with pe.Fori(0, n):
                            sums(t)
                        sums(t, True, {0: lambda: turn(t - 1), 2: lambda: mix(t - 1, 0), 4: lambda: mix(t - 1, 1)}
                             if past else ())

                    pe.matmul(into(0), zero[:, 0:P], zero[:, 0:width], start=True, stop=False)
                    tile_steps(0, 0)
                    pe.wait_ge(mix_made, l + 1)
                    gated(pe)
                    with pe.Fori(1, NT) as t:
                        tile_steps(t, 1)
                    pe.matmul(into(NT), zero[:, 0:P], zero[:, 0:width], start=False, stop=True).then_inc(chunk_end, 1)
                    turn(NT - 1)
                    mix(NT - 1, 0)
                    mix(NT - 1, 1)

                    for i in range(NB):
                        pe.wait_ge(applied, l * NB + i + 1)
                        for t in range(i * BT, min(i * BT + BT, NT), 2):
                            pe.wait_ge(row_taken, l * NPAIR + t // 2 + 1)
                            for u in range(min(2, NT - t)):
                                for k in range(KD):
                                    mm = pe.transpose(bank[:, 4 + t // 2 % 4, ds(u * D + k * P, P)],
                                                      feat_t[:, k, (t + u) * P:(t + u + 1) * P], ident[:])
                            mm.then_inc(row_turned, 1)

                pe.sem_inc(chunk_done, K)
                pe.sem_inc(sum_turned, 1)
                pe.sem_inc(mixed, 1)
                in_layers(pe, layer)


        route_w = sb("route_w", [P, KD, X])
        bias1 = sb("bias1", [P, (X + 1) * KF])
        slot_of = sb("slot_of", [P, NT, 2], I32)
        weight_of = sb("weight_of", [P, NT, 2])
        plan_x = sb("plan_x", [1, 2 * X + 1], I32)

        second_norm = Norm("norm2", 0)
        var2_ready = sem("var2_ready")
        std2_ready = sem("std2_ready")
        logits_ready = sem("logits_ready")
        logits_taken = sem("logits_taken")
        logits_done = sem("logits_done")
        route_w_in = sem("route_w_in")
        bias1_in = sem("bias1_in")
        bias1_turned = sem("bias1_turned")
        sets_in = sem("sets_in")

        free = [0]

        def room(n):
            free[0] += n
            assert free[0] <= arena.shape[1]
            return arena[:, free[0] - n:free[0]]

        bias1_rows = room(P)
        logits_t = room(NT * P)[0:X, :]

        def load_set(engine, s, w1, w2, done):
            engine.dma_start(w1_set(s), w1).then_inc(done, 16)
            engine.dma_start(w2_set(s), w2).then_inc(done, 16)

        with nc.Block() as block:
            @block.sync
            def _(sp):
                sp.dma_start(route_w[:], wr.rearrange("(k p) e -> p k e", p=P)).then_inc(route_w_in, 16)
                sp.dma_start(bias1_rows[0:X * KF, :], b1p.rearrange("x (c p) -> (x c) p", p=P)).then_inc(bias1_in, 16)
                sp.dma_start(bias1_rows[X * KF:(X + 1) * KF, :], b1s.rearrange("(c p) -> c p", p=P))\
                    .then_inc(bias1_in, 16)
                load_set(sp, 2, w1s.rearrange("(k p) f -> p k f", p=P), w2s.rearrange("(c p) d -> p c d", p=P), sets_in)
                for e in range(2):
                    load_set(sp, e, w1p[e].rearrange("(k p) f -> p k f", p=P),
                             w2p[e].rearrange("(c p) d -> p c d", p=P), sets_in)
                sp.wait_ge(sets_in, 96)

            @block.vector
            def _(dve):
                dve.wait_ge(stats2_v, NT)
                for t in range(NT):
                    last = dve.bn_aggr(ln_mv[:, t, :], ln_stats[:, t, :])
                last.then_inc(stats2_v, 1)
                dve.wait_ge(stats2_v, NT + 1)
                dve.tensor_scalar(ln_std[:], ln_mv[:, :, 1], EPS, None, ALU.add).then_inc(var2_ready, 1)
                dve.wait_ge(std2_ready, 1)
                dve.reciprocal(ln_rstd[:], ln_std[:]).then_inc(stats2_v, 1)
                dve.wait_ge(stats2_v, NT + 2)
                dve.scalar_tensor_tensor(ln_shift[:], ln_mv[:, :, 0], -1.0, ln_rstd[:], ALU.mult, ALU.mult)\
                    .then_inc(ln_ready, 1)
                dve.sem_inc(second_norm.placed, 2)

                def take_logits(i, s, nt):
                    dve.wait_ge(logits_ready, i + 1)
                    gated(dve)
                    dve.tensor_copy(logits_t[:, nodes(i * 4, nt)], bank[0:X, 3 + s % 2, 0:nt * P])\
                        .then_inc(logits_taken, 1)

                def place(i, s, nt, v):
                    for u in range(nt):
                        second_norm.place(dve, i * 4 + u, u % 2)
                    if not isinstance(i, int) or i > 0:
                        take_logits(i - 1, s + 1, 4)

                in_fours(dve, place)
                take_logits(NT // 4, 0, 1)
                dve.wait_ge(bias1_turned, 1)
                dve.tensor_copy(bias1[:], bank[:, 2, 0:(X + 1) * KF])

            @block.scalar
            def _(act):
                act.wait_ge(var2_ready, 1)
                act.activation(ln_std[:], ln_std[:], ACT.Sqrt).then_inc(std2_ready, 1)
                act.wait_ge(ln_ready, 2)
                tile_pairs(act, lambda t, s: second_norm.normalise(act, t, s))

            @block.tensor
            def _(pe):
                pe.wait_ge(bias1_in, 32)
                pe.transpose(bank[:, 2, 0:(X + 1) * KF], bias1_rows[0:(X + 1) * KF, :],
                             ident[0:(X + 1) * KF, 0:(X + 1) * KF]).then_inc(bias1_turned, 1)
                pe.wait_ge(route_w_in, 16)
                pe.sem_inc(second_norm.turned, 2)
                LAG = 2

                def logits(i):
                    nt = min(4, NT - i * 4)
                    pe.wait_ge(second_norm.placed, i * 4 + nt + 2)
                    if i >= 2:
                        pe.wait_ge(logits_taken, i - 1)
                    for k in range(KD):
                        mm = pe.matmul(bank[0:X, 3 + i % 2, 0:nt * P], route_w[:, k, :],
                                       feat_t[:, k, i * 4 * P:(i * 4 + nt) * P], start=k == 0, stop=k == KD - 1)
                    mm.then_inc(logits_ready, 1)

                def turn_logits(i):
                    pe.wait_ge(logits_taken, i + 1)
                    for t in range(i * 4, min(i * 4 + 4, NT)):
                        mm = pe.transpose(bank[:, 7, t * X:(t + 1) * X], logits_t[:, t * P:(t + 1) * P],
                                          ident[0:X, 0:X])
                    return mm

                for t in range(NT):
                    second_norm.turn(pe, t, t % 2)
                    i = (t - LAG) // 4
                    if t >= LAG and (t - LAG) % 4 == 3:
                        logits(i)
                        if i >= 1:
                            turn_logits(i - 1)
                done = (NT - 1 - LAG + 1) // 4
                for i in range(done, NT // 4 + 1):
                    logits(i)
                for i in range(done - 1, NT // 4 + 1):
                    mm = turn_logits(i)
                mm.then_inc(logits_done, 1)

        free[0] = 0

        def per_expert():
            return room(NT * X).rearrange("p (t e) -> p t e", e=X)

        def over_experts(v):
            return v.unsqueeze(2).to_broadcast([P, NT, X])

        logit, prob, prob2, score, pick1, pick2, place_all, until = (per_expert() for _ in range(8))
        top1, top2, most, total_p, real, node_no = (room(NT) for _ in range(6))
        order = room(X)
        region = room(X)
        counts = room(X)
        counts_up = room(X)
        counts_i = room(X).bitcast(I32)
        blocks_i = room(X).bitcast(I32)
        blocks_f = room(X)
        picks_b = room(NT * X // 2).bitcast(BF16)
        before = room(P // 2).bitcast(BF16)
        ones_b = room(P // 2).bitcast(BF16)

        route_c = sem("route_c")
        route_v = sem("route_v")
        shifted = sem("shifted")
        powers = sem("powers")
        picked = sem("picked")
        ranked = sem("ranked")

        with nc.Block() as block:
            @block.gpsimd
            def _(pool):
                imp = dict(allow_small_or_imprecise_dtypes=True)
                pool.iota(order, [[-1, X]], X, 0, **imp).then_inc(route_c, 1)
                pool.iota(node_no, [[P, NT]], 0, 1, **imp).then_inc(route_c, 1)
                pool.memset(ones_b, 1.0).then_inc(route_c, 1)
                pool.wait_ge(route_c, 3)
                pool.affine_select(out=before, in_=ones_b, compare_op=ALU.is_gt, fill=0.0, base=0,
                                   pattern=[[1, P]], channel_multiplier=-1).then_inc(route_c, 1)

            @block.scalar
            def _(act):
                act.wait_ge(shifted, 1)
                act.activation(prob, prob2, ACT.Exp).then_inc(powers, 1)

            @block.tensor
            def _(pe):
                pe.wait_ge(picked, 1)
                pe.wait_ge(route_c, 4)
                pe.matmul(bank[:, 5, 0:NT * X], before, picks_b, start=True, stop=True)
                pe.matmul(bank[:, 6, 0:NT * X], ones_b, picks_b, start=True, stop=True).then_inc(ranked, 1)

            @block.vector
            def _(dve):
                n = [0]

                def link(ins):
                    n[0] += 1
                    ins.then_inc(route_v, 1)
                    dve.wait_ge(route_v, n[0])

                dve.wait_ge(route_c, 4)
                link(dve.tensor_copy(logit, bank[:, 7, 0:NT * X].rearrange("p (t e) -> p t e", e=X)))
                link(dve.tensor_reduce(most, logit, AX_X, ALU.max))
                dve.tensor_tensor(prob2, logit, over_experts(most), ALU.subtract).then_inc(shifted, 1)
                dve.tensor_scalar(real, node_no, float(N), None, ALU.is_lt)
                dve.wait_ge(powers, 1)
                link(dve.tensor_reduce(total_p, prob, AX_X, ALU.add))
                link(dve.reciprocal(most, total_p))
                link(dve.tensor_tensor(prob, prob, over_experts(most), ALU.mult))

                def pick(probs, top, into):
                    link(dve.tensor_reduce(top, probs, AX_X, ALU.max))
                    link(dve.tensor_tensor(score, probs, over_experts(top), ALU.is_equal))
                    link(dve.tensor_tensor(score, score, order.unsqueeze(1).to_broadcast([P, NT, X]), ALU.mult))
                    link(dve.tensor_reduce(most, score, AX_X, ALU.max))
                    link(dve.tensor_tensor(into, score, over_experts(most), ALU.is_equal))

                pick(prob, top1, pick1)
                link(dve.scalar_tensor_tensor(prob2, pick1, -2.0, prob, ALU.mult, ALU.add))
                pick(prob2, top2, pick2)
                link(dve.tensor_tensor(total_p, top1, top2, ALU.add))
                link(dve.reciprocal(most, total_p))
                dve.tensor_tensor(weight_of[:, :, 0], top1, most, ALU.mult)
                dve.tensor_tensor(weight_of[:, :, 1], top2, most, ALU.mult)
                dve.tensor_tensor(pick1, pick1, over_experts(real), ALU.mult)
                link(dve.tensor_tensor(pick2, pick2, over_experts(real), ALU.mult))
                dve.tensor_tensor(picks_b.rearrange("p (t e) -> p t e", e=X), pick1, pick2, ALU.add)\
                    .then_inc(picked, 1)
                dve.wait_ge(ranked, 1)
                link(dve.tensor_copy(score, bank[:, 6, 0:NT * X].rearrange("p (t e) -> p t e", e=X)))
                dve.memset(top1, 1.0).then_inc(route_v, 1)
                n[0] += 1
                dve.wait_ge(route_v, n[0])
                for e in range(X):
                    last = dve.tensor_tensor_scan(until[:, :, e], top1, score[:, :, e], 0.0, ALU.mult, ALU.add)
                link(last)
                link(dve.tensor_tensor(place_all, until, score, ALU.subtract))
                link(dve.tensor_scalar(counts_up, until[:, NT - 1, :], float(TOK - 1), None, ALU.add))
                link(dve.tensor_copy(counts_i, counts_up))
                link(dve.tensor_scalar(blocks_i, counts_i, TOK.bit_length() - 1, None, ALU.arith_shift_right))
                link(dve.tensor_copy(blocks_f, blocks_i))
                link(dve.tensor_scalar(counts, blocks_f, 1.0, None, ALU.max))
                dve.tensor_copy(plan_x[:, X:2 * X], counts[0:1, :])
                link(dve.tensor_tensor_scan(blocks_f, top1[:, 0:X], counts, 0.0, ALU.mult, ALU.add))
                dve.tensor_scalar(plan_x[:, 2 * X:2 * X + 1], blocks_f[0:1, X - 1:X], float(TOK), None, ALU.mult)
                link(dve.tensor_tensor(counts_up, blocks_f, counts, ALU.subtract))
                link(dve.tensor_scalar(region, counts_up, float(TOK), None, ALU.mult))
                link(dve.tensor_tensor(counts, region, until[:, NT - 1, :], ALU.add))
                dve.tensor_copy(plan_x[:, 0:X], counts[0:1, :])
                link(dve.tensor_tensor(place_all, place_all, region.unsqueeze(1).to_broadcast([P, NT, X]), ALU.add))
                link(dve.tensor_tensor(place_all, place_all,
                                       bank[:, 5, 0:NT * X].rearrange("p (t e) -> p t e", e=X), ALU.add))
                dve.tensor_tensor(prob, place_all, pick1, ALU.mult)
                link(dve.tensor_tensor(prob2, place_all, pick2, ALU.mult))
                dve.tensor_reduce(top1, prob, AX_X, ALU.add)
                link(dve.tensor_reduce(top2, prob2, AX_X, ALU.add))
                dve.tensor_copy(slot_of[:, :, 0], top1)
                dve.tensor_copy(slot_of[:, :, 1], top2)


        free[0] = 0
        hidden = room(KF * TOK).rearrange("p (c n) -> p c n", c=KF)
        bias2 = room((X + 1) * D).rearrange("p (x d) -> p x d", d=D)
        block_in = room(TB * D).rearrange("p (u d) -> p u d", u=TB)
        block_out = room(TB * D).rearrange("p (u d) -> p u d", u=TB)
        block_t = normed
        send = row_out[:, 0, :, :]
        fetched = row_out
        send_at = sb("send_at", [P, 4, 2], I32)
        turned_rows = mix_w[:, :, :].rearrange("p (s k) n -> p s k n", s=2)

        bias2_in = sem("bias2_in")
        tail_zero = sem("tail_zero")
        tails_in = sem("tails_in")
        results_zero = sem("results_zero")

        def block_rows_of(ap, b):
            return ap[ds(b * TOK, TOK), :].rearrange("(u p) d -> p u d", p=P)

        send_ready = sem("send_ready")
        sent = [sem(f"sent{u}") for u in range(4)]
        bias_added = sem("bias_added")

        class Expert:

            def __init__(self, name):
                self.up_done = sem(name + "_up_done")
                self.hidden_ready = sem(name + "_hidden_ready")
                self.down_done = sem(name + "_down_done")
                self.sums_taken = sem(name + "_sums_taken")

            def tensor(self, pe, at, s, rows_in, nt, between=None):
                w1, w2 = w1_set(s), w2_set(s)

                def up(c):
                    pe.wait_ge(self.hidden_ready, at * KF + c + 1)
                    for k in range(KD):
                        mm = pe.matmul(bank[:, c % 4, 0:nt * P], w1[:, k, c * P:(c + 1) * P], rows_in(k),
                                       start=k == 0, stop=k == KD - 1)
                    mm.then_inc(self.up_done, 1)

                def down(c):
                    pe.wait_ge(self.hidden_ready, at * KF + c + 5)
                    if c == 0:
                        pe.wait_ge(self.sums_taken, at + 1)
                    for u in range(nt):
                        mm = pe.matmul(bank[:, 4 + u, 0:D], hidden[:, c, u * P:(u + 1) * P], w2[:, c, :],
                                       start=c == 0, stop=c == KF - 1)
                    mm.then_inc(self.down_done, 1)

                up(0)
                for c in range(1, KF):
                    up(c)
                    down(c - 1)
                    if between and c == KF // 2:
                        between()
                down(KF - 1)

            def scalar(self, act, at, bias, nt):
                for c in range(KF):
                    act.wait_ge(self.up_done, at * KF + c + 1)
                    act.wait_ge(self.down_done, at * KF + c + 1)
                    act.activation(hidden[:, c, 0:nt * P], bank[:, c % 4, 0:nt * P], ACT.Gelu,
                                   bias=bias(c)).then_inc(self.hidden_ready, 1)

        shared = Expert("shared")
        NS = NT // TB
        NS1 = NS // 2
        assert NS1 == NT // 4 and NS == 2 * NS1

        def shared_bias(c):
            return bias1[:, X * KF + c:X * KF + c + 1]

        def take_shared(dve, b, nt):
            dve.wait_ge(shared.down_done, b * KF + 2 * KF)
            for u in range(nt):
                last = dve.tensor_tensor(tile(resid, b * TB + u), bank[:, 4 + u, 0:D],
                                         tile(resid, b * TB + u), ALU.add)
            last.then_inc(shared.sums_taken, 1)

        with nc.Block() as block:
            @block.sync
            def _(sp):
                sp.dma_start(bias2[:, X, :], b2s.partition_broadcast(P)).then_inc(bias2_in, 16)
                sp.dma_start(bias2[:, 0:X, :].rearrange("p x d -> p (x d)"),
                             b2p.rearrange("x d -> (x d)").partition_broadcast(P)).then_inc(bias2_in, 16)
                sp.wait_ge(tail_zero, 1)
                for e in range(X + 1):
                    at = e if e < X else 2 * X
                    n = sp.value_load(plan_x[:, at:at + 1], min_val=0, max_val=MAXB * TOK)
                    sp.dma_start(expert_in[ds(n, TOK), :].rearrange("(u p) d -> p u d", p=P), block_in)\
                        .then_inc(tails_in, 16)
                    sp.wait_ge(tails_in, 16 * (e + 1))
                with sp.Fori(0, MAXB) as b:
                    sp.dma_start(block_rows_of(expert_out, b), block_in).then_inc(results_zero, 16)
                sp.wait_ge(results_zero, 16 * MAXB)
                sp.wait_ge(bias2_in, 32)

            @block.gpsimd
            def _(pool):
                def scatter(t, u, p):
                    pool.wait_ge(send_ready, t + 1)
                    gated(pool)
                    for w in range(2):
                        pool.indirect_dma_start(expert_in, bass.IndirectOffsetOnAxis(ap=send_at[0:p, u, w:w + 1], axis=0),
                                                send[0:p, u, :], None).then_inc(sent[u], 16)

                pool.wait_ge(tails_in, 16 * (X + 1))
                with pool.Fori(0, NT // 4) as i:
                    for u in range(4):
                        scatter(i * 4 + u, u, P)
                scatter(NT - 1, 0, LAST)
                pool.wait_ge(sent[0], 32 * (NT // 4 + 1))
                for u in range(1, 4):
                    pool.wait_ge(sent[u], 32 * (NT // 4))

            @block.scalar
            def _(act):
                act.sem_inc(shared.hidden_ready, 4)
                with act.Fori(0, NS1) as b:
                    shared.scalar(act, b, shared_bias, TB)

            @block.vector
            def _(dve):
                dve.memset(block_in, 0.0).then_inc(tail_zero, 1)
                dve.wait_ge(bias2_in, 32)

                def prepare(t, u, seen):
                    wait_past(dve, sent[u], seen)
                    dve.tensor_scalar(send[:, u, :], tile(resid, t), ln_mv[:, ds(t, 1), 0], ln_rstd[:, ds(t, 1)],
                                      ALU.subtract, ALU.mult)
                    dve.tensor_copy(send_at[:, u, :], tile(slot_of, t)).then_inc(send_ready, 1)
                    dve.tensor_tensor(tile(resid, t), tile(resid, t), bias2[:, X, :], ALU.add).then_inc(bias_added, 1)

                def four(i):
                    if not isinstance(i, int):
                        take_shared(dve, i, TB)
                    for u in range(4):
                        prepare(i * 4 + u, u, i * 32)
                    dve.wait_ge(bias_added, i * 4 + 4)
                    if isinstance(i, int):
                        take_shared(dve, i, TB)

                dve.sem_inc(shared.sums_taken, 1)
                loop(dve, NT // 4, four)
                prepare(NT - 1, 0, 32 * (NT // 4))

            @block.tensor
            def _(pe):
                pe.sem_inc(shared.down_done, KF)
                with pe.Fori(0, NS1) as b:
                    shared.tensor(pe, b, 2, lambda k: feat_t[:, k, nodes(b * TB, TB)], TB)

        routed = Expert("routed")
        rows_in = sem("rows_in")
        rows_turned = sem("rows_turned")
        rows_placed = sem("rows_placed")
        out_stored = sem("out_stored")
        out_free = sem("out_free")
        expert_done = sem("expert_done")
        weights_in = [sem(f"weights_in{s}") for s in range(2)]
        set_ready = [sem(f"set_ready{s}") for s in range(2)]
        def experts(engine, name, body, before=None, after=None):
            r = counter(engine, name)
            with engine.Fori(0, X // 2) as v:
                for s in range(2):
                    e = v * 2 + s
                    if before:
                        before(e, s, v)
                    n = engine.value_load(plan_x[:, ds(e + X, 1)], min_val=1, max_val=EACH)
                    with engine.Fori(0, n):
                        at = engine.snap(r, min_val=0, max_val=MAXB - 1)
                        body(e, s, at)
                        engine.reg_add(r, r, 1)
                    if after:
                        after()
            return engine.snap(r, min_val=0, max_val=MAXB)

        with nc.Block() as block:
            @block.sync
            def _(sp):
                def load(at):
                    sp.wait_ge(rows_turned, at + 1)
                    gated(sp)
                    sp.dma_start(block_in, block_rows_of(expert_in, at)).then_inc(rows_in, 16)

                def body(e, s, at):
                    load(at + 1)
                    sp.wait_ge(routed.sums_taken, at + 2)
                    gated(sp)
                    sp.dma_start(block_rows_of(expert_out, at), block_out).then_inc(out_stored, 16)
                    sp.wait_ge(out_stored, at * 16 + 16)
                    sp.sem_inc(out_free, 1)

                sp.sem_inc(out_free, 1)
                load(0)
                at = experts(sp, "sp_blocks", body)
                sp.wait_ge(rows_in, at * 16 + 16)
                gated(sp)

            @block.gpsimd
            def _(pool):
                for s in range(2):
                    pool.sem_inc(set_ready[s], 1)
                with pool.Fori(0, X // 2 - 1) as v:
                    for s in range(2):
                        pool.wait_ge(expert_done, v * 2 + s + 1)
                        gated(pool)
                        e = v * 2 + (s + 2)
                        load_set(pool, s, w1p[ds(e, 1), :, :].rearrange("a (k p) f -> p (a k) f", p=P),
                                 w2p[ds(e, 1), :, :].rearrange("a (c p) d -> p (a c) d", p=P), weights_in[s])
                        pool.wait_ge(weights_in[s], v * 32 + 32)
                        pool.sem_inc(set_ready[s], 1)

            @block.scalar
            def _(act):
                def body(e, s, at):
                    routed.scalar(act, at, lambda c: bias1[:, ds(e * KF + c, 1)], TB)

                act.sem_inc(routed.hidden_ready, 4)
                experts(act, "act_blocks", body)

            @block.vector
            def _(dve):
                def place(at):
                    dve.wait_ge(rows_turned, at + 2)
                    dve.tensor_copy(turned_rows[:, ds(at % 2, 1), :, :].rearrange("p a k n -> p (a k) n"),
                                    bank[:, 6, :].rearrange("p (k n) -> p k n", k=KD)).then_inc(rows_placed, 1)

                def body(e, s, at):
                    place(at + 1)
                    dve.wait_ge(routed.down_done, at * KF + 2 * KF)
                    dve.wait_ge(out_free, at + 1)
                    for u in range(TB):
                        last = dve.tensor_tensor(block_out[:, u, :], bank[:, 4 + u, 0:D], tile(bias2, e), ALU.add)
                    last.then_inc(routed.sums_taken, 1)

                dve.sem_inc(rows_placed, 1)
                dve.sem_inc(routed.sums_taken, 1)
                place(0)
                experts(dve, "dve_blocks", body)

            @block.tensor
            def _(pe):
                def turn(at):
                    pe.wait_ge(rows_in, at * 16 + 16)
                    pe.wait_ge(rows_placed, at + 1)
                    for k in range(KD):
                        for u in range(TB):
                            mm = pe.transpose(bank[:, 6, (k * TB + u) * P:(k * TB + u + 1) * P],
                                              block_in[:, u, k * P:(k + 1) * P], ident[:])
                    mm.then_inc(rows_turned, 1)

                def before(e, s, v):
                    pe.wait_ge(set_ready[s], v + 1)
                    gated(pe)

                def body(e, s, at):
                    pe.wait_ge(rows_placed, at + 2)
                    slot = turned_rows[:, ds(at % 2, 1), :, :].rearrange("p a k n -> p (a k) n")
                    routed.tensor(pe, at, s, lambda k: slot[:, k, :], TB, between=lambda: turn(at + 1))

                pe.sem_inc(routed.down_done, KF)
                pe.sem_inc(rows_turned, 1)
                turn(0)
                experts(pe, "pe_blocks", body, before,
                        lambda: pe.matmul(bank[:, 7, 0:8], zero[:, 0:P], zero[:, 0:8], start=True, stop=True)
                        .then_inc(expert_done, 1))

        fetch_at = send_at
        fetch_ready = sem("fetch_ready")
        fetched_in = [sem(f"fetched_in{u}") for u in range(4)]
        half_added = sem("half_added")
        added = sem("added")
        stored = [sem(f"stored{u}") for u in range(4)]

        def fours(engine, body):
            def four(i):
                for u in range(4):
                    body(i * 4 + u, u, i, P)

            loop(engine, NT // 4, four)
            body(NT - 1, 0, NT // 4, LAST)

        with nc.Block() as block:
            @block.sync
            def _(sp):
                def store(t, u, i, p):
                    sp.wait_ge(added, t + 1)
                    gated(sp)
                    sp.dma_start(out[ds(t * P, p), :], tile(resid, t)[0:p, :]).then_inc(stored[u], 16)

                fours(sp, store)
                sp.wait_ge(stored[0], 16 * (NT // 4 + 1))
                for u in range(1, 4):
                    sp.wait_ge(stored[u], 16 * (NT // 4))

            @block.gpsimd
            def _(pool):
                def fetch(t, u, i, p):
                    pool.wait_ge(fetch_ready, t + 1)
                    wait_past(pool, added, i * 4)
                    gated(pool)
                    for w in range(2):
                        pool.indirect_dma_start(
                            fetched[:, w, u, :], None, expert_out,
                            bass.IndirectOffsetOnAxis(ap=fetch_at[:, u, w:w + 1], axis=0)).then_inc(fetched_in[u], 16)

                fours(pool, fetch)

            @block.scalar
            def _(act):
                def indices(t, u, i):
                    wait_past(act, fetched_in[u], i * 32)
                    act.activation(fetch_at[:, u, :], tile(slot_of, t), ACT.Copy).then_inc(fetch_ready, 1)

                def four(i):
                    for u in range(4):
                        indices(i * 4 + u, u, i)
                    shared.scalar(act, i + NS1, shared_bias, TB)

                loop(act, NT // 4, four)
                indices(NT - 1, 0, NT // 4)
                shared.scalar(act, NS, shared_bias, 1)

            @block.vector
            def _(dve):
                def add(t, u, i):
                    dve.wait_ge(fetched_in[u], i * 32 + 32)
                    for w in range(2):
                        dve.scalar_tensor_tensor(tile(resid, t), fetched[:, w, u, :], tile(weight_of, t)[:, w:w + 1],
                                                 tile(resid, t), ALU.mult, ALU.add)\
                            .then_inc([half_added, added][w], 1)
                        if w == 0:
                            dve.wait_ge(half_added, t + 1)

                def four(i):
                    take_shared(dve, i + NS1, TB)
                    dve.wait_ge(shared.sums_taken, i + NS1 + 2)
                    for u in range(4):
                        add(i * 4 + u, u, i)

                loop(dve, NT // 4, four)
                take_shared(dve, NS, 1)
                dve.wait_ge(shared.sums_taken, NS + 2)
                add(NT - 1, 0, NT // 4)

            @block.tensor
            def _(pe):
                with pe.Fori(NS1, NS) as b:
                    shared.tensor(pe, b, 2, lambda k: feat_t[:, k, nodes(b * TB, TB)], TB)
                shared.tensor(pe, NS, 2, lambda k: feat_t[:, k, nodes(NT - 1)], 1)


_INS = ['x', 'src', 'dst', 'edge_attr_4', 'L0_gnn_mlp_w', 'L0_gnn_mlp_b', 'L0_gnn_ew1', 'L0_gnn_ew2',
        'L0_gnn_bn_g', 'L0_gnn_bn_b', 'L0_ffn_Wr', 'L0_ffn_W1s', 'L0_ffn_b1s', 'L0_ffn_W2s', 'L0_ffn_b2s',
        'L0_ffn_W1p', 'L0_ffn_b1p', 'L0_ffn_W2p', 'L0_ffn_b2p']
_OUTS = [((6250, 256), 'float32')]


def kernel(**inputs):
    import numpy as _np
    import concourse.bacc as _bacc
    from concourse import mybir as _mybir
    from concourse.bass_utils import run_bass_kernel_spmd as _run

    nc = _bacc.Bacc("TRN2", target_bir_lowering=False, num_devices=1)
    arrays, args = {}, []
    for name in _INS:
        a = _np.ascontiguousarray(inputs[name])
        arrays[f"in_{name}_dram"] = a
        args.append(nc.dram_tensor(f"in_{name}_dram", a.shape, _mybir.dt.from_np(a.dtype), kind="ExternalInput").ap())
    for i, (shape, dtype) in enumerate(_OUTS):
        dt = _mybir.dt.from_np(_np.dtype(dtype))
        args.append(nc.dram_tensor(f"out_{i}_dram", shape, dt, kind="ExternalOutput").ap())
    build(nc, *args)
    r = _run(nc, [arrays], core_ids=[0])
    got = tuple(r.results[0][f"out_{i}_dram"] for i in range(len(_OUTS)))
    return got[0]
```
